# Optimizing a Trainium2 kernel written in Bass

```python
import numpy as np
import jax
import jax.numpy as jnp

def _softmax(x, axis=-1):
    return jax.nn.softmax(x, axis=axis)

def _gelu(x):
    return jax.nn.gelu(x, approximate=True)

def _silu(x):
    return jax.nn.silu(x)

def _sigmoid(x):
    return jax.nn.sigmoid(x)

def _layernorm(x, axis=-1, eps=1e-05):
    m = jnp.mean(x, axis=axis, keepdims=True)
    v = jnp.var(x, axis=axis, keepdims=True)
    return (x - m) / jnp.sqrt(v + eps)

def _scatter_add(tgt, idx, src, axis=0):
    return tgt.at[idx].add(src)

def _segment_sum(src, seg, n):
    return jax.ops.segment_sum(src, seg, n)
kernel_name = 'mk_adj_resnorm_d2_adj_r2_e434e1'

def setup_inputs(seed: int=0):
    np.random.seed(seed)
    _w = jnp.asarray

    def _rec_inputs():
        import jax
        import jax.numpy as jnp
        _gk = jax.random.key(seed)
        x = -0.0004776 + 1.001 * jax.random.normal(jax.random.fold_in(_gk, 1), (2048, 512), jnp.float32)
        _a = jax.random.bernoulli(jax.random.fold_in(_gk, 2), 0.00390625, (2048, 2048))
        _a = jnp.logical_or(_a, jnp.eye(2048, dtype=bool))
        _af = _a.astype(jnp.float32)
        adj = _af
        return (x, adj)
    x, adj = _rec_inputs()

    def _L0_gnn_setup():
        import jax, jax.numpy as jnp
        import numpy as np
        N, H, E, HEADS = (1500, 512, 10000, 8)
        DK = H // HEADS
        key = jax.random.key(seed)
        k1, k2, k3, k4 = jax.random.split(key, 4)
        inst_feature = jax.random.normal(k1, (N, H), dtype=jnp.float32)
        rel_pair_index = jax.random.randint(k2, (E, 2), 0, N, dtype=jnp.int64)
        agg = jnp.zeros((N, N), dtype=jnp.float32)
        agg = agg.at[rel_pair_index[:, 0], rel_pair_index[:, 1]].set(1.0)
        agg = agg.at[jnp.arange(N), jnp.arange(N)].set(1.0)
        std = float(np.sqrt(2.0 / (H + DK)))
        Wq = jax.random.normal(k3, (H, H), dtype=jnp.float32) * std
        Wk = jax.random.normal(k4, (H, H), dtype=jnp.float32) * std
        bq = jnp.zeros((H,), dtype=jnp.float32)
        bk = jnp.zeros((H,), dtype=jnp.float32)
        return {'inst_feature': inst_feature, 'aggregator_matrix': agg, 'rel_pair_index': rel_pair_index, 'Wq': Wq, 'bq': bq, 'Wk': Wk, 'bk': bk}
    _L0_gnn_all = _L0_gnn_setup()
    _L0_gnn_in = {k: v for k, v in _L0_gnn_all.items() if k in ('rel_pair_index', 'Wq', 'bq', 'Wk', 'bk')}
    del _L0_gnn_all

    def _L1_gnn_setup():
        import jax, jax.numpy as jnp
        import numpy as np
        N = 4096
        D = 512

        def adjacent_mat(adj):
            adj = adj + jnp.eye(adj.shape[0], dtype=adj.dtype)
            deg = jnp.sum(adj, axis=1)
            dinv = jnp.where(deg > 0, deg ** (-0.5), 0.0).astype(adj.dtype)
            return dinv[:, None] * adj * dinv[None, :]
        key = jax.random.key(seed)
        k1, k2 = jax.random.split(key)
        x = jax.random.normal(k1, (N, D), dtype=jnp.float32)
        Coefficient2 = 1e-08 * jnp.ones((N, N), dtype=jnp.float32)
        A = jax.random.uniform(k2, (N, N), dtype=jnp.float32)
        return {'x': x, 'Coefficient2': Coefficient2, 'A': A}
    _L1_gnn_all = _L1_gnn_setup()
    _L1_gnn_in = {k: v for k, v in _L1_gnn_all.items() if k in ()}
    del _L1_gnn_all
    return {'x': x, 'adj': adj, 'L0_gnn_rel_pair_index': _L0_gnn_in['rel_pair_index'], 'L0_gnn_Wq': _L0_gnn_in['Wq'], 'L0_gnn_bq': _L0_gnn_in['bq'], 'L0_gnn_Wk': _L0_gnn_in['Wk'], 'L0_gnn_bk': _L0_gnn_in['bk']}

def reference(x, adj, L0_gnn_rel_pair_index, L0_gnn_Wq, L0_gnn_bq, L0_gnn_Wk, L0_gnn_bk):
    import jax
    import jax.numpy as jnp

    def _L0_gnn_ref(inst_feature, aggregator_matrix, rel_pair_index, Wq, bq, Wk, bk):
        import jax, jax.numpy as jnp
        import numpy as np
        N, H, E, HEADS = (1500, 512, 10000, 8)
        DK = H // HEADS
        n = inst_feature.shape[0]
        sub = rel_pair_index[:, 0]
        obj = rel_pair_index[:, 1]
        q = (inst_feature[sub] @ Wq.T + bq).reshape(-1, HEADS, DK)
        k = (inst_feature[obj] @ Wk.T + bk).reshape(-1, HEADS, DK)
        att = ((q * k).sum(-1) / np.sqrt(DK)).T.astype(inst_feature.dtype)
        scores = jnp.zeros((HEADS, n, n), dtype=inst_feature.dtype)
        scores = scores.at[:, sub, obj].set(att)
        mask = (1.0 - aggregator_matrix).astype(bool)
        scores = jnp.where(mask[None], -jnp.inf, scores)
        di = jnp.arange(n)
        scores = scores.at[:, di, di].set(1e-07)
        attn = jax.nn.softmax(scores, axis=2)
        aggregator_factor = attn.sum(axis=0) / HEADS
        return aggregator_factor @ inst_feature

    def _L1_gnn_ref(x, Coefficient2, A):
        import jax, jax.numpy as jnp
        import numpy as np
        N = 4096
        D = 512

        def adjacent_mat(adj):
            adj = adj + jnp.eye(adj.shape[0], dtype=adj.dtype)
            deg = jnp.sum(adj, axis=1)
            dinv = jnp.where(deg > 0, deg ** (-0.5), 0.0).astype(adj.dtype)
            return dinv[:, None] * adj * dinv[None, :]
        A_c = jax.lax.stop_gradient(A)
        adj = adjacent_mat((A_c + A_c.T) * 0.5)
        y = Coefficient2 @ adj
        y = y @ x
        return y
    x = _layernorm(x + _L0_gnn_ref(x, adj, L0_gnn_rel_pair_index, L0_gnn_Wq, L0_gnn_bq, L0_gnn_Wk, L0_gnn_bk), axis=-1)
    x = _layernorm(x + _L1_gnn_ref(x, adj, adj), axis=-1)
    return x

_drawn_inputs = setup_inputs


def setup_inputs(seed=0):
    import zlib

    import numpy as np

    out = dict(_drawn_inputs(seed))
    spreads = {'L0_gnn_bq': (0.0, 2.0), 'L0_gnn_bk': (0.0, 2.0)}
    factors = {'L0_gnn_Wq': 17.029, 'L0_gnn_Wk': 18.457}
    for name, (base, spread) in spreads.items():
        noise = np.random.default_rng([zlib.crc32(name.encode()), seed]).standard_normal(out[name].shape)
        drawn = base * np.exp(spread * noise) if base else spread * noise
        out[name] = jnp.asarray(drawn.astype(out[name].dtype))
    for name, factor in factors.items():
        out[name] = (out[name] * factor).astype(out[name].dtype)
    return out
```

```python
import concourse.bass as bass
from concourse import mybir
from contextlib import ExitStack


def gnn_resnorm_kernel(nc: bass.Bass, x: bass.AP, adj: bass.AP, pairs: bass.AP, wq: bass.AP, bq: bass.AP,
                       wk: bass.AP, bk: bass.AP, out: bass.AP):
    f32, f16, i32, u8 = mybir.dt.float32, mybir.dt.float16, mybir.dt.int32, mybir.dt.uint8
    ALU, ACT, AX = mybir.AluOpType, mybir.ActivationFunctionType, mybir.AxisListType
    SIZE = {f32: 4, f16: 2, i32: 4, u8: 1}

    N, D = x.shape
    E = pairs.shape[0]
    P, HEADS, DK = 128, 8, 64
    NB, KB = N // P, D // P
    EC = 80
    EP = E // EC
    HI, LO = P, N // P
    G4, G8 = EC // 4, EC // 8
    SLOTS = 8
    NV = HEADS + 1
    MAGIC = 1.5 * 2.0 ** 23
    XS, WS, VS, ZS, AS = 2.0 ** 4, 2.0 ** 6, 2.0 ** 10, 2.0 ** 5, 2.0 ** 14
    EPS, DIAG = 1e-5, 1e-7
    LASTCOL, LASTROW = EC - 1, EP - 1
    K = 1024
    LOG_N, LOG_P, LOG_LO = 11, 7, 4
    assert EP * EC == E and EP <= P and HEADS * DK == D and HI * LO == N
    assert (1 << LOG_N, 1 << LOG_P, 1 << LOG_LO) == (N, P, LO)

    q_tab = nc.dram_tensor("q_tab", (N, D), f32).ap()
    k_tab = nc.dram_tensor("k_tab", (N, D), f32).ap()
    corr_tab = nc.dram_tensor("corr_tab", (N * N, 1), f32).ap()
    deg_tab = nc.dram_tensor("deg_tab", (N,), f32).ap()
    base_tab = nc.dram_tensor("base_tab", (N,), f32).ap()
    diag_tab = nc.dram_tensor("diag_tab", (N,), f32).ap()
    edge_tab = nc.dram_tensor("edge_tab", (E, 2), f32).ap()
    piece_tab = [nc.dram_tensor(f"piece_tab{n}", (2 * EP, 10), f32).ap() for n in range(2)]
    x1_tab = nc.dram_tensor("x1_tab", (N, D), f32).ap()

    ctx = ExitStack()
    with ctx:
        ARENA = 212800
        arena = ctx.enter_context(nc.sbuf_tensor("arena", [P, ARENA], u8))
        ps = ctx.enter_context(nc.psum_tensor("ps", [P, 8, 512], f32))

        def place(first, shape, dt, end=None):
            n = SIZE[dt]
            for s in shape[1:]:
                n *= s
            assert first % 4 == 0 and first + n <= (end or ARENA), (first, n)
            v = arena[0:shape[0], first:first + n].bitcast(dt)
            names = "abcde"[:len(shape) - 1]
            if len(shape) > 2:
                v = v.rearrange(f"p ({' '.join(names)}) -> p {' '.join(names)}",
                                **{c: s for c, s in zip(names[1:], shape[2:])})
            return v

        def row_of(first, end):
            here = [first]

            def take(shape, dt=f32):
                v = place(here[0], shape, dt, end)
                n = SIZE[dt]
                for s in shape[1:]:
                    n *= s
                here[0] += (n + 3) // 4 * 4
                return v
            return take

        def sem(name):
            return ctx.enter_context(nc.semaphore(name))

        sym8 = place(0, [P, NB, N], u8)
        bias_in = place(32 * K, [P, 2, D], f32)
        bias_hi, bias_mid = place(36 * K, [P, 2, D], f16), place(38 * K, [P, 2, D], f16)
        adjT8 = place(32 * K, [P, NB, N], u8)
        xf = place(64 * K, [P, NB, D], f32)
        t_ = row_of(64 * K, 92 * K)
        cnt, incl = t_([P, LO, EC]), t_([P, LO, EC])
        tab = t_([P, EC, 3, LO], f16)
        picked = t_([EP, 2, 8 * 3 * LO])
        posf = t_([EP, EC, 3])
        restart = t_([P, LO, EC], f16)
        hotlo = t_([EP, EC, LO], f16)
        rank, junk = t_([EP, EC]), t_([P, P], f16)
        payhots = [place(64 * K, [EP, EC, f, EC], f16) for f in (2, 3)]
        proj = place(92 * K, [P, 2, D], f32)
        rows = place(64 * K, [EP, SLOTS, 2, D], f32)
        vhl = place(64 * K, [P, NB, 2, D], f16)
        xT = place(96 * K, [P, KB, 2, N], f16)
        e_ = row_of(96 * K, 128 * K)
        att = e_([EP, HEADS, EC])
        flagF, flagB = e_([EP, NV, EC], f16), e_([EP, NV, EC], f16)
        val, scF, scB = e_([EP, NV, EC]), e_([EP, NV, EC]), e_([EP, NV, EC])
        arg = e_([EP, 3, HEADS, EC])
        sub, obj, degE, weight = (e_([EP, EC]) for _ in range(4))
        selF, selL, tmpE = (e_([EP, EC]) for _ in range(3))
        subI, objI, tmpI, cidx = (e_([EP, EC], i32) for _ in range(4))
        sums, corrE, edge_rows = e_([EP, 3, EC]), e_([EP, EC]), e_([EP, EC, 2])
        piece, totals = e_([EP, 2, 10]), e_([EP, 2, NV])
        before16, before = e_([EP, 2, 4], f16), e_([EP, 2])
        corr_in = place(96 * K, [P, 2, NB, P], f32)
        agg = place(112 * K, [P, 2, NB, P], f32)
        wT = place(128 * K, [P, 2, KB, 2, D], f16)
        adj_in = place(144 * K, [P, 2, N], f32)
        xhl = place(128 * K, [P, NB, 2, D], f16)
        hot = place(160 * K, [EP, EC, HI], f16)
        tgt = place(160 * K, [EP, EC, EP], f16)
        rec = place(160 * K, [EP, 2 * EP, 10], f32)
        recprod = place(170 * K, [EP, NV, 2 * EP], f32)
        agghl = place(160 * K, [P, 2, 2, NB, P], f16)
        stage16 = place(160 * K, [P, 2, NB, P], f16)
        w_in = place(180 * K, [P, 2, KB, D], f32)
        hotT = place(180 * K, [P, EC, EP], f16)
        b_ = row_of(180 * K, 180 * K + 20000)
        prod = b_([EP, 4, D])
        x_in = b_([P, 2, D])
        eqs = b_([EP, 2, 2 * EP])
        shift = b_([EP, EP], f16)
        c_ = row_of(180 * K, 180 * K + 20000)
        res, xt, nrm = c_([P, D]), c_([P, 2, D]), c_([P, 2, D])
        baseB = c_([P, N])
        k_ = row_of(180 * K + 20000, ARENA)
        raw = k_([EP, EC, 2], i32)
        q32 = raw.rearrange("p c f -> p (c f)").bitcast(f32)
        tcol, tpart = q32[:, 0:EC], q32[:, EC:2 * EC]
        adj_idx, valid = k_([EP, EC], i32), k_([EP, EC])
        key, key16 = k_([EP, EC]), k_([EP, EC], f16)
        payload = k_([EP, 3, EC])
        off, tot = k_([P, LO]), k_([P, LO])
        rowsum, adjii, degm, dinv, dcorr, vscale, zscale, baseC = (k_([P, NB]) for _ in range(8))
        degr, rowI = k_([P, LO]), k_([P, LO], i32)
        rowv, stat = k_([P, LO, 2]), k_([P, 2, 8])
        aoff, rowtot = k_([P, 1]), k_([P, 1])
        ident32, upper = k_([P, P]), k_([P, P])
        ident16, iota = k_([P, P], f16), k_([P, P], f16)
        lower, const16 = k_([EP, EP + 1], f16), k_([P, P], f16)
        zeros = k_([P, P])
        bias16 = k_([P, 2, D], f16)

        s_const, s_zero_src, s_zeroed = sem("constants"), sem("zero_source"), sem("corr_table_zeroed")
        s_raw, s_x, s_w, s_b = sem("pairs_loaded"), sem("x_loaded"), sem("w_loaded"), sem("bias_loaded")
        s_bias, s_idx, s_valid = sem("bias_split"), sem("adj_index"), sem("adj_picked")
        s_dve = sem("dve_chain")
        s_hot, s_group, s_hotT, s_rank = sem("hot_built"), sem("key_group"), sem("hotT_copied"), sem("ranked")
        s_cnt, s_rowtot, s_aoff = sem("counts_copied"), sem("row_totals"), sem("row_offsets")
        s_tab, s_pick, s_pickmul, s_picked = sem("table"), sem("pick_product"), sem("pick_mul"), sem("picked")
        s_onehots, s_perm, s_permcopied = sem("one_hots"), sem("permuted"), sem("permuted_copied")
        s_tr, s_trhi, s_trlo = sem("transposed"), sem("transposed_hi"), sem("transposed_lo")
        s_adj = [sem(f"adj_loaded{n}") for n in range(2)]
        s_adjrow, s_fill, s_drain = sem("adj_rows_kept"), sem("stream_filled"), sem("stream_drained")
        s_kst, s_qst = sem("k_stored"), sem("q_stored")
        s_degm, s_degst, s_degr = sem("degrees"), sem("degrees_stored"), sem("degrees_by_row")
        s_eidx, s_before16, s_before = sem("edge_indices"), sem("last_edges"), sem("edge_before")
        s_rows = [sem(f"rows_gathered{n}") for n in range(SLOTS)]
        s_prod, s_att = sem("products"), sem("attention")
        s_xin = [sem(f"x_again{n}") for n in range(2)]
        s_xhi, s_xlo = sem("x_hi"), sem("x_lo")
        s_piece, s_pst = sem("pieces"), [sem(f"pieces_stored{n}") for n in range(2)]
        s_rec = [sem(f"pieces_spread{n}") for n in range(2)]
        s_args, s_exp = sem("exponents"), sem("exponentials")
        s_corr, s_scat = sem("corrections"), sem("corrections_scattered")
        s_edge, s_est = sem("edge_rows"), sem("edge_rows_stored")
        s_default, s_rowg = sem("row_defaults"), sem("row_values_gathered")
        s_split, s_rst, s_rowld = sem("row_values"), sem("row_values_stored"), sem("row_values_loaded")
        s_cin = [sem(f"corr_loaded{n}") for n in range(2)]
        s_xt = [sem(f"x_tile{n}") for n in range(2)]
        s_scaled, s_agg, s_agghi, s_agglo = sem("adj_scaled"), sem("agg"), sem("agg_hi"), sem("agg_lo")
        s_mm1, s_res1, s_ln1 = sem("agg_product"), sem("residual1"), sem("ln1_chain")
        s_x1, s_vhi, s_vlo, s_x1st = sem("x1"), sem("v_hi"), sem("v_lo"), [sem(f"x1_stored{n}") for n in range(2)]
        s_st2, s_mm2, s_zhi, s_zlo = sem("sym_staged"), sem("sym_product"), sem("z_hi"), sem("z_lo")
        s_st3, s_mm3, s_ln3, s_y = sem("adj_staged"), sem("adj_product"), sem("ln3_chain"), sem("y")
        s_x1in = [sem(f"x1_tile{n}") for n in range(2)]
        s_out = [sem(f"out_stored{n}") for n in range(2)]
        s_pool, s_res3, s_dg = sem("pool_chain"), sem("residual3"), sem("diagonal_added")
        s_sym, s_deg, s_degroot = sem("symmetric_rows"), sem("symmetric_degrees"), sem("degree_roots")
        s_var1, s_root1, s_var3, s_root3 = sem("variance1"), sem("deviation1"), sem("variance3"), sem("deviation3")

        FIELDS = (2, 3)

        ps_hotT = ps[:, 0:2, :].rearrange("p g m -> p (g m)").bitcast(f16).rearrange("p (g u e) -> p g u e", g=2, u=8)
        ps_cnt = ps[:, 5:8, :].rearrange("p b c -> p (b c)")
        TRANSPOSES = 2 * KB + KB * 4
        SEGMENT = NB // 4
        x_rows = x.rearrange("(b p) d -> p b d", p=P)
        adj_rows = adj.rearrange("(b p) j -> b p j", p=P)
        corr_blocks = corr_tab.rearrange("(b p m) o -> b p (m o)", b=NB, p=P)
        x1_rows = x1_tab.rearrange("(b p) d -> b p d", p=P)
        xb_rows = x.rearrange("(b p) d -> b p d", p=P)
        out_rows = out.rearrange("(b p) d -> b p d", p=P)
        q_rows = q_tab.rearrange("(b p) d -> b p d", p=P)
        k_rows = k_tab.rearrange("(b p) d -> b p d", p=P)

        block = ctx.enter_context(nc.Block())

        @block.sync
        def _(sp):
            sp.dma_start(raw, pairs.rearrange("(p c) f -> p c f", p=EP)).then_inc(s_raw, 16)
            sp.dma_start(bias_in[:, 0], bk.partition_broadcast(P)).then_inc(s_b, 16)
            sp.dma_start(bias_in[:, 1], bq.partition_broadcast(P)).then_inc(s_b, 16)
            sp.dma_start(w_in[:, 0], wk.rearrange("(b p) d -> p b d", p=P)).then_inc(s_w, 16)
            sp.dma_start(w_in[:, 1], wq.rearrange("(b p) d -> p b d", p=P)).then_inc(s_w, 16)
            for b in range(0, NB, 4):
                sp.dma_start(xf[:, b:b + 4], x_rows[:, b:b + 4]).then_inc(s_x, 16)
            sp.wait_ge(s_zero_src, 1)
            for b in range(NB):
                dst = corr_blocks[b].rearrange("p (a m) -> p a m", m=P)
                sp.dma_start(dst, zeros.unsqueeze(1).to_broadcast([P, NB, P])).then_inc(s_zeroed, 16)
            sp.wait_ge(s_degm, 1)
            with nc.allow_non_contiguous_dma("2048 single values"):
                sp.dma_start(deg_tab.rearrange("(b p) -> p b", p=P), degm).then_inc(s_degst, 16)
            sp.wait_ge(s_degst, 16)
            sp.dma_start(degr, deg_tab.rearrange("(a b) -> a b", b=LO)).then_inc(s_degr, 16)
            for b in range(NB):
                if b == 0:
                    sp.wait_ge(s_perm, 2)
                if b >= 2:
                    sp.wait_ge(s_xlo, b - 1)
                sp.dma_start(x_in[:, b % 2], xb_rows[b]).then_inc(s_xin[b % 2], 16)
            for n in range(2):
                sp.wait_ge(s_piece, n + 1)
                sp.dma_start(piece_tab[n].rearrange("(p k) v -> p k v", k=2), piece).then_inc(s_pst[n], 16)
                sp.wait_ge(s_pst[n], 16)
                sp.dma_start(rec.rearrange("p q v -> p (q v)"),
                             piece_tab[n].rearrange("q v -> (q v)").partition_broadcast(EP)).then_inc(s_rec[n], 16)
            sp.wait_ge(s_edge, 1)
            sp.dma_start(edge_tab.rearrange("(p c) v -> p c v", p=EP), edge_rows).then_inc(s_est, 16)
            sp.wait_ge(s_split, 1)
            sp.dma_start(base_tab.rearrange("(a b) -> a b", b=LO), off).then_inc(s_rst, 16)
            sp.dma_start(diag_tab.rearrange("(a b) -> a b", b=LO), tot).then_inc(s_rst, 16)
            sp.wait_ge(s_rst, 32)
            sp.dma_start(baseB, base_tab.partition_broadcast(P)).then_inc(s_rowld, 16)
            with nc.allow_non_contiguous_dma("2048 single values"):
                sp.dma_start(baseC, base_tab.rearrange("(b p) -> p b", p=P)).then_inc(s_rowld, 16)
                sp.dma_start(dcorr, diag_tab.rearrange("(b p) -> p b", p=P)).then_inc(s_rowld, 16)
            sp.wait_ge(s_scat, 16 * EC)
            for b in range(2):
                sp.dma_start(corr_in[:, b].rearrange("p j i -> p (j i)"), corr_blocks[b]).then_inc(s_cin[b], 16)
                sp.dma_start(xt[:, b], xb_rows[b]).then_inc(s_xt[b], 16)
            with sp.Fori(2, NB - 1, 2) as b0:
                for s in range(2):
                    sp.wait_ge(s_agg, b0 + s - 1)
                    sp.dma_start(corr_in[:, s].rearrange("p j i -> p (j i)"),
                                 corr_blocks[b0 + s]).then_inc(s_cin[s], 16)
                    sp.wait_ge(s_res1, b0 + s - 1)
                    sp.dma_start(xt[:, s], xb_rows[b0 + s]).then_inc(s_xt[s], 16)
            for n in range(2):
                sp.wait_ge(s_x1st[n], 16 * (NB // 2))
            sp.wait_ge(s_res1, NB)
            for s in range(2):
                sp.dma_start(xt[:, s], x1_rows[s]).then_inc(s_x1in[s], 16)
            with sp.Fori(2, NB - 1, 2) as b0:
                for s in range(2):
                    sp.wait_ge(s_res3, b0 + s - 1)
                    sp.dma_start(xt[:, s], x1_rows[b0 + s]).then_inc(s_x1in[s], 16)
            for n in range(2):
                sp.wait_ge(s_out[n], 16 * (NB // 2))

        @block.gpsimd
        def _(pool):
            chain = [0]

            def link(ins):
                chain[0] += 1
                ins.then_inc(s_pool, 1)
                pool.wait_ge(s_pool, chain[0])

            nc.gpsimd.memset(zeros, 0.0).then_inc(s_zero_src, 1)
            link(nc.gpsimd.memset(ident32, 0.0))
            link(nc.gpsimd.affine_select(out=ident32, in_=ident32, compare_op=ALU.not_equal, fill=1.0, base=0,
                                         pattern=[[-1, P]], channel_multiplier=1))
            link(nc.gpsimd.tensor_copy(ident16, ident32))
            link(nc.gpsimd.iota(iota, pattern=[[1, P]], base=0, channel_multiplier=0,
                                allow_small_or_imprecise_dtypes=True))
            link(nc.gpsimd.memset(lower, 1.0))
            link(nc.gpsimd.affine_select(out=lower, in_=lower, compare_op=ALU.is_gt, fill=0.0, base=0,
                                         pattern=[[-1, EP + 1]], channel_multiplier=1))
            link(nc.gpsimd.memset(upper, 1.0))
            link(nc.gpsimd.affine_select(out=upper, in_=upper, compare_op=ALU.is_gt, fill=0.0, base=0,
                                         pattern=[[1, P]], channel_multiplier=-1))
            link(nc.gpsimd.memset(const16, XS * WS))
            nc.gpsimd.memset(bias16, 0.0).then_inc(s_const, 1)
            pool.wait_ge(s_idx, 1)
            adj_flat = adj.rearrange("i (j o) -> (i j) o", o=1)
            for c in range(EC):
                pool.indirect_dma_start(valid[:, c:c + 1], None, adj_flat,
                                        bass.IndirectOffsetOnAxis(ap=adj_idx[:, c:c + 1], axis=0)).then_inc(s_valid, 16)
            pool.wait_ge(s_eidx, 1)
            pool.wait_ge(s_kst, 16 * NB)
            pool.wait_ge(s_qst, 16 * NB)
            for c in range(EC):
                n, s = divmod(c, SLOTS)
                if n:
                    pool.wait_ge(s_prod, c - SLOTS + 1)
                pool.indirect_dma_start(rows[:, s, 0], None, q_tab,
                                        bass.IndirectOffsetOnAxis(ap=subI[:, c:c + 1], axis=0)).then_inc(s_rows[s], 16)
                pool.indirect_dma_start(rows[:, s, 1], None, k_tab,
                                        bass.IndirectOffsetOnAxis(ap=objI[:, c:c + 1], axis=0)).then_inc(s_rows[s], 16)
            pool.wait_ge(s_est, 16)
            pool.wait_ge(s_default, 1)
            for b in range(LO):
                pool.indirect_dma_start(rowv[:, b], None, edge_tab,
                                        bass.IndirectOffsetOnAxis(ap=rowI[:, b:b + 1], axis=0),
                                        bounds_check=E - 1, oob_is_err=False).then_inc(s_rowg, 16)
            pool.wait_ge(s_corr, 1)
            pool.wait_ge(s_zeroed, 16 * NB)
            for c in range(EC):
                pool.indirect_dma_start(corr_tab, bass.IndirectOffsetOnAxis(ap=cidx[:, c:c + 1], axis=0),
                                        corrE[:, c:c + 1], None,
                                        bounds_check=N * N - 1, oob_is_err=False).then_inc(s_scat, 16)
            with pool.Fori(0, NB - 1, 2) as b0:
                for s in range(2):
                    pool.wait_ge(s_scaled, b0 + s + 1)
                    pool.wait_ge(s_cin[s], b0 * 8 + 16)
                    nc.gpsimd.tensor_tensor(agg[:, s], agg[:, s], corr_in[:, s], ALU.add).then_inc(s_agg, 1)
            with pool.Fori(0, NB - 1, 2) as b0:
                for s in range(2):
                    pool.wait_ge(s_y, b0 + s + 1)
                    pool.dma_start(out_rows[b0 + s], nrm[:, s]).then_inc(s_out[s], 16)

        @block.tensor
        def _(pe):
            def sort_groups(n):
                pe.wait_ge(s_hot, n + 1)

                def group(g):
                    for u in range(4):
                        c = 4 * g + u
                        nc.tensor.transpose(ps_hotT[:, g % 2, u, 0:EP], hot[:, c],
                                            ident16[0:EP, 0:EP])
                        nc.tensor.matmul(ps_cnt[:, bass.ds(c * LO, LO)], hot[:, c], hotlo[:, c], start=True, stop=True)
                        r = nc.tensor.matmul(ps[0:EP, 3 + g % 2, u * P:u * P + EP],
                                             key16[:, bass.ds(c, 1)].to_broadcast([EP, EP]), ident16[0:EP, 0:EP],
                                             start=True, stop=True)
                    r.then_inc(s_group, 1)

                if n:
                    pe.wait_ge(s_permcopied, n)
                    pe.wait_ge(s_drain, 3 * SEGMENT * 6)
                else:
                    pe.wait_ge(s_trhi, TRANSPOSES)
                    pe.wait_ge(s_trlo, TRANSPOSES)
                group(0)
                group(1)
                with pe.Fori(2, G4) as g:
                    pe.wait_ge(s_hotT, G4 * n + g - 1)
                    pe.wait_ge(s_rank, G4 * n + g - 1)
                    group(g)

            def sort_offsets(n):
                pe.wait_ge(s_rowtot, n + 1)
                nc.tensor.matmul(ps[:, 2, 0:1], upper, rowtot, start=True, stop=True).then_inc(s_aoff, 1)

            def sort_pick(n, fields):
                pe.wait_ge(s_tab, n + 1)

                def group(g):
                    for u in range(8):
                        c = 8 * g + u
                        r = nc.tensor.matmul(ps[0:EP, 3 + g % 2, u * fields * LO:(u + 1) * fields * LO], hotT[:, c],
                                             tab[:, c, 0:fields].rearrange("p f b -> p (f b)"), start=True, stop=True)
                    r.then_inc(s_pick, 1)

                group(0)
                group(1)
                with pe.Fori(2, G8) as g:
                    pe.wait_ge(s_pickmul, G8 * n + g - 1)
                    group(g)

            def sort_permute(n, fields):
                payhot = payhots[n]
                """Payloads to their places: sum over edges of partition one-hot x column one-hot."""
                pe.wait_ge(s_onehots, EC * (n + 1))

                def product(c, start, stop):
                    return nc.tensor.matmul(ps[0:EP, 5, 0:fields * EC], tgt[:, c],
                                            payhot[:, c, 0:fields].rearrange("p f c -> p (f c)"),
                                            start=start, stop=stop)

                product(0, True, False)
                with pe.Fori(1, LASTCOL) as c:
                    product(c, False, False)
                product(LASTCOL, False, True).then_inc(s_perm, 1)

            pe.wait_ge(s_const, 1)
            pe.wait_ge(s_w, 32)
            for g in range(TRANSPOSES):
                if g == 2 * KB:
                    pe.wait_ge(s_x, 16 * (NB // 4))
                if g >= 2:
                    pe.wait_ge(s_trhi, g - 1)
                    pe.wait_ge(s_trlo, g - 1)
                for u in range(4):
                    if g < 2 * KB:
                        src = w_in[:, g // KB, u, (g % KB) * P:(g % KB + 1) * P]
                    else:
                        k, c = divmod(g - 2 * KB, 4)
                        src = xf[:, 4 * c + u, k * P:(k + 1) * P]
                    r = nc.tensor.transpose(ps[:, g % 2, u * P:(u + 1) * P], src, ident32)
                r.then_inc(s_tr, 1)

            def stream(segment):
                def pair(b0, first):
                    for s in range(2):
                        b = b0 + s
                        pe.wait_ge(s_adj[s], b0 * 8 + 16)
                        for g in range(4):
                            if not (first and s == 0 and g < 2):
                                pe.wait_ge(s_drain, b * 6 + g - 1)
                            for u in range(4):
                                j = 4 * g + u
                                r = nc.tensor.transpose(ps[:, g % 2, u * P:(u + 1) * P],
                                                        adj_in[:, s, j * P:(j + 1) * P], ident32)
                            r.then_inc(s_fill, 1)
                        for w in range(2):
                            pe.wait_ge(s_drain, b * 6 + 3 + w)
                            for k in range(KB):
                                for i, j in ((0, 0), (0, 1), (1, 0)):
                                    nc.tensor.matmul(ps[:, w, :], xT[:, k, i, bass.ds(b * P, P)], wT[:, w, k, j],
                                                     start=(k == 0 and i == 0 and j == 0), stop=False)
                            nc.tensor.matmul(ps[:, w, :], const16, bias16[:, w], start=False,
                                             stop=True).then_inc(s_fill, 1)

                if segment == 0:
                    pair(0, True)
                with pe.Fori(segment * SEGMENT + 2 * (segment == 0), (segment + 1) * SEGMENT - 1, 2) as b0:
                    pair(b0, False)

            sort_groups(0)
            pe.wait_ge(s_bias, 1)
            pe.wait_ge(s_hotT, G4)
            stream(0)
            sort_offsets(0)
            sort_pick(0, FIELDS[0])
            stream(1)
            sort_permute(0, FIELDS[0])
            stream(2)
            sort_groups(1)
            pe.wait_ge(s_hotT, 2 * G4)
            stream(3)
            sort_offsets(1)
            sort_pick(1, FIELDS[1])
            sort_permute(1, FIELDS[1])
            pe.wait_ge(s_before16, 1)
            nc.tensor.matmul(ps[0:EP, 6, 0:2], shift, before16[:, 0, 0:2], start=True, stop=True).then_inc(s_before, 1)

            pe.wait_ge(s_xhi, NB)
            pe.wait_ge(s_xlo, NB)

            def aggregate(b0, first):
                for s in range(2):
                    if not first:
                        pe.wait_ge(s_res1, b0 + s - 1)
                    pe.wait_ge(s_agghi, b0 + s + 1)
                    pe.wait_ge(s_agglo, b0 + s + 1)
                    for k in range(NB):
                        for i, j in ((0, 0), (0, 1), (1, 0)):
                            r = nc.tensor.matmul(ps[:, s, :], agghl[:, s, i, k], xhl[:, k, j],
                                                 start=(k == 0 and i == 0 and j == 0), stop=(k == NB - 1 and i == 1))
                    r.then_inc(s_mm1, 1)

            aggregate(0, True)
            with pe.Fori(2, NB - 1, 2) as b0:
                aggregate(b0, False)
            pe.wait_ge(s_vhi, NB)
            pe.wait_ge(s_vlo, NB)
            for staged, rhs, done, read in ((s_st2, vhl, s_mm2, s_zlo), (s_st3, xhl, s_mm3, s_res3)):
                if done is s_mm3:
                    pe.wait_ge(s_zhi, NB)
                    pe.wait_ge(s_zlo, NB)

                def blocks(b0, first):
                    for s in range(2):
                        pe.wait_ge(staged, b0 + s + 1)
                        if not first:
                            pe.wait_ge(read, b0 + s - 1)
                        for k in range(NB):
                            for j in range(2):
                                r = nc.tensor.matmul(ps[:, 2 + s, :], stage16[:, s, k], rhs[:, k, j],
                                                     start=(k == 0 and j == 0), stop=(k == NB - 1 and j == 1))
                        r.then_inc(done, 1)

                blocks(0, True)
                with pe.Fori(2, NB - 1, 2) as b0:
                    blocks(b0, False)

        @block.scalar
        def _(act):
            act.dma_start(adj_in[:, 0], adj_rows[0]).then_inc(s_adj[0], 16)
            act.dma_start(adj_in[:, 1], adj_rows[1]).then_inc(s_adj[1], 16)
            act.wait_ge(s_const, 1)
            for g in range(TRANSPOSES):
                act.wait_ge(s_tr, g + 1)
                if g < 2 * KB:
                    dst, scale = wT[:, g // KB, g % KB, 0], WS
                else:
                    k, c = divmod(g - 2 * KB, 4)
                    dst, scale = xT[:, k, 0, c * 512:(c + 1) * 512], XS
                nc.scalar.activation(dst, ps[:, g % 2, :], ACT.Copy, scale=scale).then_inc(s_trhi, 1)

            def copy_hotT(n):
                with act.Fori(0, G4) as g:
                    act.wait_ge(s_group, G4 * n + g + 1)
                    nc.scalar.activation(hotT[:, bass.ds(4 * g, 4)], ps_hotT[:, g % 2, 0:4, 0:EP], ACT.Copy).then_inc(s_hotT, 1)

            def stream(segment):
                def pair(b0, first, last):
                    for s in range(2):
                        b = b0 + s
                        act.wait_ge(s_adj[s], b0 * 8 + 16)
                        nc.scalar.activation(sym8[:, b], adj_in[:, s], ACT.Copy,
                                             accum_out=rowsum[:, bass.ds(b, 1)]).then_inc(s_adjrow, 1)
                        for g in range(4):
                            act.wait_ge(s_fill, b * 6 + g + 1)
                            src = ps[:, g % 2, :].rearrange("p (u i) -> p u i", u=4)
                            nc.scalar.activation(adjT8[:, 4 * g:4 * g + 4, bass.ds(b * P, P)], src,
                                                 ACT.Copy).then_inc(s_drain, 1)
                        if not last:
                            act.wait_ge(s_adjrow, b + 1)
                            act.dma_start(adj_in[:, s], adj_rows[b + 2]).then_inc(s_adj[s], 16)
                        for w, tab_rows, stored in ((0, k_rows, s_kst), (1, q_rows, s_qst)):
                            act.wait_ge(s_fill, b * 6 + 5 + w)
                            if not (first and s == 0):
                                act.wait_ge(stored, b * 16)
                            nc.scalar.activation(proj[:, w], ps[:, w, :], ACT.Copy,
                                                 scale=1.0 / (XS * WS)).then_inc(s_drain, 1)
                            act.wait_ge(s_drain, b * 6 + 5 + w)
                            act.dma_start(tab_rows[b], proj[:, w]).then_inc(stored, 16)

                if segment == 0:
                    pair(0, True, False)
                start, end = segment * SEGMENT + 2 * (segment == 0), (segment + 1) * SEGMENT - 1 - 2 * (segment == 3)
                with act.Fori(start, end, 2) as b0:
                    pair(b0, False, False)
                if segment == 3:
                    pair(NB - 2, False, True)

            copy_hotT(0)
            stream(0)
            stream(1)
            stream(2)
            copy_hotT(1)
            stream(3)
            with act.Fori(0, NB - 1, 2) as b0:
                for s in range(2):
                    act.wait_ge(s_xin[s], b0 * 8 + 16)
                    nc.scalar.activation(xhl[:, b0 + s, 0], x_in[:, s], ACT.Copy, scale=XS).then_inc(s_xhi, 1)
            act.wait_ge(s_deg, 1)
            nc.scalar.activation(dinv, dinv, ACT.Sqrt).then_inc(s_degroot, 1)
            act.wait_ge(s_args, 1)
            nc.scalar.activation(arg, arg, ACT.Exp).then_inc(s_exp, 1)

            def high(b, s, first):
                act.wait_ge(s_agg, b + 1)
                if not first:
                    act.wait_ge(s_mm1, b - 1)
                nc.scalar.activation(agghl[:, s, 0], agg[:, s], ACT.Copy).then_inc(s_agghi, 1)

            def deviation(variance, root, b, s):
                act.wait_ge(variance, b + 1)
                nc.scalar.activation(stat[:, s, 1:2], stat[:, s, 0:1], ACT.Sqrt).then_inc(root, 1)

            def keep_x1(b, s):
                deviation(s_var1, s_root1, b, s)
                act.wait_ge(s_x1, b + 1)
                act.dma_start(x1_rows[b], nrm[:, s]).then_inc(s_x1st[s], 16)
                nc.scalar.activation(vhl[:, b, 0], nrm[:, s], ACT.Copy,
                                     scale=vscale[:, bass.ds(b, 1)]).then_inc(s_vhi, 1)

            high(0, 0, True)
            high(1, 1, True)
            keep_x1(0, 0)
            with act.Fori(2, NB - 1, 2) as b0:
                high(b0, 0, False)
                keep_x1(b0 - 1, 1)
                high(b0 + 1, 1, False)
                keep_x1(b0, 0)
            keep_x1(NB - 1, 1)

            def stage(src, b, s, signal):
                nc.scalar.activation(stage16[:, s], src[:, :, bass.ds(b * P, P)], ACT.Copy).then_inc(signal, 1)

            def high_z(b, s):
                act.wait_ge(s_mm2, b + 1)
                nc.scalar.activation(xhl[:, b, 0], ps[:, 2 + s, :], ACT.Copy,
                                     scale=zscale[:, bass.ds(b, 1)]).then_inc(s_zhi, 1)

            act.wait_ge(s_mm1, NB)
            for s in range(2):
                stage(sym8, s, s, s_st2)
            with act.Fori(0, NB - 3, 2) as b0:
                for s in range(2):
                    high_z(b0 + s, s)
                    stage(sym8, b0 + s + 2, s, s_st2)
            for s in range(2):
                high_z(NB - 2 + s, s)
                stage(adjT8, s, s, s_st3)
            with act.Fori(0, NB - 3, 2) as b0:
                for s in range(2):
                    act.wait_ge(s_mm3, b0 + s + 1)
                    stage(adjT8, b0 + s + 2, s, s_st3)
                    deviation(s_var3, s_root3, b0 + s, s)
            for s in range(2):
                deviation(s_var3, s_root3, NB - 2 + s, s)

        @block.vector
        def _(dve):
            V = nc.vector
            chain = [0]

            def link(ins):
                chain[0] += 1
                ins.then_inc(s_dve, 1)
                dve.wait_ge(s_dve, chain[0])

            def wide(v, mid):
                return v.unsqueeze(1).to_broadcast([v.shape[0], mid, v.shape[1]])

            def deep(v, last):
                return v.unsqueeze(2).to_broadcast([v.shape[0], v.shape[1], last])

            intA, intB = raw.rearrange("p c f -> p (c f)")[:, 0:EC], raw.rearrange("p c f -> p (c f)")[:, EC:2 * EC]

            def one_hot_high():
                link(V.tensor_copy(key16, key))
                link(V.tensor_copy(intA, key))
                link(V.tensor_single_scalar(intB, intA, LOG_LO, ALU.logical_shift_right))
                link(V.tensor_tensor(hot, wide(iota[0:EP], EC), deep(intB, HI), ALU.is_equal))

            def one_hot_low():
                link(V.tensor_single_scalar(intA, intA, LO - 1, ALU.bitwise_and))
                V.tensor_tensor(hotlo, wide(iota[0:EP, 0:LO], EC), deep(intA, LO), ALU.is_equal).then_inc(s_hot, 1)

            dve.wait_ge(s_raw, 16)
            link(V.tensor_single_scalar(adj_idx, raw[:, :, 0], LOG_N, ALU.logical_shift_left))
            V.tensor_tensor(adj_idx, adj_idx, raw[:, :, 1], ALU.bitwise_or).then_inc(s_idx, 1)
            link(V.tensor_copy(payload[:, 0], raw[:, :, 0]))
            link(V.tensor_copy(payload[:, 1], raw[:, :, 1]))
            link(V.tensor_copy(key, payload[:, 1]))
            dve.wait_ge(s_const, 1)
            one_hot_high()
            dve.wait_ge(s_b, 32)
            link(V.tensor_copy(bias_hi, bias_in))
            link(V.tensor_copy(bias16[0:1], bias_hi[0:1]))
            link(V.tensor_tensor(bias_in, bias_in, bias_hi, ALU.subtract))
            link(V.tensor_copy(bias_mid, bias_in))
            link(V.tensor_copy(bias16[32:33], bias_mid[32:33]))
            V.tensor_tensor(bias16[64:65], bias_in[64:65], bias_mid[64:65], ALU.subtract).then_inc(s_bias, 1)
            for g in range(TRANSPOSES):
                dve.wait_ge(s_trhi, g + 1)
                if g < 2 * KB:
                    w, scale = wT[:, g // KB, g % KB], WS
                    lo, hi = w[:, 1], w[:, 0]
                else:
                    k, c = divmod(g - 2 * KB, 4)
                    lo, hi, scale = xT[:, k, 1, c * 512:(c + 1) * 512], xT[:, k, 0, c * 512:(c + 1) * 512], XS
                V.scalar_tensor_tensor(lo, ps[:, g % 2, :], scale, hi, ALU.mult, ALU.subtract).then_inc(s_trlo, 1)
            one_hot_low()

            def row_degrees():
                dve.wait_ge(s_adjrow, NB)
                for b in range(NB):
                    link(V.scalar_tensor_tensor(junk, sym8[:, b, b * P:(b + 1) * P], 1.0, ident32, ALU.mult, ALU.mult,
                                                accum_out=adjii[:, b:b + 1]))
                V.tensor_tensor(degm, rowsum, adjii, ALU.subtract).then_inc(s_degm, 1)

            def sort(n):
                fields, payhot = FIELDS[n], payhots[n]
                link(V.memset(restart, 1.0))
                link(V.memset(restart[:, :, 0:1], 0.0))
                with dve.Fori(0, G4) as g:
                    dve.wait_ge(s_group, G4 * n + g + 1)
                    for u in range(4):
                        keys = ps[0:EP, 3 + g % 2, u * P:u * P + EP]
                        r = V.scalar_tensor_tensor(keys, keys, key[:, bass.ds(4 * g + u, 1)], lower[:, 0:EP],
                                                   ALU.is_equal, ALU.mult,
                                                   accum_out=rank[:, bass.ds(4 * g + u, 1)])
                    r.then_inc(s_rank, 1)
                dve.wait_ge(s_rank, G4 * (n + 1))
                if n == 1:
                    row_degrees()
                link(V.tensor_copy(cnt, ps_cnt[:, 0:EC * LO].rearrange("p (c b) -> p b c", b=LO)))
                link(V.tensor_tensor_scan(incl.rearrange("p b c -> p (b c)"), restart.rearrange("p b c -> p (b c)"),
                                          cnt.rearrange("p b c -> p (b c)"), 0.0, ALU.mult, ALU.add))
                link(V.tensor_copy(tot, incl[:, :, LASTCOL]))
                link(V.tensor_tensor_scan(off, tot, zeros[:, 0:LO], 0.0, ALU.add, ALU.add))
                V.tensor_copy(rowtot, off[:, LO - 1:LO]).then_inc(s_rowtot, 1)
                link(V.tensor_tensor(incl, incl, cnt, ALU.subtract))
                dve.wait_ge(s_aoff, n + 1)
                link(V.tensor_copy(aoff, ps[:, 2, 0:1]))
                link(V.scalar_tensor_tensor(off, off, aoff, tot, ALU.add, ALU.subtract))
                link(V.tensor_tensor(incl, incl, deep(off, EC), ALU.add))
                high, low = (tab[:, :, f].rearrange("p c b -> p b c") for f in (0, 1))
                link(V.tensor_scalar(cnt, incl, 1.0 / P, MAGIC, ALU.mult, ALU.add))
                link(V.tensor_scalar(high, cnt, MAGIC, None, ALU.subtract))
                if n == 1:
                    dve.wait_ge(s_degr, 16)
                    link(V.tensor_copy(tab[:, :, 2], wide(degr, EC)))
                V.scalar_tensor_tensor(low, high, -float(P), incl, ALU.mult, ALU.add).then_inc(s_tab, 1)
                with dve.Fori(0, G8) as g:
                    dve.wait_ge(s_pick, G8 * n + g + 1)
                    took = picked[:, g % 2, 0:8 * fields * LO].rearrange("p (c f b) -> p c f b", c=8, f=fields)
                    src = ps[0:EP, 3 + g % 2, 0:8 * fields * LO].rearrange("p (c f b) -> p c f b", c=8, f=fields)
                    low_hot = hotlo[:, bass.ds(8 * g, 8)].unsqueeze(2).to_broadcast([EP, 8, fields, LO])
                    V.tensor_tensor(took, src, low_hot, ALU.mult).then_inc(s_pickmul, 1)
                    dve.wait_ge(s_pickmul, G8 * n + g + 1)
                    V.tensor_reduce(posf[:, bass.ds(8 * g, 8), 0:fields], took, AX.X, ALU.add).then_inc(s_picked, 1)
                dve.wait_ge(s_picked, G8 * (n + 1))
                link(V.scalar_tensor_tensor(tcol, posf[:, :, 0], float(P), posf[:, :, 1], ALU.mult, ALU.add))
                link(V.tensor_tensor(rank, rank, tcol, ALU.add))
                whole, part, size = ((tcol, tpart, EP), (tpart, tcol, EC))[n]
                link(V.tensor_scalar(whole, rank, -(size - 1) / 2.0, 1.0 / size, ALU.add, ALU.mult))
                link(V.tensor_scalar(whole, whole, MAGIC, None, ALU.add))
                link(V.tensor_scalar(whole, whole, MAGIC, None, ALU.subtract))
                link(V.scalar_tensor_tensor(part, whole, -float(size), rank, ALU.mult, ALU.add))
                if n == 0:
                    dve.wait_ge(s_valid, 16 * EC)
                    link(V.tensor_scalar(valid, valid, 1.0, 2.0, ALU.is_equal, ALU.mult))
                    link(V.tensor_scalar(valid, valid, -1.0, None, ALU.add))
                    link(V.scalar_tensor_tensor(payload[:, 0], payload[:, 0], 1.0, valid, ALU.add, ALU.mult))
                else:
                    link(V.tensor_copy(payload[:, 2], posf[:, :, 2]))
                    dve.wait_ge(s_kst, 16 * NB)
                    dve.wait_ge(s_qst, 16 * NB)
                V.tensor_tensor(tgt, wide(iota[0:EP, 0:EP], EC), deep(tpart, EP), ALU.is_equal)
                with dve.Fori(0, EC - 3, 4) as c0:
                    for c in range(4):
                        for f in range(fields):
                            r = V.tensor_scalar(payhot[:, c0 + c, f], iota[0:EP, 0:EC], tcol[:, bass.ds(c0 + c, 1)],
                                                payload[:, f, bass.ds(c0 + c, 1)], ALU.is_equal, ALU.mult)
                        r.then_inc(s_onehots, 1)
                dve.wait_ge(s_perm, n + 1)
                V.tensor_copy(payload[:, 0:fields],
                              ps[0:EP, 5, 0:fields * EC].rearrange("p (f c) -> p f c", f=fields)).then_inc(s_permcopied, 1)
                dve.wait_ge(s_permcopied, n + 1)

            sort(0)
            link(V.scalar_tensor_tensor(key, payload[:, 0], -1.0, payload[:, 0], ALU.mult, ALU.max))
            link(V.tensor_scalar(key, key, -1.0, None, ALU.add))
            one_hot_high()
            one_hot_low()
            sort(1)

            link(V.scalar_tensor_tensor(sub, payload[:, 0], -1.0, payload[:, 0], ALU.mult, ALU.max))
            link(V.tensor_scalar(sub, sub, -1.0, None, ALU.add))
            link(V.tensor_copy(subI, sub))
            V.tensor_copy(objI, payload[:, 1]).then_inc(s_eidx, 1)
            link(V.tensor_copy(obj, payload[:, 1]))
            link(V.tensor_copy(degE, payload[:, 2]))
            link(V.memset(shift, 0.0))
            link(V.tensor_copy(shift[:, 1:EP], ident16[0:EP, 0:EP - 1]))
            link(V.tensor_scalar(before16[:, 0, 0:1], sub[:, LASTCOL:EC], 1.0, None, ALU.add))
            V.tensor_copy(before16[:, 0, 1:2], obj[:, LASTCOL:EC]).then_inc(s_before16, 1)
            link(V.memset(flagF, 0.0))
            link(V.memset(flagB, 0.0))
            link(V.tensor_tensor(flagF[:, :, 1:EC], wide(sub[:, 1:EC], NV), wide(sub[:, 0:LASTCOL], NV), ALU.is_equal))
            link(V.tensor_copy(flagB[:, :, 0:LASTCOL], flagF[:, :, 1:EC]))
            link(V.tensor_scalar(selF, sub, sub[:, 0:1], None, ALU.is_equal))
            link(V.tensor_scalar(selL, sub, sub[:, LASTCOL:EC], None, ALU.is_equal))
            dve.wait_ge(s_before, 1)
            link(V.tensor_copy(before, ps[0:EP, 6, 0:2]))
            link(V.tensor_tensor(tmpE[:, 1:EC], obj[:, 1:EC], obj[:, 0:LASTCOL], ALU.is_equal))
            link(V.tensor_tensor(tmpE[:, 1:EC], tmpE[:, 1:EC], flagF[:, 0, 1:EC], ALU.mult))
            link(V.scalar_tensor_tensor(tmpE[:, 0:1], sub[:, 0:1], 1.0, before[:, 0:1], ALU.add, ALU.is_equal))
            link(V.scalar_tensor_tensor(tmpE[:, 0:1], obj[:, 0:1], before[:, 1:2], tmpE[:, 0:1], ALU.is_equal, ALU.mult))
            link(V.tensor_scalar(tmpE, tmpE, -1.0, 1.0, ALU.mult, ALU.add))
            link(V.tensor_tensor(weight, sub, obj, ALU.not_equal))
            link(V.tensor_tensor(weight, weight, tmpE, ALU.mult))
            link(V.scalar_tensor_tensor(weight, payload[:, 0], 0.0, weight, ALU.is_gt, ALU.mult))
            link(V.tensor_scalar(cidx, subI, LOG_P, LOG_N + LOG_P, ALU.logical_shift_right, ALU.logical_shift_left))
            link(V.tensor_scalar(tmpI, objI, P - 1, LOG_N, ALU.bitwise_and, ALU.logical_shift_left))
            link(V.tensor_tensor(cidx, cidx, tmpI, ALU.bitwise_or))
            link(V.tensor_scalar(tmpI, objI, LOG_P, LOG_P, ALU.logical_shift_right, ALU.logical_shift_left))
            link(V.tensor_tensor(cidx, cidx, tmpI, ALU.bitwise_or))
            link(V.tensor_single_scalar(tmpI, subI, P - 1, ALU.bitwise_and))
            link(V.tensor_tensor(cidx, cidx, tmpI, ALU.bitwise_or))
            link(V.tensor_scalar(tmpI, weight, 0.0, None, ALU.is_equal))
            link(V.tensor_single_scalar(tmpI, tmpI, 2 * LOG_N + 1, ALU.logical_shift_left))
            link(V.tensor_tensor(cidx, cidx, tmpI, ALU.bitwise_or))
            link(V.tensor_scalar(tot, tot, 0.0, float(2 * E), ALU.is_equal, ALU.mult))
            link(V.tensor_tensor(rowI, tot, off, ALU.add))
            e0 = 1.0 - DIAG
            link(V.tensor_scalar(tot, degr, e0, 1.0, ALU.mult, ALU.add))
            link(V.reciprocal(rowv[:, :, 1], tot))
            V.tensor_scalar(rowv[:, :, 0], rowv[:, :, 1], e0, None, ALU.mult).then_inc(s_default, 1)

            def scores(c0, first):
                for s in range(SLOTS + 1):
                    if s < SLOTS:
                        dve.wait_ge(s_rows[s], c0 * 4 + 32)
                        if not first or s >= 4:
                            dve.wait_ge(s_att, c0 + s - 3)
                        V.tensor_tensor(prod[:, s % 4], rows[:, s, 0], rows[:, s, 1], ALU.mult).then_inc(s_prod, 1)
                    if s:
                        dve.wait_ge(s_prod, c0 + s)
                        V.tensor_reduce(att[:, :, bass.ds(c0 + s - 1, 1)].rearrange("p h o -> p (h o)"),
                                        prod[:, (s - 1) % 4].rearrange("p (h d) -> p h d", h=HEADS),
                                        AX.X, ALU.add).then_inc(s_att, 1)

            def scores_and_rows(b0, first):
                scores(b0 * (SLOTS // 2), first)
                for s in range(2):
                    V.scalar_tensor_tensor(sym8[:, b0 + s], adjT8[:, b0 + s], 0.0, sym8[:, b0 + s], ALU.add, ALU.add,
                                           accum_out=vscale[:, bass.ds(b0 + s, 1)]).then_inc(s_sym, 1)
                    dve.wait_ge(s_xhi, b0 + s + 1)
                    V.scalar_tensor_tensor(xhl[:, b0 + s, 1], x_in[:, s], XS, xhl[:, b0 + s, 0],
                                           ALU.mult, ALU.subtract).then_inc(s_xlo, 1)

            scores_and_rows(0, True)
            with dve.Fori(2, NB - 1, 2) as b0:
                scores_and_rows(b0, False)
            with dve.Fori(NB * SLOTS // 2, EC - SLOTS + 1, SLOTS) as c0:
                scores(c0, False)
            dve.wait_ge(s_sym, NB)
            for b in range(NB):
                blk = sym8[:, b, b * P:(b + 1) * P]
                link(V.scalar_tensor_tensor(blk, ident32, 2.0, blk, ALU.mult, ALU.add))
            V.tensor_scalar(dinv, vscale, 0.5, 1.0, ALU.mult, ALU.add).then_inc(s_deg, 1)
            dve.wait_ge(s_degroot, 1)
            link(V.reciprocal(dinv, dinv))
            link(V.tensor_scalar(vscale, dinv, VS, None, ALU.mult))
            link(V.tensor_scalar(zscale, dinv, ZS / (2 * VS), None, ALU.mult))

            def row_totals(n, heads, op):
                v, f, b, ff, fb = (a[:, 0:heads].rearrange("p h c -> p (h c)") for a in (val, scF, scB, flagF, flagB))
                link(V.tensor_tensor_scan(f, ff, v, 0.0, ALU.mult, op))
                link(V.tensor_tensor_scan(b[:, ::-1], fb[:, ::-1], v[:, ::-1], 0.0, ALU.mult, op))
                if op is ALU.max:
                    link(V.tensor_tensor(f, f, b, op))
                else:
                    link(V.tensor_tensor(f, f, b, op))
                    link(V.tensor_tensor(f, f, v, ALU.subtract))
                T = scF[:, 0:heads]
                link(V.memset(piece, 0.0))
                link(V.tensor_copy(piece[:, 0, 0:1], sub[:, 0:1]))
                link(V.tensor_copy(piece[:, 1, 0:1], sub[:, LASTCOL:EC]))
                link(V.tensor_copy(piece[:, 0, 1:1 + heads], T[:, :, 0]))
                link(V.tensor_scalar(tmpE[:, 0:1], sub[:, 0:1], sub[:, LASTCOL:EC], None, ALU.not_equal))
                V.tensor_scalar(piece[:, 1, 1:1 + heads], T[:, :, LASTCOL], tmpE[:, 0:1], None,
                                ALU.mult).then_inc(s_piece, 1)
                dve.wait_ge(s_rec[n], 16)
                for k, edge in ((0, sub[:, 0:1]), (1, sub[:, LASTCOL:EC])):
                    link(V.tensor_scalar(eqs[:, k], rec[:, :, 0], edge, None, ALU.is_equal))
                for k in range(2):
                    link(V.tensor_tensor(recprod[:, 0:heads], rec[:, :, 1:1 + heads].rearrange("p q h -> p h q"),
                                         wide(eqs[:, k], heads), ALU.mult))
                    link(V.tensor_reduce(totals[:, k, 0:heads], recprod[:, 0:heads], AX.X, op))
                for k, sel in ((0, selF), (1, selL)):
                    other = scB[:, 0:heads]
                    link(V.tensor_tensor(other, deep(totals[:, k, 0:heads], EC), T, ALU.subtract))
                    link(V.tensor_tensor(other, other, wide(sel, heads), ALU.mult))
                    link(V.tensor_tensor(T, T, other, ALU.add))

            dve.wait_ge(s_att, EC)
            link(V.tensor_scalar(att, att, DK ** -0.5, None, ALU.mult))
            link(V.scalar_tensor_tensor(val[:, 0:HEADS].rearrange("p h c -> p (h c)"),
                                        att.rearrange("p h c -> p (h c)"), 0.0,
                                        att.rearrange("p h c -> p (h c)"), ALU.max, ALU.max))
            link(V.tensor_tensor(val[:, 0:HEADS], val[:, 0:HEADS], wide(weight, HEADS), ALU.mult))
            row_totals(0, HEADS, ALU.max)
            top = scF[:, 0:HEADS]
            link(V.tensor_scalar(top, top, DIAG, None, ALU.max))
            link(V.tensor_tensor(arg[:, 0], att, top, ALU.subtract))
            link(V.tensor_scalar(arg[:, 0], arg[:, 0], 0.0, None, ALU.min))
            link(V.tensor_scalar(arg[:, 1], top, -1.0, None, ALU.mult))
            V.tensor_scalar(arg[:, 2], top, -1.0, DIAG, ALU.mult, ALU.add).then_inc(s_args, 1)
            dve.wait_ge(s_exp, 1)
            link(V.tensor_tensor(val[:, 0:HEADS], arg[:, 0], wide(weight, HEADS), ALU.mult))
            link(V.tensor_copy(val[:, HEADS], weight))
            row_totals(1, NV, ALU.add)
            den = scF[:, 0:HEADS]
            link(V.tensor_tensor(tmpE, degE, scF[:, HEADS], ALU.subtract))
            link(V.tensor_tensor(scB[:, 0:HEADS], arg[:, 1], wide(tmpE, HEADS), ALU.mult))
            link(V.tensor_tensor(den, den, scB[:, 0:HEADS], ALU.add))
            link(V.tensor_tensor(den, den, arg[:, 2], ALU.add))
            link(V.reciprocal(den, den))
            for k in range(3):
                link(V.tensor_tensor(arg[:, k], arg[:, k], den, ALU.mult))
                link(V.tensor_reduce(sums[:, k], arg[:, k].rearrange("p h c -> p c h"), AX.X, ALU.add))
            link(V.tensor_scalar(edge_rows[:, :, 0], sums[:, 1], 1.0 / HEADS, None, ALU.mult))
            V.tensor_scalar(edge_rows[:, :, 1], sums[:, 2], 1.0 / HEADS, None, ALU.mult).then_inc(s_edge, 1)
            link(V.tensor_tensor(corrE, sums[:, 0], sums[:, 1], ALU.subtract))
            V.tensor_scalar(corrE, corrE, AS / HEADS, None, ALU.mult).then_inc(s_corr, 1)
            dve.wait_ge(s_rowg, 16 * LO)
            link(V.tensor_copy(off, rowv[:, :, 0]))
            V.tensor_copy(tot, rowv[:, :, 1]).then_inc(s_split, 1)
            dve.wait_ge(s_rowld, 48)
            link(V.tensor_tensor(baseC, baseC, adjii, ALU.mult))
            link(V.tensor_tensor(dcorr, dcorr, baseC, ALU.subtract))

            def scaled(b, s, first):
                if not first:
                    dve.wait_ge(s_agglo, b - 1)
                V.scalar_tensor_tensor(agg[:, s], adjT8[:, :, bass.ds(b * P, P)], AS,
                                       wide(baseB[:, bass.ds(b * P, P)], NB), ALU.mult, ALU.mult).then_inc(s_scaled, 1)

            def low(b, s):
                dve.wait_ge(s_agghi, b + 1)
                V.tensor_tensor(agghl[:, s, 1], agg[:, s], agghl[:, s, 0], ALU.subtract).then_inc(s_agglo, 1)

            def normalise(signal, variance, root, b, s, done):
                V.bn_stats(stat[:, s, 0:6], res).then_inc(signal, 1)
                dve.drain()
                V.bn_aggr(stat[:, s, 6:8], stat[:, s, 0:6]).then_inc(signal, 1)
                dve.wait_ge(signal, 3 * b + 2)
                V.tensor_scalar(stat[:, s, 0:1], stat[:, s, 7:8], EPS, None, ALU.add).then_inc(variance, 1)
                dve.wait_ge(root, b + 1)
                V.reciprocal(stat[:, s, 0:1], stat[:, s, 1:2]).then_inc(signal, 1)
                dve.wait_ge(signal, 3 * b + 3)
                V.tensor_scalar(nrm[:, s], res, stat[:, s, 6:7], stat[:, s, 0:1], ALU.subtract, ALU.mult).then_inc(done, 1)

            def post1(b, s, first):
                dve.wait_ge(s_xt[s], (b - s) * 8 + 16)
                if not (first and s == 0):
                    dve.wait_ge(s_x1, b)
                V.scalar_tensor_tensor(res, xt[:, s], dcorr[:, bass.ds(b, 1)], xt[:, s], ALU.mult,
                                       ALU.add).then_inc(s_dg, 1)
                dve.wait_ge(s_dg, b + 1)
                dve.wait_ge(s_mm1, b + 1)
                V.scalar_tensor_tensor(res, ps[:, s, :], 1.0 / (AS * XS), res, ALU.mult, ALU.add).then_inc(s_res1, 1)
                dve.wait_ge(s_res1, b + 1)
                if not first:
                    dve.wait_ge(s_x1st[s], (b - s) * 8)
                    dve.wait_ge(s_vlo, b - 1)
                normalise(s_ln1, s_var1, s_root1, b, s, s_x1)
                dve.wait_ge(s_vhi, b + 1)
                V.scalar_tensor_tensor(vhl[:, b, 1], nrm[:, s], vscale[:, bass.ds(b, 1)], vhl[:, b, 0], ALU.mult,
                                       ALU.subtract).then_inc(s_vlo, 1)

            dve.wait_ge(s_scat, 16 * EC)
            scaled(0, 0, True)
            scaled(1, 1, True)
            low(0, 0)
            scaled(2, 0, False)
            low(1, 1)
            post1(0, 0, True)
            scaled(3, 1, False)
            low(2, 0)
            post1(1, 1, True)
            with dve.Fori(3, NB - 2, 2) as b:
                scaled(b + 1, 0, False)
                low(b, 1)
                post1(b - 1, 0, False)
                scaled(b + 2, 1, False)
                low(b + 1, 0)
                post1(b, 1, False)
            low(NB - 1, 1)
            post1(NB - 2, 0, False)
            post1(NB - 1, 1, False)

            with dve.Fori(0, NB - 1, 2) as b0:
                for s in range(2):
                    dve.wait_ge(s_zhi, b0 + s + 1)
                    V.scalar_tensor_tensor(xhl[:, b0 + s, 1], ps[:, 2 + s, :], zscale[:, bass.ds(b0 + s, 1)],
                                           xhl[:, b0 + s, 0], ALU.mult, ALU.subtract).then_inc(s_zlo, 1)

            def post3(b, s, first):
                dve.wait_ge(s_x1in[s], (b - s) * 8 + 16)
                if not (first and s == 0):
                    dve.wait_ge(s_y, b)
                dve.wait_ge(s_mm3, b + 1)
                V.scalar_tensor_tensor(res, ps[:, 2 + s, :], 1.0 / ZS, xt[:, s], ALU.mult, ALU.add).then_inc(s_res3, 1)
                dve.wait_ge(s_res3, b + 1)
                if not first:
                    dve.wait_ge(s_out[s], (b - s) * 8)
                normalise(s_ln3, s_var3, s_root3, b, s, s_y)

            post3(0, 0, True)
            post3(1, 1, True)
            with dve.Fori(2, NB - 1, 2) as b0:
                for s in range(2):
                    post3(b0 + s, s, False)


_INS = ['x', 'adj', 'L0_gnn_rel_pair_index', 'L0_gnn_Wq', 'L0_gnn_bq', 'L0_gnn_Wk', 'L0_gnn_bk']
_OUTS = [((2048, 512), 'float32')]


def kernel(**inputs):
    import numpy as _np
    import concourse.bacc as _bacc
    from concourse import mybir as _mybir
    from concourse.bass_utils import run_bass_kernel_spmd as _run

    nc = _bacc.Bacc("TRN2", target_bir_lowering=False, num_devices=1)
    arrays, args = {}, []
    for name in _INS:
        a = _np.ascontiguousarray(inputs[name])
        arrays[f"in_{name}_dram"] = a
        args.append(nc.dram_tensor(f"in_{name}_dram", a.shape, _mybir.dt.from_np(a.dtype), kind="ExternalInput").ap())
    for i, (shape, dtype) in enumerate(_OUTS):
        dt = _mybir.dt.from_np(_np.dtype(dtype))
        args.append(nc.dram_tensor(f"out_{i}_dram", shape, dt, kind="ExternalOutput").ap())
    gnn_resnorm_kernel(nc, *args)
    r = _run(nc, [arrays], core_ids=[0])
    return r.results[0]["out_0_dram"]
```

```python
import concourse.bass as bass
from concourse import mybir
from contextlib import ExitStack


def gnn_resnorm_kernel(nc: bass.Bass, x: bass.AP, adj: bass.AP, pairs: bass.AP, wq: bass.AP, bq: bass.AP,
                       wk: bass.AP, bk: bass.AP, out: bass.AP):
    f32, f16, i32 = mybir.dt.float32, mybir.dt.float16, mybir.dt.int32
    u8, u16 = mybir.dt.uint8, mybir.dt.uint16
    ALU, ACT, AX = mybir.AluOpType, mybir.ActivationFunctionType, mybir.AxisListType
    SIZE = {f32: 4, f16: 2, i32: 4, u8: 1}

    N, D = x.shape
    E = pairs.shape[0]
    P, HEADS, DK = 128, 8, 64
    NB, KB = N // P, D // P
    EC = 80
    EP = E // EC
    HI, LO = P, N // P
    G4, G8 = EC // 4, EC // 8
    SLOTS = 8
    NV = HEADS + 1
    MAGIC = 1.5 * 2.0 ** 23
    XS, WS, VS, ZS, AS = 2.0 ** 4, 2.0 ** 6, 2.0 ** 10, 2.0 ** 5, 2.0 ** 14
    EPS, DIAG = 1e-5, 1e-7
    LASTCOL, LASTROW = EC - 1, EP - 1
    K = 1024
    LOG_N, LOG_P, LOG_LO = 11, 7, 4
    assert EP * EC == E and EP <= P and HEADS * DK == D and HI * LO == N
    assert (1 << LOG_N, 1 << LOG_P, 1 << LOG_LO) == (N, P, LO)

    q_tab = nc.dram_tensor("q_tab", (N, D), f32).ap()
    k_tab = nc.dram_tensor("k_tab", (N, D), f32).ap()
    corr_tab = nc.dram_tensor("corr_tab", (N * N, 1), f32).ap()
    deg_tab = nc.dram_tensor("deg_tab", (N,), f32).ap()
    base_tab = nc.dram_tensor("base_tab", (N,), f32).ap()
    diag_tab = nc.dram_tensor("diag_tab", (N,), f32).ap()
    edge_tab = nc.dram_tensor("edge_tab", (E, 2), f32).ap()
    piece_tab = [nc.dram_tensor(f"piece_tab{n}", (2 * EP, 10), f32).ap() for n in range(2)]
    x1_tab = nc.dram_tensor("x1_tab", (N, D), f32).ap()

    ctx = ExitStack()
    with ctx:
        ARENA = 212800
        arena = ctx.enter_context(nc.sbuf_tensor("arena", [P, ARENA], u8))
        ps = ctx.enter_context(nc.psum_tensor("ps", [P, 8, 512], f32))

        def place(first, shape, dt, end=None):
            n = SIZE[dt]
            for s in shape[1:]:
                n *= s
            assert first % 4 == 0 and first + n <= (end or ARENA), (first, n)
            v = arena[0:shape[0], first:first + n].bitcast(dt)
            names = "abcde"[:len(shape) - 1]
            if len(shape) > 2:
                v = v.rearrange(f"p ({' '.join(names)}) -> p {' '.join(names)}",
                                **{c: s for c, s in zip(names[1:], shape[2:])})
            return v

        def row_of(first, end):
            here = [first]

            def take(shape, dt=f32):
                v = place(here[0], shape, dt, end)
                n = SIZE[dt]
                for s in shape[1:]:
                    n *= s
                here[0] += (n + 3) // 4 * 4
                return v
            return take

        def sem(name):
            return ctx.enter_context(nc.semaphore(name))

        sym8 = place(0, [P, NB, N], u8)
        bias_in = place(32 * K, [P, 2, D], f32)
        bias_hi, bias_mid = place(36 * K, [P, 2, D], f16), place(38 * K, [P, 2, D], f16)
        adjT8 = place(32 * K, [P, NB, N], u8)
        xf = place(64 * K, [P, NB, D], f32)
        t_ = row_of(64 * K, 92 * K)
        cnt, incl = t_([P, LO, EC]), t_([P, LO, EC])
        tab = t_([P, EC, 3, LO], f16)
        picked = t_([EP, 2, 8 * 3 * LO])
        posf = t_([EP, EC, 3])
        restart = t_([P, LO, EC], f16)
        hotlo = t_([EP, EC, LO], f16)
        rank, junk = t_([EP, EC]), t_([P, P], f16)
        rowparts = t_([P, NB, 4])
        payhot = place(64 * K, [EP, EC, 2, EC], f16)
        proj = place(92 * K, [P, 2, D], f32)
        rows = place(64 * K, [EP, SLOTS, 2, D], f32)
        vhl = place(64 * K, [P, NB, 2, D], f16)
        xT = place(96 * K, [P, KB, 2, N], f16)
        e_ = row_of(96 * K, 128 * K)
        att = e_([EP, HEADS, EC])
        flagF, flagB = e_([EP, NV, EC], f16), e_([EP, NV, EC], f16)
        val, scF, scB = e_([EP, NV, EC]), e_([EP, NV, EC]), e_([EP, NV, EC])
        arg = e_([EP, 3, HEADS, EC])
        sub, obj, degE, weight = (e_([EP, EC]) for _ in range(4))
        selF, selL, tmpE = (e_([EP, EC]) for _ in range(3))
        subI, objI, tmpI, cidx = (e_([EP, EC], i32) for _ in range(4))
        sums, corrE, edge_rows = e_([EP, 3, EC]), e_([EP, EC]), e_([EP, EC, 2])
        piece, totals = e_([EP, 2, 10]), e_([EP, 2, NV])
        before16, before = e_([EP, 2, 4], f16), e_([EP, 2])
        corr_in = place(96 * K, [P, 2, NB, P], f32)
        agg = place(112 * K, [P, 2, NB, P], f32)
        wT = place(128 * K, [P, 2, KB, 2, D], f16)
        adj_in = place(144 * K, [P, 2, N], f32)
        deghot = place(144 * K, [EP, EC, EC], f16)
        xhl = place(128 * K, [P, NB, 2, D], f16)
        hot = place(160 * K, [EP, EC, HI], f16)
        tgt = place(160 * K, [EP, EC, EP], f16)
        rec = place(160 * K, [EP, 2 * EP, 10], f32)
        recprod = place(170 * K, [EP, NV, 2 * EP], f32)
        agghl = place(160 * K, [P, 2, 2, NB, P], f16)
        stage16 = place(160 * K, [P, 2, NB, P], f16)
        w_in = place(180 * K, [P, 2, KB, D], f32)
        hotT = place(180 * K, [P, EC, EP], f16)
        b_ = row_of(180 * K, 180 * K + 20000)
        prod = b_([EP, 4, D])
        x_in = b_([P, 2, D])
        eqs = b_([EP, 2, 2 * EP])
        shift = b_([EP, EP], f16)
        c_ = row_of(180 * K, 180 * K + 20000)
        res, xt, nrm = c_([P, D]), c_([P, 2, D]), c_([P, 2, D])
        baseB = c_([P, N])
        k_ = row_of(180 * K + 20000, ARENA)
        raw = k_([EP, EC, 2], i32)
        q32 = raw.rearrange("p c f -> p (c f)").bitcast(f32)
        tcol, tpart = q32[:, 0:EC], q32[:, EC:2 * EC]
        adj_idx, valid = k_([EP, EC], i32), k_([EP, EC])
        key, key16 = k_([EP, EC]), k_([EP, EC], f16)
        payload = k_([EP, 3, EC])
        off, tot = k_([P, LO]), k_([P, LO])
        rowsum, adjii, degm, dinv, dcorr, vscale, zscale, baseC = (k_([P, NB]) for _ in range(8))
        degr, rowI = k_([P, LO]), k_([P, LO], i32)
        rowpart, rowcol = (place(b, [P, LO], f32) for b in (126 * K, 126 * K + 64))
        rowv, stat = k_([P, LO, 2]), k_([P, 2, 8])
        rowtot, spread = k_([P, 1]), k_([P, 2])
        ones, width, perwidth, widthI = k_([P, 1]), k_([P, 1]), k_([P, 1]), k_([P, 1], i32)
        aoff, placed = spread[:, 0:1], spread[:, 1:2]
        ident32, upper = k_([P, P]), k_([P, P])
        ident16, iota = k_([P, P], f16), k_([P, P], f16)
        lower, const16 = k_([EP, EP + 1], f16), k_([P, P], f16)
        zeros = k_([P, P])
        bias16 = k_([P, 2, D], f16)

        s_const, s_zero_src, s_zeroed = sem("constants"), sem("zero_source"), sem("corr_table_zeroed")
        s_raw, s_x, s_w, s_b = sem("pairs_loaded"), sem("x_loaded"), sem("w_loaded"), sem("bias_loaded")
        s_width, s_symadd, s_symsum, s_symdiag = sem("width"), sem("sym_added"), sem("sym_summed"), sem("sym_diagonal")
        s_scattered, s_x16, s_attz = sem("scattered_all"), sem("x_scaled"), sem("attention_cleared")
        s_bias, s_idx, s_valid = sem("bias_split"), sem("adj_index"), sem("adj_picked")
        s_dve = sem("dve_chain")
        s_hot, s_group, s_hotT, s_rank = sem("hot_built"), sem("key_group"), sem("hotT_copied"), sem("ranked")
        s_cnt, s_rowtot, s_aoff = sem("counts_copied"), sem("row_totals"), sem("row_offsets")
        s_tab, s_pick, s_pickmul, s_picked = sem("table"), sem("pick_product"), sem("pick_mul"), sem("picked")
        s_columns, s_objhot, s_tgt = sem("column_one_hots"), sem("obj_one_hots"), sem("target_one_hots")
        s_onehots, s_perm, s_permcopied = sem("payload_one_hots"), sem("permuted"), sem("permuted_copied")
        s_tr, s_trhi, s_trlo = sem("transposed"), sem("transposed_hi"), sem("transposed_lo")
        s_adj = [sem(f"adj_loaded{n}") for n in range(2)]
        s_adjrow, s_fill, s_drain = sem("adj_rows_kept"), sem("stream_filled"), sem("stream_drained")
        s_kst, s_qst = sem("k_stored"), sem("q_stored")
        s_degm, s_degst, s_degr = sem("degrees"), sem("degrees_stored"), sem("degrees_by_row")
        s_eidx, s_before16, s_before = sem("edge_indices"), sem("last_edges"), sem("edge_before")
        s_rows = [sem(f"rows_gathered{n}") for n in range(SLOTS)]
        s_prod, s_att = sem("products"), sem("attention")
        s_xin = [sem(f"x_again{n}") for n in range(2)]
        s_xhi, s_xlo = sem("x_hi"), sem("x_lo")
        s_piece, s_pst = sem("pieces"), [sem(f"pieces_stored{n}") for n in range(2)]
        s_rec = [sem(f"pieces_spread{n}") for n in range(2)]
        s_args, s_exp = sem("exponents"), sem("exponentials")
        s_corr, s_scat = sem("corrections"), sem("corrections_scattered")
        s_edge, s_est = sem("edge_rows"), sem("edge_rows_stored")
        s_default, s_rowg = sem("row_defaults"), sem("row_values_gathered")
        s_split, s_rst, s_rowld = sem("row_values"), sem("row_values_stored"), sem("row_values_loaded")
        s_cin = [sem(f"corr_loaded{n}") for n in range(2)]
        s_xt = [sem(f"x_tile{n}") for n in range(2)]
        s_scaled, s_agg, s_agghi, s_agglo = sem("adj_scaled"), sem("agg"), sem("agg_hi"), sem("agg_lo")
        s_mm1, s_res1, s_ln1 = sem("agg_product"), sem("residual1"), sem("ln1_chain")
        s_x1, s_vhi, s_vlo, s_x1st = sem("x1"), sem("v_hi"), sem("v_lo"), [sem(f"x1_stored{n}") for n in range(2)]
        s_st2, s_mm2, s_zhi, s_zlo = sem("sym_staged"), sem("sym_product"), sem("z_hi"), sem("z_lo")
        s_st3, s_mm3, s_ln3, s_y = sem("adj_staged"), sem("adj_product"), sem("ln3_chain"), sem("y")
        s_x1in = [sem(f"x1_tile{n}") for n in range(2)]
        s_out = [sem(f"out_stored{n}") for n in range(2)]
        s_pool, s_res3, s_dg = sem("pool_chain"), sem("residual3"), sem("diagonal_added")
        s_deg, s_degroot = sem("symmetric_degrees"), sem("degree_roots")
        s_var1, s_root1, s_var3, s_root3 = sem("variance1"), sem("deviation1"), sem("variance3"), sem("deviation3")

        FIELDS = (2, 3)

        ps_hotT = ps[:, 2, :].bitcast(f16).rearrange("p (u e) -> p u e", u=8)
        ps_cnt = ps[:, 5:8, :].rearrange("p b c -> p (b c)")
        TRANSPOSES = 2 * KB + KB * 4
        QUARTERS = 4 * NB
        adj_q, proj_q = (lambda a, b: [("adj", i) for i in range(a, b)]), (lambda a, b: [("project", i) for i in range(a, b)])
        DURING_RANKS = ([adj_q(g, g + 1) for g in range(G4)],
                        [adj_q(52 + g, 53 + g) if g < 12 else proj_q(11 + (g - 12) // 2, 12 + (g - 12) // 2) if g % 2 else []
                         for g in range(G4)])
        DURING_OFFSETS = (adj_q(20, 24), [])
        DURING_TABLE = (adj_q(24, 28) + proj_q(0, 1), proj_q(15, 17))
        DURING_PICKS = ([adj_q(28 + g, 29 + g) for g in range(G8)],
                        [proj_q(17 + g // 3, 18 + g // 3) if g % 3 == 2 else [] for g in range(G8)])
        DURING_PLACES = (sum((adj_q(38 + 2 * i, 40 + 2 * i) + proj_q(1 + i, 2 + i) for i in range(7)), []),
                         proj_q(20, 2 * NB))
        DURING_KEYS = proj_q(8, 11)
        order = []
        for n in range(2):
            order += sum(DURING_RANKS[n], []) + DURING_OFFSETS[n] + DURING_TABLE[n]
            order += sum(DURING_PICKS[n], []) + DURING_PLACES[n] + (DURING_KEYS if n == 0 else [])
        assert sorted(order) == adj_q(0, QUARTERS) + proj_q(0, 2 * NB)
        ADJ_DRAINED = order.index(("adj", QUARTERS - 1)) + 1
        x_rows = x.rearrange("(b p) d -> p b d", p=P)
        adj_rows = adj.rearrange("(b p) j -> b p j", p=P)
        corr_blocks = corr_tab.rearrange("(b p m) o -> b p (m o)", b=NB, p=P)
        x1_rows = x1_tab.rearrange("(b p) d -> b p d", p=P)
        xb_rows = x.rearrange("(b p) d -> b p d", p=P)
        out_rows = out.rearrange("(b p) d -> b p d", p=P)
        q_rows = q_tab.rearrange("(b p) d -> b p d", p=P)
        k_rows = k_tab.rearrange("(b p) d -> b p d", p=P)

        block = ctx.enter_context(nc.Block())

        @block.sync
        def _(sp):
            sp.dma_start(raw, pairs.rearrange("(p c) f -> p c f", p=EP)).then_inc(s_raw, 16)
            sp.dma_start(bias_in[:, 0], bk.partition_broadcast(P)).then_inc(s_b, 16)
            sp.dma_start(bias_in[:, 1], bq.partition_broadcast(P)).then_inc(s_b, 16)
            sp.dma_start(w_in[:, 0], wk.rearrange("(b p) d -> p b d", p=P)).then_inc(s_w, 16)
            sp.dma_start(w_in[:, 1], wq.rearrange("(b p) d -> p b d", p=P)).then_inc(s_w, 16)
            for b in range(0, NB, 4):
                sp.dma_start(xf[:, b:b + 4], x_rows[:, b:b + 4]).then_inc(s_x, 16)
            sp.wait_ge(s_zero_src, 1)
            sp.wait_ge(s_adjrow, QUARTERS - 8)
            for b in range(NB):
                dst = corr_blocks[b].rearrange("p (a m) -> p a m", m=P)
                sp.dma_start(dst, zeros.unsqueeze(1).to_broadcast([P, NB, P])).then_inc(s_zeroed, 16)
            sp.wait_ge(s_degm, 1)
            with nc.allow_non_contiguous_dma("2048 single values"):
                sp.dma_start(deg_tab.rearrange("(b p) -> p b", p=P), degm).then_inc(s_degst, 16)
            sp.wait_ge(s_degst, 16)
            sp.dma_start(degr, deg_tab.rearrange("(a b) -> a b", b=LO)).then_inc(s_degr, 16)
            for b in range(NB):
                if b == 0:
                    sp.wait_ge(s_perm, 2)
                if b >= 2:
                    sp.wait_ge(s_xlo, b - 1)
                sp.dma_start(x_in[:, b % 2], xb_rows[b]).then_inc(s_xin[b % 2], 16)
            for n in range(2):
                sp.wait_ge(s_piece, n + 1)
                sp.dma_start(piece_tab[n].rearrange("(p k) v -> p k v", k=2), piece).then_inc(s_pst[n], 16)
                sp.wait_ge(s_pst[n], 16)
                sp.dma_start(rec.rearrange("p q v -> p (q v)"),
                             piece_tab[n].rearrange("q v -> (q v)").partition_broadcast(EP)).then_inc(s_rec[n], 16)
            sp.wait_ge(s_edge, 1)
            sp.dma_start(edge_tab.rearrange("(p c) v -> p c v", p=EP), edge_rows).then_inc(s_est, 16)
            sp.wait_ge(s_split, 1)
            sp.dma_start(base_tab.rearrange("(a b) -> a b", b=LO), off).then_inc(s_rst, 16)
            sp.dma_start(diag_tab.rearrange("(a b) -> a b", b=LO), tot).then_inc(s_rst, 16)
            sp.wait_ge(s_rst, 32)
            sp.wait_ge(s_xlo, NB)
            sp.dma_start(baseB, base_tab.partition_broadcast(P)).then_inc(s_rowld, 16)
            with nc.allow_non_contiguous_dma("2048 single values"):
                sp.dma_start(baseC, base_tab.rearrange("(b p) -> p b", p=P)).then_inc(s_rowld, 16)
                sp.dma_start(dcorr, diag_tab.rearrange("(b p) -> p b", p=P)).then_inc(s_rowld, 16)
            sp.wait_ge(s_scattered, 1)
            for b in range(2):
                sp.dma_start(corr_in[:, b].rearrange("p j i -> p (j i)"), corr_blocks[b]).then_inc(s_cin[b], 16)
                sp.dma_start(xt[:, b], xb_rows[b]).then_inc(s_xt[b], 16)
            with sp.Fori(2, NB - 1, 2) as b0:
                for s in range(2):
                    sp.wait_ge(s_agg, b0 + s - 1)
                    sp.dma_start(corr_in[:, s].rearrange("p j i -> p (j i)"),
                                 corr_blocks[b0 + s]).then_inc(s_cin[s], 16)
                    sp.wait_ge(s_res1, b0 + s - 1)
                    sp.dma_start(xt[:, s], xb_rows[b0 + s]).then_inc(s_xt[s], 16)
            for n in range(2):
                sp.wait_ge(s_x1st[n], 16 * (NB // 2))
            sp.wait_ge(s_res1, NB)
            for s in range(2):
                sp.dma_start(xt[:, s], x1_rows[s]).then_inc(s_x1in[s], 16)
            with sp.Fori(2, NB - 1, 2) as b0:
                for s in range(2):
                    sp.wait_ge(s_res3, b0 + s - 1)
                    sp.dma_start(xt[:, s], x1_rows[b0 + s]).then_inc(s_x1in[s], 16)
            for n in range(2):
                sp.wait_ge(s_out[n], 16 * (NB // 2))

        @block.gpsimd
        def _(pool):
            chain = [0]

            def link(ins):
                chain[0] += 1
                ins.then_inc(s_pool, 1)
                pool.wait_ge(s_pool, chain[0])

            nc.gpsimd.memset(zeros, 0.0).then_inc(s_zero_src, 1)
            link(nc.gpsimd.memset(ident32, 0.0))
            link(nc.gpsimd.affine_select(out=ident32, in_=ident32, compare_op=ALU.not_equal, fill=1.0, base=0,
                                         pattern=[[-1, P]], channel_multiplier=1))
            link(nc.gpsimd.tensor_copy(ident16, ident32))
            link(nc.gpsimd.iota(iota, pattern=[[1, P]], base=0, channel_multiplier=0,
                                allow_small_or_imprecise_dtypes=True))
            link(nc.gpsimd.memset(lower, 1.0))
            link(nc.gpsimd.affine_select(out=lower, in_=lower, compare_op=ALU.is_gt, fill=0.0, base=0,
                                         pattern=[[-1, EP + 1]], channel_multiplier=1))
            link(nc.gpsimd.memset(upper, 1.0))
            link(nc.gpsimd.affine_select(out=upper, in_=upper, compare_op=ALU.is_gt, fill=0.0, base=0,
                                         pattern=[[1, P]], channel_multiplier=-1))
            link(nc.gpsimd.memset(const16, XS * WS))
            link(nc.gpsimd.memset(ones, 1.0))
            nc.gpsimd.memset(bias16, 0.0).then_inc(s_const, 1)
            pool.wait_ge(s_idx, 1)
            adj_flat = adj.rearrange("i (j o) -> (i j) o", o=1)
            for c in range(EC):
                pool.indirect_dma_start(valid[:, c:c + 1], None, adj_flat,
                                        bass.IndirectOffsetOnAxis(ap=adj_idx[:, c:c + 1], axis=0)).then_inc(s_valid, 16)
            for n in range(2):
                pool.wait_ge(s_columns, n + 1)
                nc.gpsimd.tensor_tensor(payhot[:, :, 1], payhot[:, :, 0],
                                        payload[:, 1].unsqueeze(2).to_broadcast([EP, EC, EC]),
                                        ALU.mult).then_inc(s_objhot, 1)
            pool.wait_ge(s_eidx, 1)
            pool.wait_ge(s_kst, 16 * NB)
            pool.wait_ge(s_qst, 16 * NB)
            filled = pool.value_load(widthI[0:1, 0:1], min_val=1, max_val=EC)
            for g in range(G8):
                with pool.If(filled > 8 * g):
                    for c in range(8 * g, 8 * g + 8):
                        s = c % SLOTS
                        if g:
                            pool.wait_ge(s_prod, c - SLOTS + 1)
                        pool.indirect_dma_start(rows[:, s, 0], None, q_tab,
                                                bass.IndirectOffsetOnAxis(ap=subI[:, c:c + 1], axis=0)).then_inc(s_rows[s], 16)
                        pool.indirect_dma_start(rows[:, s, 1], None, k_tab,
                                                bass.IndirectOffsetOnAxis(ap=objI[:, c:c + 1], axis=0)).then_inc(s_rows[s], 16)
            with pool.Fori(0, NB - 1, 2) as b0:
                for s in range(2):
                    pool.wait_ge(s_x16, b0 + s + 1)
                    nc.gpsimd.tensor_tensor(xhl[:, b0 + s, 1], x_in[:, s], xhl[:, b0 + s, 0],
                                            ALU.subtract).then_inc(s_xlo, 1)
            pool.wait_ge(s_est, 16)
            pool.wait_ge(s_default, 1)
            for b in range(LO):
                pool.indirect_dma_start(rowv[:, b], None, edge_tab,
                                        bass.IndirectOffsetOnAxis(ap=rowI[:, b:b + 1], axis=0),
                                        bounds_check=E - 1, oob_is_err=False).then_inc(s_rowg, 16)
            pool.wait_ge(s_corr, 1)
            pool.wait_ge(s_zeroed, 16 * NB)
            for g in range(G8):
                with pool.If(filled > 8 * g):
                    for c in range(8 * g, 8 * g + 8):
                        pool.indirect_dma_start(corr_tab, bass.IndirectOffsetOnAxis(ap=cidx[:, c:c + 1], axis=0),
                                                corrE[:, c:c + 1], None,
                                                bounds_check=N * N - 1, oob_is_err=False).then_inc(s_scat, 16)
                    pool.wait_ge(s_scat, 16 * (8 * g + 8))
            nc.gpsimd.memset(ones, 1.0).then_inc(s_scattered, 1)
            with pool.Fori(0, NB - 1, 2) as b0:
                for s in range(2):
                    pool.wait_ge(s_scaled, b0 + s + 1)
                    pool.wait_ge(s_cin[s], b0 * 8 + 16)
                    nc.gpsimd.tensor_tensor(agg[:, s], agg[:, s], corr_in[:, s], ALU.add).then_inc(s_agg, 1)
            with pool.Fori(0, NB - 1, 2) as b0:
                for s in range(2):
                    pool.wait_ge(s_y, b0 + s + 1)
                    pool.dma_start(out_rows[b0 + s], nrm[:, s]).then_inc(s_out[s], 16)

        @block.tensor
        def _(pe):
            fills = [0]

            def fill(steps):
                for kind, i in steps:
                    n, bank = fills[0], fills[0] % 2
                    fills[0] += 1
                    if n >= 2:
                        pe.wait_ge(s_drain, n - 1)
                    if kind == "adj":
                        b, q = divmod(i, 4)
                        pe.wait_ge(s_adj[b % 2], 16 * (b // 2 + 1))
                        for u in range(4):
                            j = 4 * q + u
                            r = nc.tensor.transpose(ps[:, bank, u * P:(u + 1) * P],
                                                    adj_in[:, b % 2, j * P:(j + 1) * P], ident32)
                    else:
                        b, w = divmod(i, 2)
                        for k in range(KB):
                            for x_part, w_part in ((0, 0), (0, 1), (1, 0)):
                                nc.tensor.matmul(ps[:, bank, :], xT[:, k, x_part, b * P:(b + 1) * P],
                                                 wT[:, w, k, w_part], start=(k == x_part == w_part == 0), stop=False)
                        r = nc.tensor.matmul(ps[:, bank, :], const16, bias16[:, w], start=False, stop=True)
                    r.then_inc(s_fill, 1)

            def sort_groups(n):
                pe.wait_ge(s_hot, n + 1)
                if n:
                    pe.wait_ge(s_permcopied, n)
                for g in range(G4):
                    if n or g:
                        pe.wait_ge(s_hotT, G4 * n + g)
                    if g >= 2:
                        pe.wait_ge(s_rank, G4 * n + g - 1)
                    for u in range(4):
                        c = 4 * g + u
                        nc.tensor.transpose(ps_hotT[:, u, 0:EP], hot[:, c], ident16[0:EP, 0:EP])
                        nc.tensor.matmul(ps_cnt[:, c * LO:(c + 1) * LO], hot[:, c], hotlo[:, c], start=True, stop=True)
                        r = nc.tensor.matmul(ps[0:EP, 3 + g % 2, u * P:u * P + EP],
                                             key16[:, c:c + 1].to_broadcast([EP, EP]), ident16[0:EP, 0:EP],
                                             start=True, stop=True)
                    r.then_inc(s_group, 1)
                    fill(DURING_RANKS[n][g])

            def sort_offsets(n):
                fill(DURING_OFFSETS[n])
                pe.wait_ge(s_rowtot, n + 1)
                nc.tensor.matmul(ps[:, 3, 0:1], upper, rowtot, start=True, stop=True)
                nc.tensor.matmul(ps[:, 3, 1:2], rowtot.to_broadcast([P, P]), ones, start=True, stop=True).then_inc(s_aoff, 1)
                fill(DURING_TABLE[n])

            def sort_pick(n, fields):
                pe.wait_ge(s_tab, n + 1)
                pe.wait_ge(s_hotT, G4 * (n + 1))
                for g in range(G8):
                    if g >= 2:
                        pe.wait_ge(s_pickmul, G8 * n + g - 1)
                    for u in range(8):
                        c = 8 * g + u
                        r = nc.tensor.matmul(ps[0:EP, 3 + g % 2, u * fields * LO:(u + 1) * fields * LO], hotT[:, c],
                                             tab[:, c, 0:fields].rearrange("p f b -> p (f b)"), start=True, stop=True)
                    r.then_inc(s_pick, 1)
                    fill(DURING_PICKS[n][g])

            def sort_permute(n, fields):
                fill(DURING_PLACES[n])
                pe.wait_ge(s_tgt, n + 1)
                pe.wait_ge(s_onehots, n + 1)
                for c in range(EC):
                    r = nc.tensor.matmul(ps[0:EP, 5, 0:2 * EC], tgt[:, c], payhot[:, c].rearrange("p f c -> p (f c)"),
                                         start=c == 0, stop=c == LASTCOL)
                    if fields == 3:
                        r = nc.tensor.matmul(ps[0:EP, 6, 0:EC], tgt[:, c], deghot[:, c],
                                             start=c == 0, stop=c == LASTCOL)
                r.then_inc(s_perm, 1)

            pe.wait_ge(s_const, 1)
            pe.wait_ge(s_w, 32)
            for g in range(TRANSPOSES):
                if g == 2 * KB:
                    pe.wait_ge(s_x, 16 * (NB // 4))
                if g >= 8:
                    pe.wait_ge(s_trhi, g - 7)
                    pe.wait_ge(s_trlo, g - 7)
                for u in range(4):
                    if g < 2 * KB:
                        src = w_in[:, g // KB, u, (g % KB) * P:(g % KB + 1) * P]
                    else:
                        k, c = divmod(g - 2 * KB, 4)
                        src = xf[:, 4 * c + u, k * P:(k + 1) * P]
                    r = nc.tensor.transpose(ps[:, g % 8, u * P:(u + 1) * P], src, ident32)
                r.then_inc(s_tr, 1)

            pe.wait_ge(s_bias, 1)
            pe.wait_ge(s_trhi, TRANSPOSES)
            pe.wait_ge(s_trlo, TRANSPOSES)
            for n in range(2):
                sort_groups(n)
                sort_offsets(n)
                sort_pick(n, FIELDS[n])
                sort_permute(n, FIELDS[n])
                if n == 0:
                    fill(DURING_KEYS)
            pe.wait_ge(s_before16, 1)
            nc.tensor.matmul(ps[0:EP, 6, 0:2], shift, before16[:, 0, 0:2], start=True, stop=True).then_inc(s_before, 1)

            pe.wait_ge(s_xhi, NB)
            pe.wait_ge(s_xlo, NB)

            def aggregate(b0, first):
                for s in range(2):
                    if not first:
                        pe.wait_ge(s_res1, b0 + s - 1)
                    pe.wait_ge(s_agghi, b0 + s + 1)
                    pe.wait_ge(s_agglo, b0 + s + 1)
                    for k in range(NB):
                        for i, j in ((0, 0), (0, 1), (1, 0)):
                            r = nc.tensor.matmul(ps[:, s, :], agghl[:, s, i, k], xhl[:, k, j],
                                                 start=(k == 0 and i == 0 and j == 0), stop=(k == NB - 1 and i == 1))
                    r.then_inc(s_mm1, 1)

            aggregate(0, True)
            with pe.Fori(2, NB - 1, 2) as b0:
                aggregate(b0, False)
            pe.wait_ge(s_vhi, NB)
            pe.wait_ge(s_vlo, NB)
            for staged, rhs, done, read in ((s_st2, vhl, s_mm2, s_zlo), (s_st3, xhl, s_mm3, s_res3)):
                if done is s_mm3:
                    pe.wait_ge(s_zhi, NB)
                    pe.wait_ge(s_zlo, NB)

                def blocks(b0, first):
                    for s in range(2):
                        pe.wait_ge(staged, b0 + s + 1)
                        if not first:
                            pe.wait_ge(read, b0 + s - 1)
                        for k in range(NB):
                            for j in range(2):
                                r = nc.tensor.matmul(ps[:, 2 + s, :], stage16[:, s, k], rhs[:, k, j],
                                                     start=(k == 0 and j == 0), stop=(k == NB - 1 and j == 1))
                        r.then_inc(done, 1)

                blocks(0, True)
                with pe.Fori(2, NB - 1, 2) as b0:
                    blocks(b0, False)

        @block.scalar
        def _(act):
            act.dma_start(adj_in[:, 0], adj_rows[0]).then_inc(s_adj[0], 16)
            act.dma_start(adj_in[:, 1], adj_rows[1]).then_inc(s_adj[1], 16)
            act.wait_ge(s_const, 1)
            for g in range(TRANSPOSES):
                act.wait_ge(s_tr, g + 1)
                if g < 2 * KB:
                    dst, scale = wT[:, g // KB, g % KB, 0], WS
                else:
                    k, c = divmod(g - 2 * KB, 4)
                    dst, scale = xT[:, k, 0, c * 512:(c + 1) * 512], XS
                nc.scalar.activation(dst, ps[:, g % 8, :], ACT.Copy, scale=scale).then_inc(s_trhi, 1)

            drains = [0]

            def drain(steps):
                for kind, i in steps:
                    n, bank = drains[0], drains[0] % 2
                    drains[0] += 1
                    if kind == "adj":
                        b, q = divmod(i, 4)
                        act.wait_ge(s_adj[b % 2], 16 * (b // 2 + 1))
                        cols = slice(q * 4 * P, (q + 1) * 4 * P)
                        nc.scalar.activation(sym8[:, b, cols], adj_in[:, b % 2, cols], ACT.Copy,
                                             accum_out=rowparts[:, b, q:q + 1]).then_inc(s_adjrow, 1)
                        act.wait_ge(s_fill, n + 1)
                        nc.scalar.activation(adjT8[:, 4 * q:4 * q + 4, b * P:(b + 1) * P],
                                             ps[:, bank, :].rearrange("p (u i) -> p u i", u=4),
                                             ACT.Copy).then_inc(s_drain, 1)
                        if q == 3 and b + 2 < NB:
                            act.wait_ge(s_adjrow, i + 1)
                            act.dma_start(adj_in[:, b % 2], adj_rows[b + 2]).then_inc(s_adj[b % 2], 16)
                    else:
                        b, w = divmod(i, 2)
                        tab_rows, stored = ((k_rows, s_kst), (q_rows, s_qst))[w]
                        if b:
                            act.wait_ge(stored, 16 * b)
                        act.wait_ge(s_fill, n + 1)
                        nc.scalar.activation(proj[:, w], ps[:, bank, :], ACT.Copy,
                                             scale=1.0 / (XS * WS)).then_inc(s_drain, 1)
                        act.wait_ge(s_drain, n + 1)
                        act.dma_start(tab_rows[b], proj[:, w]).then_inc(stored, 16)

            for n in range(2):
                for g in range(G4):
                    act.wait_ge(s_group, G4 * n + g + 1)
                    nc.scalar.activation(hotT[:, 4 * g:4 * g + 4], ps_hotT[:, 0:4, 0:EP], ACT.Copy).then_inc(s_hotT, 1)
                    drain(DURING_RANKS[n][g])
                drain(DURING_OFFSETS[n])
                drain(DURING_TABLE[n])
                for g in range(G8):
                    drain(DURING_PICKS[n][g])
                drain(DURING_PLACES[n])
                if n == 0:
                    drain(DURING_KEYS)
            with act.Fori(0, NB - 1, 2) as b0:
                for s in range(2):
                    act.wait_ge(s_xin[s], b0 * 8 + 16)
                    nc.scalar.activation(xhl[:, b0 + s, 0], x_in[:, s], ACT.Copy, scale=XS).then_inc(s_xhi, 1)
                    act.wait_ge(s_xhi, b0 + s + 1)
                    nc.scalar.activation(x_in[:, s], x_in[:, s], ACT.Copy, scale=XS).then_inc(s_x16, 1)
            act.wait_ge(s_args, 1)
            nc.scalar.activation(arg, arg, ACT.Exp).then_inc(s_exp, 1)
            for b in range(NB):
                act.wait_ge(s_symadd, b + 1)
                nc.scalar.activation(sym8[:, b], sym8[:, b], ACT.Copy, accum_out=vscale[:, b:b + 1]).then_inc(s_symsum, 1)
            act.wait_ge(s_deg, 1)
            nc.scalar.activation(dinv, dinv, ACT.Sqrt).then_inc(s_degroot, 1)

            def high(b, s, first):
                act.wait_ge(s_agg, b + 1)
                if not first:
                    act.wait_ge(s_mm1, b - 1)
                nc.scalar.activation(agghl[:, s, 0], agg[:, s], ACT.Copy).then_inc(s_agghi, 1)

            def deviation(variance, root, b, s):
                act.wait_ge(variance, b + 1)
                nc.scalar.activation(stat[:, s, 1:2], stat[:, s, 0:1], ACT.Sqrt).then_inc(root, 1)

            def keep_x1(b, s):
                deviation(s_var1, s_root1, b, s)
                act.wait_ge(s_x1, b + 1)
                act.dma_start(x1_rows[b], nrm[:, s]).then_inc(s_x1st[s], 16)
                nc.scalar.activation(vhl[:, b, 0], nrm[:, s], ACT.Copy,
                                     scale=vscale[:, bass.ds(b, 1)]).then_inc(s_vhi, 1)

            high(0, 0, True)
            high(1, 1, True)
            keep_x1(0, 0)
            with act.Fori(2, NB - 1, 2) as b0:
                high(b0, 0, False)
                keep_x1(b0 - 1, 1)
                high(b0 + 1, 1, False)
                keep_x1(b0, 0)
            keep_x1(NB - 1, 1)

            def stage(src, b, s, signal):
                nc.scalar.activation(stage16[:, s], src[:, :, bass.ds(b * P, P)], ACT.Copy).then_inc(signal, 1)

            def high_z(b, s):
                act.wait_ge(s_mm2, b + 1)
                nc.scalar.activation(xhl[:, b, 0], ps[:, 2 + s, :], ACT.Copy,
                                     scale=zscale[:, bass.ds(b, 1)]).then_inc(s_zhi, 1)

            act.wait_ge(s_symdiag, NB)
            act.wait_ge(s_mm1, NB)
            for s in range(2):
                stage(sym8, s, s, s_st2)
            with act.Fori(0, NB - 3, 2) as b0:
                for s in range(2):
                    high_z(b0 + s, s)
                    stage(sym8, b0 + s + 2, s, s_st2)
            for s in range(2):
                high_z(NB - 2 + s, s)
                stage(adjT8, s, s, s_st3)
            with act.Fori(0, NB - 3, 2) as b0:
                for s in range(2):
                    act.wait_ge(s_mm3, b0 + s + 1)
                    stage(adjT8, b0 + s + 2, s, s_st3)
                    deviation(s_var3, s_root3, b0 + s, s)
            for s in range(2):
                deviation(s_var3, s_root3, NB - 2 + s, s)

        @block.vector
        def _(dve):
            V = nc.vector
            chain = [0]

            def link(ins):
                chain[0] += 1
                ins.then_inc(s_dve, 1)
                dve.wait_ge(s_dve, chain[0])

            def wide(v, mid):
                return v.unsqueeze(1).to_broadcast([v.shape[0], mid, v.shape[1]])

            def deep(v, last):
                return v.unsqueeze(2).to_broadcast([v.shape[0], v.shape[1], last])

            intA, intB = raw.rearrange("p c f -> p (c f)")[:, 0:EC], raw.rearrange("p c f -> p (c f)")[:, EC:2 * EC]

            def one_hot_high():
                link(V.tensor_copy(key16, key))
                link(V.tensor_copy(intA, key))
                link(V.tensor_single_scalar(intB, intA, LOG_LO, ALU.logical_shift_right))
                link(V.tensor_tensor(hot, wide(iota[0:EP], EC), deep(intB, HI), ALU.is_equal))

            def one_hot_low():
                link(V.tensor_single_scalar(intA, intA, LO - 1, ALU.bitwise_and))
                V.tensor_tensor(hotlo, wide(iota[0:EP, 0:LO], EC), deep(intA, LO), ALU.is_equal).then_inc(s_hot, 1)

            dve.wait_ge(s_raw, 16)
            link(V.tensor_single_scalar(adj_idx, raw[:, :, 0], LOG_N, ALU.logical_shift_left))
            V.tensor_tensor(adj_idx, adj_idx, raw[:, :, 1], ALU.bitwise_or).then_inc(s_idx, 1)
            link(V.tensor_copy(payload[:, 0], raw[:, :, 0]))
            link(V.tensor_copy(payload[:, 1], raw[:, :, 1]))
            link(V.tensor_copy(key, payload[:, 1]))
            dve.wait_ge(s_const, 1)
            one_hot_high()
            dve.wait_ge(s_b, 32)
            link(V.tensor_copy(bias_hi, bias_in))
            link(V.tensor_copy(bias16[0:1], bias_hi[0:1]))
            link(V.tensor_tensor(bias_in, bias_in, bias_hi, ALU.subtract))
            link(V.tensor_copy(bias_mid, bias_in))
            link(V.tensor_copy(bias16[32:33], bias_mid[32:33]))
            V.tensor_tensor(bias16[64:65], bias_in[64:65], bias_mid[64:65], ALU.subtract).then_inc(s_bias, 1)
            for g in range(TRANSPOSES):
                dve.wait_ge(s_trhi, g + 1)
                if g < 2 * KB:
                    w, scale = wT[:, g // KB, g % KB], WS
                    lo, hi = w[:, 1], w[:, 0]
                else:
                    k, c = divmod(g - 2 * KB, 4)
                    lo, hi, scale = xT[:, k, 1, c * 512:(c + 1) * 512], xT[:, k, 0, c * 512:(c + 1) * 512], XS
                V.scalar_tensor_tensor(lo, ps[:, g % 8, :], scale, hi, ALU.mult, ALU.subtract).then_inc(s_trlo, 1)
            one_hot_low()

            def row_degrees():
                dve.wait_ge(s_adjrow, QUARTERS)
                dve.wait_ge(s_drain, ADJ_DRAINED)
                link(V.tensor_reduce(rowsum, rowparts, AX.X, ALU.add))
                for b in range(NB):
                    link(V.scalar_tensor_tensor(junk, adjT8[:, b, b * P:(b + 1) * P], 1.0, ident32, ALU.mult, ALU.mult,
                                                accum_out=adjii[:, b:b + 1]))
                V.tensor_tensor(degm, rowsum, adjii, ALU.subtract).then_inc(s_degm, 1)

            def by_width(place, part, col, parts):
                w, per = width[0:parts], perwidth[0:parts]
                link(V.tensor_scalar(col, w.to_broadcast([parts, col.shape[1]]), -0.5, 0.5, ALU.mult, ALU.add))
                link(V.tensor_tensor(part, place, col, ALU.add))
                link(V.tensor_scalar(part, part, per, None, ALU.mult))
                link(V.tensor_scalar(part, part, MAGIC, None, ALU.add))
                link(V.tensor_scalar(part, part, MAGIC, None, ALU.subtract))
                link(V.tensor_scalar(col, part, w, None, ALU.mult))
                link(V.tensor_tensor(col, place, col, ALU.subtract))

            def sort(n):
                fields = FIELDS[n]
                link(V.memset(restart, 1.0))
                link(V.memset(restart[:, :, 0:1], 0.0))
                for g in range(G4):
                    dve.wait_ge(s_group, G4 * n + g + 1)
                    for u in range(4):
                        keys = ps[0:EP, 3 + g % 2, u * P:u * P + EP]
                        r = V.scalar_tensor_tensor(keys, keys, key[:, bass.ds(4 * g + u, 1)], lower[:, 0:EP],
                                                   ALU.is_equal, ALU.mult,
                                                   accum_out=rank[:, bass.ds(4 * g + u, 1)])
                    r.then_inc(s_rank, 1)
                dve.wait_ge(s_rank, G4 * (n + 1))
                if n == 1:
                    row_degrees()
                link(V.tensor_copy(cnt, ps_cnt[:, 0:EC * LO].rearrange("p (c b) -> p b c", b=LO)))
                link(V.tensor_tensor_scan(incl.rearrange("p b c -> p (b c)"), restart.rearrange("p b c -> p (b c)"),
                                          cnt.rearrange("p b c -> p (b c)"), 0.0, ALU.mult, ALU.add))
                link(V.tensor_copy(tot, incl[:, :, LASTCOL]))
                link(V.tensor_tensor_scan(off, tot, zeros[:, 0:LO], 0.0, ALU.add, ALU.add))
                V.tensor_copy(rowtot, off[:, LO - 1:LO]).then_inc(s_rowtot, 1)
                link(V.tensor_tensor(incl, incl, cnt, ALU.subtract))
                dve.wait_ge(s_aoff, n + 1)
                link(V.tensor_copy(spread, ps[:, 3, 0:2]))
                link(V.scalar_tensor_tensor(off, off, aoff, tot, ALU.add, ALU.subtract))
                link(V.tensor_tensor(incl, incl, deep(off, EC), ALU.add))
                high, low = (tab[:, :, f].rearrange("p c b -> p b c") for f in (0, 1))
                link(V.tensor_scalar(cnt, incl, 1.0 / P, MAGIC, ALU.mult, ALU.add))
                link(V.tensor_scalar(high, cnt, MAGIC, None, ALU.subtract))
                if n == 1:
                    dve.wait_ge(s_degr, 16)
                    link(V.tensor_copy(tab[:, :, 2], wide(degr, EC)))
                V.scalar_tensor_tensor(low, high, -float(P), incl, ALU.mult, ALU.add).then_inc(s_tab, 1)
                for g in range(G8):
                    dve.wait_ge(s_pick, G8 * n + g + 1)
                    took = picked[:, g % 2, 0:8 * fields * LO].rearrange("p (c f b) -> p c f b", c=8, f=fields)
                    src = ps[0:EP, 3 + g % 2, 0:8 * fields * LO].rearrange("p (c f b) -> p c f b", c=8, f=fields)
                    low_hot = hotlo[:, bass.ds(8 * g, 8)].unsqueeze(2).to_broadcast([EP, 8, fields, LO])
                    V.tensor_tensor(took, src, low_hot, ALU.mult).then_inc(s_pickmul, 1)
                    dve.wait_ge(s_pickmul, G8 * n + g + 1)
                    V.tensor_reduce(posf[:, bass.ds(8 * g, 8), 0:fields], took, AX.X, ALU.add).then_inc(s_picked, 1)
                dve.wait_ge(s_picked, G8 * (n + 1))
                link(V.scalar_tensor_tensor(tcol, posf[:, :, 0], float(P), posf[:, :, 1], ALU.mult, ALU.add))
                link(V.tensor_tensor(rank, rank, tcol, ALU.add))
                if n == 0:
                    link(V.tensor_scalar(tcol, rank, -(EP - 1) / 2.0, 1.0 / EP, ALU.add, ALU.mult))
                    link(V.tensor_scalar(tcol, tcol, MAGIC, None, ALU.add))
                    link(V.tensor_scalar(tcol, tcol, MAGIC, None, ALU.subtract))
                    link(V.scalar_tensor_tensor(tpart, tcol, -float(EP), rank, ALU.mult, ALU.add))
                else:
                    link(V.tensor_scalar(width, placed, (EP - 1) / 2.0, 1.0 / EP, ALU.add, ALU.mult))
                    link(V.tensor_scalar(width, width, MAGIC, None, ALU.add))
                    link(V.tensor_scalar(width, width, MAGIC, 1.0, ALU.subtract, ALU.max))
                    link(V.tensor_copy(widthI, width))
                    link(V.reciprocal(perwidth, width))
                    by_width(rank, tpart, tcol, EP)
                    link(V.tensor_scalar(valid, payload[:, 0], 0.0, None, ALU.is_gt))
                    link(V.scalar_tensor_tensor(tcol, tcol, 1.0, valid, ALU.add, ALU.mult))
                    link(V.tensor_scalar(tcol, tcol, -1.0, None, ALU.add))
                if n == 0:
                    dve.wait_ge(s_valid, 16 * EC)
                    link(V.tensor_scalar(valid, valid, 1.0, 2.0, ALU.is_equal, ALU.mult))
                    link(V.tensor_scalar(valid, valid, -1.0, None, ALU.add))
                    link(V.scalar_tensor_tensor(payload[:, 0], payload[:, 0], 1.0, valid, ALU.add, ALU.mult))
                else:
                    link(V.tensor_copy(payload[:, 2], posf[:, :, 2]))
                first = payhot[:, :, 0]
                V.tensor_tensor(first, wide(iota[0:EP, 0:EC], EC), deep(tcol, EC), ALU.is_equal).then_inc(s_columns, 1)
                dve.wait_ge(s_columns, n + 1)
                V.tensor_tensor(tgt, wide(iota[0:EP, 0:EP], EC), deep(tpart, EP), ALU.is_equal).then_inc(s_tgt, 1)
                if n == 1:
                    link(V.tensor_tensor(deghot, first, deep(payload[:, 2], EC), ALU.mult))
                dve.wait_ge(s_objhot, n + 1)
                V.tensor_tensor(first, first, deep(payload[:, 0], EC), ALU.mult).then_inc(s_onehots, 1)
                dve.wait_ge(s_perm, n + 1)
                if n == 1:
                    link(V.tensor_copy(payload[:, 2], ps[0:EP, 6, 0:EC]))
                V.tensor_copy(payload[:, 0:2],
                              ps[0:EP, 5, 0:2 * EC].rearrange("p (f c) -> p f c", f=2)).then_inc(s_permcopied, 1)
                dve.wait_ge(s_permcopied, n + 1)

            sort(0)
            link(V.tensor_scalar(key, payload[:, 0], 0.0, -1.0, ALU.max, ALU.add))
            one_hot_high()
            one_hot_low()
            sort(1)

            link(V.tensor_scalar(tmpE, payload[:, 0], -1.0, None, ALU.add))
            link(V.tensor_scalar(subI, tmpE, 0.0, None, ALU.max))
            V.tensor_copy(objI, payload[:, 1]).then_inc(s_eidx, 1)
            link(V.tensor_tensor_scan(sub, tmpE, tmpE, -1.0, ALU.max, ALU.max))
            link(V.tensor_copy(obj, payload[:, 1]))
            link(V.tensor_copy(degE, payload[:, 2]))
            V.memset(att, 0.0).then_inc(s_attz, 1)
            link(V.memset(shift, 0.0))
            link(V.tensor_copy(shift[:, 1:EP], ident16[0:EP, 0:EP - 1]))
            link(V.tensor_scalar(before16[:, 0, 0:1], sub[:, LASTCOL:EC], 1.0, None, ALU.add))
            link(V.tensor_scalar(selF, payload[:, 0], 0.0, None, ALU.is_gt))
            link(V.tensor_copy(selL[:, LASTCOL:EC], selF[:, LASTCOL:EC]))
            link(V.tensor_tensor(selL[:, 0:LASTCOL], selF[:, 0:LASTCOL], selF[:, 1:EC], ALU.subtract))
            link(V.tensor_tensor(selL, selL, obj, ALU.mult))
            link(V.tensor_reduce(before[:, 0:1], selL, AX.X, ALU.add))
            V.tensor_copy(before16[:, 0, 1:2], before[:, 0:1]).then_inc(s_before16, 1)
            link(V.memset(flagF, 0.0))
            link(V.memset(flagB, 0.0))
            link(V.tensor_tensor(flagF[:, :, 1:EC], wide(sub[:, 1:EC], NV), wide(sub[:, 0:LASTCOL], NV), ALU.is_equal))
            link(V.tensor_copy(flagB[:, :, 0:LASTCOL], flagF[:, :, 1:EC]))
            link(V.tensor_scalar(selF, sub, sub[:, 0:1], None, ALU.is_equal))
            link(V.tensor_scalar(selL, sub, sub[:, LASTCOL:EC], None, ALU.is_equal))
            dve.wait_ge(s_before, 1)
            link(V.tensor_copy(before, ps[0:EP, 6, 0:2]))
            link(V.tensor_tensor(tmpE[:, 1:EC], obj[:, 1:EC], obj[:, 0:LASTCOL], ALU.is_equal))
            link(V.tensor_tensor(tmpE[:, 1:EC], tmpE[:, 1:EC], flagF[:, 0, 1:EC], ALU.mult))
            link(V.scalar_tensor_tensor(tmpE[:, 0:1], sub[:, 0:1], 1.0, before[:, 0:1], ALU.add, ALU.is_equal))
            link(V.scalar_tensor_tensor(tmpE[:, 0:1], obj[:, 0:1], before[:, 1:2], tmpE[:, 0:1], ALU.is_equal, ALU.mult))
            link(V.tensor_scalar(tmpE, tmpE, -1.0, 1.0, ALU.mult, ALU.add))
            link(V.tensor_tensor(weight, sub, obj, ALU.not_equal))
            link(V.tensor_tensor(weight, weight, tmpE, ALU.mult))
            link(V.scalar_tensor_tensor(weight, payload[:, 0], 0.0, weight, ALU.is_gt, ALU.mult))
            link(V.tensor_scalar(cidx, subI, LOG_P, LOG_N + LOG_P, ALU.logical_shift_right, ALU.logical_shift_left))
            link(V.tensor_scalar(tmpI, objI, P - 1, LOG_N, ALU.bitwise_and, ALU.logical_shift_left))
            link(V.tensor_tensor(cidx, cidx, tmpI, ALU.bitwise_or))
            link(V.tensor_scalar(tmpI, objI, LOG_P, LOG_P, ALU.logical_shift_right, ALU.logical_shift_left))
            link(V.tensor_tensor(cidx, cidx, tmpI, ALU.bitwise_or))
            link(V.tensor_single_scalar(tmpI, subI, P - 1, ALU.bitwise_and))
            link(V.tensor_tensor(cidx, cidx, tmpI, ALU.bitwise_or))
            link(V.tensor_scalar(tmpI, weight, 0.0, None, ALU.is_equal))
            link(V.tensor_single_scalar(tmpI, tmpI, 2 * LOG_N + 1, ALU.logical_shift_left))
            link(V.tensor_tensor(cidx, cidx, tmpI, ALU.bitwise_or))
            by_width(off, rowpart, rowcol, P)
            link(V.tensor_scalar(tot, tot, 0.0, float(2 * E), ALU.is_equal, ALU.mult))
            link(V.tensor_tensor(tot, tot, rowcol, ALU.add))
            link(V.scalar_tensor_tensor(rowI, rowpart, float(EC), tot, ALU.mult, ALU.add))
            e0 = 1.0 - DIAG
            link(V.tensor_scalar(tot, degr, e0, 1.0, ALU.mult, ALU.add))
            link(V.reciprocal(rowv[:, :, 1], tot))
            V.tensor_scalar(rowv[:, :, 0], rowv[:, :, 1], e0, None, ALU.mult).then_inc(s_default, 1)

            pair_sym, pair_T = (v.rearrange("p b j -> p (b j)").bitcast(u16) for v in (sym8, adjT8))
            V.tensor_tensor(pair_sym, pair_sym, pair_T, ALU.add).then_inc(s_symadd, NB)

            dve.wait_ge(s_attz, 1)
            columns = dve.value_load(widthI[0:1, 0:1], min_val=1, max_val=EC)
            for g in range(G8):
                with dve.If(columns > 8 * g):
                    for s in range(SLOTS + 1):
                        c = 8 * g + s
                        if s < SLOTS:
                            dve.wait_ge(s_rows[s], 32 * (g + 1))
                            if c >= 4:
                                dve.wait_ge(s_att, c - 3)
                            V.tensor_tensor(prod[:, s % 4], rows[:, s, 0], rows[:, s, 1], ALU.mult).then_inc(s_prod, 1)
                        if s:
                            dve.wait_ge(s_prod, c)
                            V.tensor_reduce(att[:, :, c - 1], prod[:, (s - 1) % 4].rearrange("p (h d) -> p h d", h=HEADS),
                                            AX.X, ALU.add).then_inc(s_att, 1)
                    dve.wait_ge(s_att, 8 * g + 8)

            def row_totals(n, heads, op):
                v, f, b, ff, fb = (a[:, 0:heads].rearrange("p h c -> p (h c)") for a in (val, scF, scB, flagF, flagB))
                link(V.tensor_tensor_scan(f, ff, v, 0.0, ALU.mult, op))
                link(V.tensor_tensor_scan(b[:, ::-1], fb[:, ::-1], v[:, ::-1], 0.0, ALU.mult, op))
                if op is ALU.max:
                    link(V.tensor_tensor(f, f, b, op))
                else:
                    link(V.tensor_tensor(f, f, b, op))
                    link(V.tensor_tensor(f, f, v, ALU.subtract))
                T = scF[:, 0:heads]
                link(V.memset(piece, 0.0))
                link(V.tensor_copy(piece[:, 0, 0:1], sub[:, 0:1]))
                link(V.tensor_copy(piece[:, 1, 0:1], sub[:, LASTCOL:EC]))
                link(V.tensor_copy(piece[:, 0, 1:1 + heads], T[:, :, 0]))
                link(V.tensor_scalar(tmpE[:, 0:1], sub[:, 0:1], sub[:, LASTCOL:EC], None, ALU.not_equal))
                V.tensor_scalar(piece[:, 1, 1:1 + heads], T[:, :, LASTCOL], tmpE[:, 0:1], None,
                                ALU.mult).then_inc(s_piece, 1)
                dve.wait_ge(s_rec[n], 16)
                for k, edge in ((0, sub[:, 0:1]), (1, sub[:, LASTCOL:EC])):
                    link(V.tensor_scalar(eqs[:, k], rec[:, :, 0], edge, None, ALU.is_equal))
                for k in range(2):
                    link(V.tensor_tensor(recprod[:, 0:heads], rec[:, :, 1:1 + heads].rearrange("p q h -> p h q"),
                                         wide(eqs[:, k], heads), ALU.mult))
                    link(V.tensor_reduce(totals[:, k, 0:heads], recprod[:, 0:heads], AX.X, op))
                for k, sel in ((0, selF), (1, selL)):
                    other = scB[:, 0:heads]
                    link(V.tensor_tensor(other, deep(totals[:, k, 0:heads], EC), T, ALU.subtract))
                    link(V.tensor_tensor(other, other, wide(sel, heads), ALU.mult))
                    link(V.tensor_tensor(T, T, other, ALU.add))

            link(V.tensor_scalar(att, att, DK ** -0.5, None, ALU.mult))
            link(V.scalar_tensor_tensor(val[:, 0:HEADS].rearrange("p h c -> p (h c)"),
                                        att.rearrange("p h c -> p (h c)"), 0.0,
                                        att.rearrange("p h c -> p (h c)"), ALU.max, ALU.max))
            link(V.tensor_tensor(val[:, 0:HEADS], val[:, 0:HEADS], wide(weight, HEADS), ALU.mult))
            row_totals(0, HEADS, ALU.max)
            top = scF[:, 0:HEADS]
            link(V.tensor_scalar(top, top, DIAG, None, ALU.max))
            link(V.tensor_tensor(arg[:, 0], att, top, ALU.subtract))
            link(V.tensor_scalar(arg[:, 0], arg[:, 0], 0.0, None, ALU.min))
            link(V.tensor_scalar(arg[:, 1], top, -1.0, None, ALU.mult))
            V.tensor_scalar(arg[:, 2], top, -1.0, DIAG, ALU.mult, ALU.add).then_inc(s_args, 1)
            dve.wait_ge(s_exp, 1)
            link(V.tensor_tensor(val[:, 0:HEADS], arg[:, 0], wide(weight, HEADS), ALU.mult))
            link(V.tensor_copy(val[:, HEADS], weight))
            row_totals(1, NV, ALU.add)
            den = scF[:, 0:HEADS]
            link(V.tensor_tensor(tmpE, degE, scF[:, HEADS], ALU.subtract))
            link(V.tensor_tensor(scB[:, 0:HEADS], arg[:, 1], wide(tmpE, HEADS), ALU.mult))
            link(V.tensor_tensor(den, den, scB[:, 0:HEADS], ALU.add))
            link(V.tensor_tensor(den, den, arg[:, 2], ALU.add))
            link(V.reciprocal(den, den))
            for k in range(3):
                link(V.tensor_tensor(arg[:, k], arg[:, k], den, ALU.mult))
                link(V.tensor_reduce(sums[:, k], arg[:, k].rearrange("p h c -> p c h"), AX.X, ALU.add))
            link(V.tensor_scalar(edge_rows[:, :, 0], sums[:, 1], 1.0 / HEADS, None, ALU.mult))
            V.tensor_scalar(edge_rows[:, :, 1], sums[:, 2], 1.0 / HEADS, None, ALU.mult).then_inc(s_edge, 1)
            link(V.tensor_tensor(corrE, sums[:, 0], sums[:, 1], ALU.subtract))
            V.tensor_scalar(corrE, corrE, AS / HEADS, None, ALU.mult).then_inc(s_corr, 1)
            dve.wait_ge(s_symsum, NB)
            V.tensor_scalar(dinv, vscale, 0.5, 1.0, ALU.mult, ALU.add).then_inc(s_deg, 1)
            for b in range(NB):
                blk = sym8[:, b, b * P:(b + 1) * P]
                V.scalar_tensor_tensor(blk, ident32, 2.0, blk, ALU.mult, ALU.add).then_inc(s_symdiag, 1)
            dve.wait_ge(s_degroot, 1)
            link(V.reciprocal(dinv, dinv))
            link(V.tensor_scalar(vscale, dinv, VS, None, ALU.mult))
            link(V.tensor_scalar(zscale, dinv, ZS / (2 * VS), None, ALU.mult))
            dve.wait_ge(s_rowg, 16 * LO)
            link(V.tensor_copy(off, rowv[:, :, 0]))
            V.tensor_copy(tot, rowv[:, :, 1]).then_inc(s_split, 1)
            dve.wait_ge(s_rowld, 48)
            link(V.tensor_tensor(baseC, baseC, adjii, ALU.mult))
            link(V.tensor_tensor(dcorr, dcorr, baseC, ALU.subtract))

            def scaled(b, s, first):
                if not first:
                    dve.wait_ge(s_agglo, b - 1)
                V.scalar_tensor_tensor(agg[:, s], adjT8[:, :, bass.ds(b * P, P)], AS,
                                       wide(baseB[:, bass.ds(b * P, P)], NB), ALU.mult, ALU.mult).then_inc(s_scaled, 1)

            def low(b, s):
                dve.wait_ge(s_agghi, b + 1)
                V.tensor_tensor(agghl[:, s, 1], agg[:, s], agghl[:, s, 0], ALU.subtract).then_inc(s_agglo, 1)

            def normalise(signal, variance, root, b, s, done):
                V.bn_stats(stat[:, s, 0:6], res).then_inc(signal, 1)
                dve.drain()
                V.bn_aggr(stat[:, s, 6:8], stat[:, s, 0:6]).then_inc(signal, 1)
                dve.wait_ge(signal, 3 * b + 2)
                V.tensor_scalar(stat[:, s, 0:1], stat[:, s, 7:8], EPS, None, ALU.add).then_inc(variance, 1)
                dve.wait_ge(root, b + 1)
                V.reciprocal(stat[:, s, 0:1], stat[:, s, 1:2]).then_inc(signal, 1)
                dve.wait_ge(signal, 3 * b + 3)
                V.tensor_scalar(nrm[:, s], res, stat[:, s, 6:7], stat[:, s, 0:1], ALU.subtract, ALU.mult).then_inc(done, 1)

            def post1(b, s, first):
                dve.wait_ge(s_xt[s], (b - s) * 8 + 16)
                if not (first and s == 0):
                    dve.wait_ge(s_x1, b)
                V.scalar_tensor_tensor(res, xt[:, s], dcorr[:, bass.ds(b, 1)], xt[:, s], ALU.mult,
                                       ALU.add).then_inc(s_dg, 1)
                dve.wait_ge(s_dg, b + 1)
                dve.wait_ge(s_mm1, b + 1)
                V.scalar_tensor_tensor(res, ps[:, s, :], 1.0 / (AS * XS), res, ALU.mult, ALU.add).then_inc(s_res1, 1)
                dve.wait_ge(s_res1, b + 1)
                if not first:
                    dve.wait_ge(s_x1st[s], (b - s) * 8)
                    dve.wait_ge(s_vlo, b - 1)
                normalise(s_ln1, s_var1, s_root1, b, s, s_x1)
                dve.wait_ge(s_vhi, b + 1)
                V.scalar_tensor_tensor(vhl[:, b, 1], nrm[:, s], vscale[:, bass.ds(b, 1)], vhl[:, b, 0], ALU.mult,
                                       ALU.subtract).then_inc(s_vlo, 1)

            dve.wait_ge(s_scattered, 1)
            scaled(0, 0, True)
            scaled(1, 1, True)
            low(0, 0)
            scaled(2, 0, False)
            low(1, 1)
            post1(0, 0, True)
            scaled(3, 1, False)
            low(2, 0)
            post1(1, 1, True)
            with dve.Fori(3, NB - 2, 2) as b:
                scaled(b + 1, 0, False)
                low(b, 1)
                post1(b - 1, 0, False)
                scaled(b + 2, 1, False)
                low(b + 1, 0)
                post1(b, 1, False)
            low(NB - 1, 1)
            post1(NB - 2, 0, False)
            post1(NB - 1, 1, False)

            with dve.Fori(0, NB - 1, 2) as b0:
                for s in range(2):
                    dve.wait_ge(s_zhi, b0 + s + 1)
                    V.scalar_tensor_tensor(xhl[:, b0 + s, 1], ps[:, 2 + s, :], zscale[:, bass.ds(b0 + s, 1)],
                                           xhl[:, b0 + s, 0], ALU.mult, ALU.subtract).then_inc(s_zlo, 1)

            def post3(b, s, first):
                dve.wait_ge(s_x1in[s], (b - s) * 8 + 16)
                if not (first and s == 0):
                    dve.wait_ge(s_y, b)
                dve.wait_ge(s_mm3, b + 1)
                V.scalar_tensor_tensor(res, ps[:, 2 + s, :], 1.0 / ZS, xt[:, s], ALU.mult, ALU.add).then_inc(s_res3, 1)
                dve.wait_ge(s_res3, b + 1)
                if not first:
                    dve.wait_ge(s_out[s], (b - s) * 8)
                normalise(s_ln3, s_var3, s_root3, b, s, s_y)

            post3(0, 0, True)
            post3(1, 1, True)
            with dve.Fori(2, NB - 1, 2) as b0:
                for s in range(2):
                    post3(b0 + s, s, False)


_INS = ['x', 'adj', 'L0_gnn_rel_pair_index', 'L0_gnn_Wq', 'L0_gnn_bq', 'L0_gnn_Wk', 'L0_gnn_bk']
_OUTS = [((2048, 512), 'float32')]


def kernel(**inputs):
    import numpy as _np
    import concourse.bacc as _bacc
    from concourse import mybir as _mybir
    from concourse.bass_utils import run_bass_kernel_spmd as _run

    nc = _bacc.Bacc("TRN2", target_bir_lowering=False, num_devices=1)
    arrays, args = {}, []
    for name in _INS:
        a = _np.ascontiguousarray(inputs[name])
        arrays[f"in_{name}_dram"] = a
        args.append(nc.dram_tensor(f"in_{name}_dram", a.shape, _mybir.dt.from_np(a.dtype), kind="ExternalInput").ap())
    for i, (shape, dtype) in enumerate(_OUTS):
        dt = _mybir.dt.from_np(_np.dtype(dtype))
        args.append(nc.dram_tensor(f"out_{i}_dram", shape, dt, kind="ExternalOutput").ap())
    gnn_resnorm_kernel(nc, *args)
    r = _run(nc, [arrays], core_ids=[0])
    return r.results[0]["out_0_dram"]
```

```python
import concourse.bass as bass
from concourse import mybir
from contextlib import ExitStack


def gnn_resnorm_kernel(nc: bass.Bass, x: bass.AP, adj: bass.AP, pairs: bass.AP, wq: bass.AP, bq: bass.AP,
                       wk: bass.AP, bk: bass.AP, out: bass.AP):
    f32, f16, i32 = mybir.dt.float32, mybir.dt.float16, mybir.dt.int32
    u8, u16 = mybir.dt.uint8, mybir.dt.uint16
    ALU, ACT, AX = mybir.AluOpType, mybir.ActivationFunctionType, mybir.AxisListType
    SIZE = {f32: 4, f16: 2, i32: 4, u8: 1}

    N, D = x.shape
    E = pairs.shape[0]
    P, HEADS, DK = 128, 8, 64
    NB, KB = N // P, D // P
    EC = 80
    EP = E // EC
    HI, LO = P, N // P
    G4, G8 = EC // 4, EC // 8
    NV = HEADS + 1
    SS = 2.0 ** 9
    MAGIC = 1.5 * 2.0 ** 23
    XS, WS, VS, ZS, AS = 2.0 ** 4, 2.0 ** 6, 2.0 ** 10, 2.0 ** 5, 2.0 ** 14
    EPS, DIAG = 1e-5, 1e-7
    COLUMN_GROUPS = [(0, 1), (1, 8)] + [(c, c + 8) for c in range(8, EC, 8)]
    FEW = 8
    K = 1024
    LOG_N, LOG_P, LOG_LO = 11, 7, 4
    assert EP * EC == E and EP <= P and HEADS * DK == D and HI * LO == N
    assert (1 << LOG_N, 1 << LOG_P, 1 << LOG_LO) == (N, P, LO)

    deg_tab = nc.dram_tensor("deg_tab", (N,), f32).ap()
    piece_tab = nc.dram_tensor("piece_tab", (2 * EP, 10), f32).ap()

    ctx = ExitStack()
    with ctx:
        ARENA = 212800
        arena = ctx.enter_context(nc.sbuf_tensor("arena", [P, ARENA], u8))
        ps = ctx.enter_context(nc.psum_tensor("ps", [P, 8, 512], f32))

        def place(first, shape, dt, end=None):
            n = SIZE[dt]
            for s in shape[1:]:
                n *= s
            assert first % 4 == 0 and first + n <= (end or ARENA), (first, n)
            v = arena[0:shape[0], first:first + n].bitcast(dt)
            names = "abcde"[:len(shape) - 1]
            if len(shape) > 2:
                v = v.rearrange(f"p ({' '.join(names)}) -> p {' '.join(names)}",
                                **{c: s for c, s in zip(names[1:], shape[2:])})
            return v

        def row_of(first, end):
            here = [first]

            def take(shape, dt=f32):
                v = place(here[0], shape, dt, end)
                n = SIZE[dt]
                for s in shape[1:]:
                    n *= s
                here[0] += (n + 3) // 4 * 4
                return v
            return take

        def packed(v, *dims):
            names = "abcdef"[:len(v.shape) - 1]
            n = 1
            for m in dims:
                n *= m
            flat = v.rearrange(f"p {' '.join(names)} -> p ({' '.join(names)})")[:, 0:n]
            names = "abcdef"[:len(dims)]
            return flat.rearrange(f"p ({' '.join(names)}) -> p {' '.join(names)}",
                                  **{a: m for a, m in zip(names[1:], dims[1:])})

        def sem(name):
            return ctx.enter_context(nc.semaphore(name))

        sym8 = place(0, [P, NB, N], u8)
        bias_in = place(32 * K, [P, 2, D], f32)
        bias_hi, bias_mid = place(36 * K, [P, 2, D], f16), place(38 * K, [P, 2, D], f16)
        adjT8 = place(32 * K, [P, NB, N], u8)
        xf = place(64 * K, [P, NB, D], f32)
        t_ = row_of(64 * K, 92 * K)
        cnt, incl = t_([P, LO, EC]), t_([P, LO, EC])
        tab = t_([P, EC, 3, LO], f16)
        picked = t_([EP, 2, 8 * 3 * LO])
        posf = t_([EP, EC, 3])
        restart = t_([P, LO, EC], f16)
        hotlo = t_([EP, EC, LO], f16)
        rank, junk = t_([EP, EC]), t_([P, P], f16)
        payhot = place(64 * K, [EP, EC, 2, EC], f16)
        acc = place(64 * K, [P, NB, D], f32)
        vhl = place(64 * K, [P, NB, 2, D], f16)
        e_ = row_of(80 * K, 112 * K)
        att = e_([EP, HEADS, EC])
        flagF, flagB = e_([EP, NV, EC], f16), e_([EP, NV, EC], f16)
        val, scF, scB = e_([EP, NV, EC]), e_([EP, NV, EC]), e_([EP, NV, EC])
        arg = e_([EP, 3, HEADS, EC])
        obj, weight = (e_([EP, EC]) for _ in range(2))
        selF, selL, tmpE = (e_([EP, EC]) for _ in range(3))
        subI = e_([EP, EC], i32)
        firstE = e_([EP, EC])
        row_parts, row_vals = e_([EP, EC, 5], f16), e_([EP, 2, EC])
        sums = e_([EP, 3, EC])
        x_first = e_([EP, D])
        piece, totals = e_([EP, 2, 10]), e_([EP, 2, NV])
        before16, before = e_([EP, 2, 4], f16), e_([EP, 2])
        x1 = place(96 * K, [P, NB, D], f32)
        wT = place(112 * K, [P, 2, KB, 2, D], f16)
        adj_in = place(96 * K, [P, 2, N], f32)
        deghot = place(92 * K, [EP, EC, EC], f16)
        xhl = place(128 * K, [P, NB, 2, D], f16)
        hot = place(160 * K, [EP, EC, HI], f16)
        tgt = place(160 * K, [EP, EC, EP], f16)
        rec = place(160 * K, [EP, 2 * EP, 10], f32)
        recprod = place(170 * K, [EP, NV, 2 * EP], f32)
        edge_x = place(160 * K, [EP, 2, 2, D], f32)
        edge_xT = place(168 * K, [P, 2, KB, 2, EP], f16)
        query = place(172 * K, [EP, D], f32)
        onehot = [place(b, [EP, NB, P], f16) for b in (160 * K, 166 * K)]
        y_ = [place(b, [EP, 2, D], f16) for b in (164 * K, 170 * K)]
        x_more = place(172 * K, [EP, D], f32)
        res = place(174 * K, [P, 2, D], f32)
        w_in = place(180 * K, [P, 2, KB, D], f32)
        hotT = place(180 * K, [P, EC, EP], f16)
        b_ = row_of(180 * K, 180 * K + 20000)
        prod = b_([EP, 2, D])
        b_([P, 2, NB, P], f16)
        stages = [place(b, [P, 2, NB, P], f16) for b in (184 * K, 166 * K)]
        staged16 = [stages[n // 2][:, n % 2] for n in range(4)]
        eqs = b_([EP, 2, 2 * EP])
        shift = b_([EP, EP + 1], f16)[:, 0:EP]
        same_row, sums16, ends = b_([EP, 2, 2, EP], f16), b_([EP, 2, 2, NV], f16), b_([EP, 2, NV])
        x_slots = [place(b, [P, 2, D], f32) for b in (180 * K, 192 * K)]
        xt = [x_slots[n // 2][:, n % 2] for n in range(4)]
        k_ = row_of(180 * K + 20000, ARENA)
        raw = k_([EP, EC, 2], i32)
        q32 = raw.rearrange("p c f -> p (c f)").bitcast(f32)
        tcol, tpart = q32[:, 0:EC], q32[:, EC:2 * EC]
        adj_idx, valid = k_([EP, EC], i32), k_([EP, EC])
        key, key16 = k_([EP, EC]), k_([EP, EC], f16)
        payload = k_([EP, 3, EC])
        corrE, sub, objI = valid, adj_idx.bitcast(f32), key.bitcast(i32)
        off, tot = k_([P, LO]), k_([P, LO])
        rowsum, adjii, degm, dinv, diag1, vscale, zscale, base = (k_([P, NB]) for _ in range(8))
        degr = k_([P, LO])
        row_got = k_([P, NB, 5])
        stat, mean_var = k_([P, 2, 8]), k_([P, 2, 2])
        neg_blocks, sub_in_block = k_([P, NB]), k_([EP, NB])
        rowtot, spread = k_([P, 1]), k_([P, 2])
        ones, width, perwidth, widthI = k_([P, 1]), k_([P, 1]), k_([P, 1]), k_([P, 1], i32)
        aoff, placed = spread[:, 0:1], spread[:, 1:2]
        ident32, upper = k_([P, P]), k_([P, P])
        ident16, iota = k_([P, P], f16), k_([P, P], f16)
        lower, const16 = k_([EP, EP + 1], f16), k_([P, P], f16)
        zeros = k_([P, LO])
        bias16 = k_([P, 2, D], f16)

        s_const = sem("constants")
        s_raw, s_w, s_b = sem("pairs_loaded"), sem("w_loaded"), sem("bias_loaded")
        s_x = [sem(f"x_loaded{n}") for n in range(4)]
        s_width, s_symadd, s_symsum, s_symdiag = sem("width"), sem("sym_added"), sem("sym_summed"), sem("sym_diagonal")
        s_attz = sem("attention_cleared")
        s_bias, s_idx, s_valid = sem("bias_split"), sem("adj_index"), sem("adj_picked")
        s_dve = sem("dve_chain")
        s_hot, s_group, s_hotT, s_rank = sem("hot_built"), sem("key_group"), sem("hotT_copied"), sem("ranked")
        s_rowtot, s_aoff = sem("row_totals"), sem("row_offsets")
        s_tab, s_pick, s_pickmul, s_picked = sem("table"), sem("pick_product"), sem("pick_mul"), sem("picked")
        s_columns, s_objhot, s_tgt = sem("column_one_hots"), sem("obj_one_hots"), sem("target_one_hots")
        s_degreehot = sem("degree_one_hots")
        s_onehots, s_perm, s_permcopied = sem("payload_one_hots"), sem("permuted"), sem("permuted_copied")
        s_tr, s_trhi, s_trlo = sem("transposed"), sem("transposed_hi"), sem("transposed_lo")
        s_adj = [sem(f"adj_loaded{n}") for n in range(2)]
        s_adjrow, s_fill, s_drain = sem("adj_rows_kept"), sem("adj_transposed"), sem("adjT_kept")
        s_degm, s_degst, s_degr = sem("degrees"), sem("degrees_stored"), sem("degrees_by_row")
        s_eidx, s_before16, s_before = sem("edge_indices"), sem("last_edges"), sem("edge_before")
        s_edgex = [sem(f"edge_x_gathered{n}") for n in range(2)]
        s_prod, s_att = sem("products"), sem("attention")
        s_edgeT, s_edgehi, s_edgelo = sem("edge_x_transposed"), sem("edge_x_hi"), sem("edge_x_lo")
        s_projected, s_query = sem("queries_and_keys"), sem("query_copied")
        s_xhi, s_xlo = sem("x_hi"), sem("x_lo")
        s_piece, s_pst = sem("pieces"), sem("pieces_stored")
        s_ends, s_sumparts, s_totals = sem("end_rows"), sem("end_sums"), sem("end_totals")
        s_rec = sem("pieces_spread")
        s_args, s_exp = sem("exponents"), sem("exponentials")
        s_st0, s_st1, s_mm1, s_acc = sem("adj_staged_by_scalar"), sem("adj_staged_by_pool"), sem("adj_x_product"), sem("adj_x_kept")
        s_xfirst, s_xmore = sem("x_rows_first_column"), sem("x_rows_more_columns")
        s_rel, s_onehot, s_parts = sem("sub_in_block"), sem("row_one_hot"), sem("row_parts")
        s_rowmm, s_rowadd = sem("row_values"), sem("row_values_added")
        s_base, s_x1init, s_more = sem("row_factors"), sem("x_in_x1"), sem("more_columns_added")
        s_morerel, s_moreoh, s_morehi, s_morey = (sem("more_sub_in_block"), sem("more_one_hot"), sem("more_rows_hi"),
                                                  sem("more_rows"))
        s_moremm, s_moreadd = sem("more_product"), sem("more_added")
        s_y0hi, s_y0, s_mmc = sem("corrected_rows_hi"), sem("corrected_rows"), sem("correction_product")
        s_xt = [sem(f"x_tile{n}") for n in range(4)]
        s_accx, s_res1, s_ln1 = sem("acc_with_x"), sem("residual1"), sem("ln1_chain")
        s_x1, s_vhi, s_vlo = sem("x1"), sem("v_hi"), sem("v_lo")
        s_st2, s_mm2, s_zhi, s_zlo = sem("sym_staged"), sem("sym_product"), sem("z_hi"), sem("z_lo")
        s_st3, s_mm3, s_ln3, s_y = sem("adj_staged"), sem("adj_product"), sem("ln3_chain"), sem("y")
        s_inv1, s_inv3 = sem("inverse_deviation1"), sem("inverse_deviation3")
        s_out = [sem(f"out_stored{n}") for n in range(2)]
        s_pool, s_res3 = sem("pool_chain"), sem("residual3")
        s_deg, s_degroot, s_vscale = sem("symmetric_degrees"), sem("degree_roots"), sem("v_scale")
        s_var1, s_root1, s_var3, s_root3 = sem("variance1"), sem("deviation1"), sem("variance3"), sem("deviation3")

        FIELDS = (2, 3)

        ps_hotT = [ps[:, n, :].bitcast(f16).rearrange("p (u e) -> p u e", u=8) for n in (1, 2)]
        ps_cnt = ps[:, 5:8, :].rearrange("p b c -> p (b c)")
        TRANSPOSES = 2 * KB
        CHUNKS = 4

        def chunks(W):
            size = EC // CHUNKS
            return [(k, first, min(first + size, W)) for k, first in enumerate(range(0, W, size))]

        QUARTERS = 4 * NB
        EXP_AT, TOTALS_AT, FACTORS_AT, FINISH_FROM = 3, 4, 5, 7
        SUMS_AT = {0: (0, 3), 1: (3, 6), 2: (6, 9), 3: (9, 11), 4: (11, 14), 5: (14, NB)}
        X1_AT = {FACTORS_AT: (0, 6), FACTORS_AT + 1: (6, NB)}
        KEY_BANKS = (3, 4, 0)
        CORR_BANKS, SYM_BANKS, ADJ_BANKS = (0, 1, 4, 5), (6, 7, 2, 3), (0, 1, 4, 5)
        FINISH_AT = {n: [] for n in range(NB)}
        for b in range(NB):
            FINISH_AT[max(FINISH_FROM + b // 2, b)].append(b)
        x_rows = x.rearrange("(b p) d -> p b d", p=P)
        adj_rows = adj.rearrange("(b p) j -> b p j", p=P)
        xb_rows = x.rearrange("(b p) d -> b p d", p=P)
        out_rows = out.rearrange("(b p) d -> b p d", p=P)

        block = ctx.enter_context(nc.Block())

        @block.sync
        def _(sp):
            def load_adj(b):
                sp.dma_start(adj_in[:, b % 2], adj_rows[b]).then_inc(s_adj[b % 2], 16)

            sp.dma_start(raw, pairs.rearrange("(p c) f -> p c f", p=EP)).then_inc(s_raw, 16)
            sp.dma_start(bias_in[:, 0], bk.partition_broadcast(P)).then_inc(s_b, 16)
            sp.dma_start(bias_in[:, 1], bq.partition_broadcast(P)).then_inc(s_b, 16)
            sp.dma_start(w_in[:, 0], wk.rearrange("(b p) d -> p b d", p=P)).then_inc(s_w, 16)
            sp.dma_start(w_in[:, 1], wq.rearrange("(b p) d -> p b d", p=P)).then_inc(s_w, 16)
            load_adj(0)
            load_adj(1)
            for b in range(0, NB, 4):
                sp.dma_start(xf[:, b:b + 4], x_rows[:, b:b + 4]).then_inc(s_x[b // 4], 16)
            for b in range(2, NB):
                sp.wait_ge(s_fill, 4 * (b - 1))
                sp.wait_ge(s_adjrow, b - 1)
                load_adj(b)
            sp.wait_ge(s_degm, 1)
            with nc.allow_non_contiguous_dma("2048 single values"):
                sp.dma_start(deg_tab.rearrange("(b p) -> p b", p=P), degm).then_inc(s_degst, 16)
            sp.wait_ge(s_degst, 16)
            sp.dma_start(degr, deg_tab.rearrange("(a b) -> a b", b=LO)).then_inc(s_degr, 16)
            sp.wait_ge(s_piece, 1)
            sp.dma_start(piece_tab.rearrange("(p k) v -> p k v", k=2), piece).then_inc(s_pst, 16)
            sp.wait_ge(s_pst, 16)
            sp.dma_start(rec.rearrange("p q v -> p (q v)"),
                         piece_tab.rearrange("q v -> (q v)").partition_broadcast(EP)).then_inc(s_rec, 16)
            for b in range(NB):
                if b == 2:
                    sp.wait_ge(s_parts, 1)
                if b >= 4:
                    sp.wait_ge(s_x1init, b - 3)
                sp.dma_start(xt[b % 4], xb_rows[b]).then_inc(s_xt[b % 4], 16)
            for n in range(2):
                sp.wait_ge(s_out[n], 16 * (NB // 2))

        @block.gpsimd
        def _(pool):
            chain = [0]

            def link(ins):
                chain[0] += 1
                ins.then_inc(s_pool, 1)
                pool.wait_ge(s_pool, chain[0])

            link(nc.gpsimd.memset(zeros, 0.0))
            link(nc.gpsimd.iota(neg_blocks, pattern=[[-P, NB]], base=0, channel_multiplier=0,
                                allow_small_or_imprecise_dtypes=True))
            link(nc.gpsimd.memset(ident32, 0.0))
            link(nc.gpsimd.affine_select(out=ident32, in_=ident32, compare_op=ALU.not_equal, fill=1.0, base=0,
                                         pattern=[[-1, P]], channel_multiplier=1))
            link(nc.gpsimd.tensor_copy(ident16, ident32))
            link(nc.gpsimd.iota(iota, pattern=[[1, P]], base=0, channel_multiplier=0,
                                allow_small_or_imprecise_dtypes=True))
            link(nc.gpsimd.memset(lower, 1.0))
            link(nc.gpsimd.affine_select(out=lower, in_=lower, compare_op=ALU.is_gt, fill=0.0, base=0,
                                         pattern=[[-1, EP + 1]], channel_multiplier=1))
            link(nc.gpsimd.memset(upper, 1.0))
            link(nc.gpsimd.affine_select(out=upper, in_=upper, compare_op=ALU.is_gt, fill=0.0, base=0,
                                         pattern=[[1, P]], channel_multiplier=-1))
            link(nc.gpsimd.memset(const16, XS * WS))
            link(nc.gpsimd.memset(ones, 1.0))
            nc.gpsimd.memset(bias16, 0.0).then_inc(s_const, 1)
            pool.wait_ge(s_idx, 1)
            adj_flat = adj.rearrange("i (j o) -> (i j) o", o=1)
            for c in range(EC):
                pool.indirect_dma_start(valid[:, c:c + 1], None, adj_flat,
                                        bass.IndirectOffsetOnAxis(ap=adj_idx[:, c:c + 1], axis=0)).then_inc(s_valid, 16)
            def times_obj(n, W):
                hots = packed(payhot, W, 2, W)
                for k, a, z in chunks(W):
                    pool.wait_ge(s_columns, CHUNKS * n + k + 1)
                    nc.gpsimd.tensor_tensor(hots[:, a:z, 1], hots[:, a:z, 0],
                                            payload[:, 1, a:z].unsqueeze(2).to_broadcast([EP, z - a, W]),
                                            ALU.mult).then_inc(s_objhot, 1)

            times_obj(0, EC)
            pool.wait_ge(s_width, 1)
            filled = pool.value_load(widthI[0:1, 0:1], min_val=1, max_val=EC)
            with pool.If(filled > FEW):
                times_obj(1, EC)
            with pool.Else():
                times_obj(1, FEW)
            pool.wait_ge(s_eidx, 1)

            def gather(first, end):
                for c in range(first, end):
                    if c >= 2:
                        pool.wait_ge(s_edgeT, 2 * c - 2)
                    for w, at in ((0, objI), (1, subI)):
                        pool.indirect_dma_start(edge_x[:, c % 2, w], None, x,
                                                bass.IndirectOffsetOnAxis(ap=at[:, c:c + 1], axis=0)).then_inc(s_edgex[c % 2], 16)

            gather(*COLUMN_GROUPS[0])
            pool.indirect_dma_start(x_first, None, x,
                                    bass.IndirectOffsetOnAxis(ap=objI[:, 0:1], axis=0)).then_inc(s_xfirst, 16)
            for first, end in COLUMN_GROUPS[1:]:
                with pool.If(filled > first):
                    gather(first, end)

            def stage(b, s):
                nc.gpsimd.tensor_copy(staged16[s], adjT8[:, :, bass.ds(b * P, P)]).then_inc(s_st1, 1)

            def stage_even(first, end):
                with pool.Fori(first, end - 1, 2) as b0:
                    pool.wait_ge(s_mm1, b0 - 1)
                    stage(b0, 0)

            stage(1, 1)
            stage_even(2, FINISH_FROM + 3)
            pool.wait_ge(s_base, 1)
            for first, end in COLUMN_GROUPS[1:]:
                with pool.If(filled > first):
                    for c in range(first, end):
                        if c > 1:
                            pool.wait_ge(s_morey, c - 1)
                        pool.indirect_dma_start(x_more, None, x,
                                                bass.IndirectOffsetOnAxis(ap=objI[:, c:c + 1], axis=0)).then_inc(s_xmore, 16)
            stage_even(FINISH_FROM + 3, NB)
            with pool.Fori(0, NB - 1, 2) as b0:
                for s in range(2):
                    pool.wait_ge(s_y, b0 + s + 1)
                    pool.dma_start(out_rows[b0 + s], xt[s]).then_inc(s_out[s], 16)

        @block.tensor
        def _(pe):
            def sort_groups(n, W):
                if n:
                    pe.wait_ge(s_permcopied, n)
                    pe.wait_ge(s_hotT, G4 * n)
                for g in range(W // 4):
                    for k, a, _z in chunks(W):
                        if a == 4 * g:
                            pe.wait_ge(s_hot, CHUNKS * n + k + 1)
                    if g >= 2:
                        pe.wait_ge(s_hotT, G4 * n + g - 1)
                    if g >= 3:
                        pe.wait_ge(s_rank, G4 * n + g - 2)
                    for u in range(4):
                        c = 4 * g + u
                        nc.tensor.transpose(ps_hotT[g % 2][:, u, 0:EP], hot[:, c], ident16[0:EP, 0:EP])
                        nc.tensor.matmul(ps_cnt[:, c * LO:(c + 1) * LO], hot[:, c], hotlo[:, c], start=True, stop=True)
                        r = nc.tensor.matmul(ps[0:EP, KEY_BANKS[g % 3], u * P:u * P + EP],
                                             key16[:, c:c + 1].to_broadcast([EP, EP]), ident16[0:EP, 0:EP],
                                             start=True, stop=True)
                    r.then_inc(s_group, 1)

            def sort_offsets(n):
                pe.wait_ge(s_rowtot, n + 1)
                nc.tensor.matmul(ps[:, 3, 0:1], upper, rowtot, start=True, stop=True)
                nc.tensor.matmul(ps[:, 3, 1:2], rowtot.to_broadcast([P, P]), ones, start=True, stop=True).then_inc(s_aoff, 1)

            def sort_pick(n, W, fields):
                pe.wait_ge(s_tab, n + 1)
                pe.wait_ge(s_hotT, G4 * n + W // 4)
                for g in range(W // 8):
                    if g >= 2:
                        pe.wait_ge(s_pickmul, G8 * n + g - 1)
                    for u in range(8):
                        c = 8 * g + u
                        r = nc.tensor.matmul(ps[0:EP, 3 + g % 2, u * fields * LO:(u + 1) * fields * LO], hotT[:, c],
                                             tab[:, c, 0:fields].rearrange("p f b -> p (f b)"), start=True, stop=True)
                    r.then_inc(s_pick, 1)

            def sort_permute(n, W, fields):
                hots, degree = packed(payhot, W, 2, W), packed(deghot, W, W)
                for c in range(W):
                    for k, a, _z in chunks(W):
                        if a == c:
                            pe.wait_ge(s_tgt, CHUNKS * n + k + 1)
                            pe.wait_ge(s_onehots, CHUNKS * n + k + 1)
                    r = nc.tensor.matmul(ps[0:EP, 5, 0:2 * W], tgt[:, c], hots[:, c].rearrange("p f c -> p (f c)"),
                                         start=c == 0, stop=c == W - 1)
                    if fields == 3:
                        r = nc.tensor.matmul(ps[0:EP, 6, 0:W], tgt[:, c], degree[:, c],
                                             start=c == 0, stop=c == W - 1)
                r.then_inc(s_perm, 1)

            def sort(n, W):
                sort_groups(n, W)
                sort_offsets(n)
                sort_pick(n, W, FIELDS[n])
                sort_permute(n, W, FIELDS[n])

            pe.wait_ge(s_const, 1)
            pe.wait_ge(s_w, 32)
            for g in range(TRANSPOSES):
                for u in range(4):
                    r = nc.tensor.transpose(ps[:, g % 8, u * P:(u + 1) * P],
                                            w_in[:, g // KB, u, (g % KB) * P:(g % KB + 1) * P], ident32)
                r.then_inc(s_tr, 1)
            pe.wait_ge(s_bias, 1)
            pe.wait_ge(s_trhi, TRANSPOSES)
            pe.wait_ge(s_trlo, TRANSPOSES)
            for i in range(QUARTERS):
                b, q = divmod(i, 4)
                if q == 0:
                    pe.wait_ge(s_adj[b % 2], 16 * (b // 2 + 1))
                if i >= 4:
                    pe.wait_ge(s_drain, i - 3)
                for u in range(4):
                    j = 4 * q + u
                    r = nc.tensor.transpose(ps[:, q, u * P:(u + 1) * P], adj_in[:, b % 2, j * P:(j + 1) * P], ident32)
                r.then_inc(s_fill, 1)
            pe.wait_ge(s_drain, QUARTERS)
            sort(0, EC)
            pe.wait_ge(s_width, 1)
            columns = pe.value_load(widthI[0:1, 0:1], min_val=1, max_val=EC)
            with pe.If(columns > FEW):
                sort(1, EC)
            with pe.Else():
                sort(1, FEW)
            pe.wait_ge(s_xhi, NB)
            pe.wait_ge(s_xlo, NB)

            def edge_before():
                pe.wait_ge(s_before16, 1)
                nc.tensor.matmul(ps[0:EP, 6, 0:2], shift, before16[:, 0, 0:2], start=True, stop=True).then_inc(s_before, 1)
                for k in range(2):
                    r = nc.tensor.matmul(ps[0:EP, 7, k * EP:(k + 1) * EP], before16[:, 1, k:k + 1].to_broadcast([EP, EP]),
                                         ident16[0:EP, 0:EP], start=True, stop=True)
                r.then_inc(s_ends, 1)

            def end_totals():
                pe.wait_ge(s_sumparts, 1)
                for k in range(2):
                    for end in range(2):
                        for i in range(2):
                            r = nc.tensor.matmul(ps[0:EP, 7, k * NV:(k + 1) * NV], same_row[:, end, k], sums16[:, i, end],
                                                 start=(end == 0 and i == 0), stop=(end == 1 and i == 1))
                r.then_inc(s_totals, 1)

            def project(first, end):
                for c in range(first, end):
                    pe.wait_ge(s_edgex[c % 2], 32 * (c // 2 + 1))
                    for w in range(2):
                        if c:
                            pe.wait_ge(s_edgelo, 2 * c - 1 + w)
                        for k in range(KB):
                            r = nc.tensor.transpose(ps[:, w, k * EP:(k + 1) * EP],
                                                    edge_x[:, c % 2, w, k * P:(k + 1) * P], ident32[0:EP, 0:EP])
                        r.then_inc(s_edgeT, 1)
                    if c:
                        pe.wait_ge(s_prod, c)
                    for w in range(2):
                        pe.wait_ge(s_edgelo, 2 * c + 1 + w)
                        for k in range(KB):
                            for x_part, w_part in ((0, 0), (0, 1), (1, 0)):
                                nc.tensor.matmul(ps[0:EP, 4 + w, :], edge_xT[:, w, k, x_part], wT[:, w, k, w_part],
                                                 start=(k == x_part == w_part == 0), stop=False)
                        nc.tensor.matmul(ps[0:EP, 4 + w, :], const16[:, 0:EP], bias16[:, w],
                                         start=False, stop=True).then_inc(s_projected, 1)

            def row_values(c):
                pe.wait_ge(s_onehot, c + 1)
                if c > 1:
                    pe.wait_ge(s_rowadd, c - 1)
                for b in range(NB):
                    r = nc.tensor.matmul(ps[:, 4 + c % 2, 5 * b:5 * b + 5], onehot[c > 0][:, b], row_parts[:, c],
                                         start=True, stop=True)
                r.then_inc(s_rowmm, 1)

            def more_corrections(c):
                pe.wait_ge(s_moreoh, c)
                pe.wait_ge(s_morey, c)
                for b in range(NB):
                    n = NB * (c - 1) + b
                    if n >= 2:
                        pe.wait_ge(s_moreadd, n - 1)
                    for j in range(2):
                        r = nc.tensor.matmul(ps[:, n % 2, :], onehot[1][:, b], y_[1][:, j], start=j == 0, stop=j == 1)
                    r.then_inc(s_moremm, 1)

            for n in range(NB):
                if n == 0 or (n > 1 and n % 2):
                    pe.wait_ge(s_st0, 1 + n // 2)
                else:
                    pe.wait_ge(s_st1, 1 + n // 2)
                if n >= 2:
                    pe.wait_ge(s_acc, n - 1)
                for k in range(NB):
                    if n == 0 and k == NB // 2:
                        edge_before()
                        project(*COLUMN_GROUPS[0])
                    for j in range(2):
                        r = nc.tensor.matmul(ps[:, 2 + n % 2, :], staged16[n % 2][:, k], xhl[:, k, j],
                                             start=(k == 0 and j == 0), stop=(k == NB - 1 and j == 1))
                r.then_inc(s_mm1, 1)
                if n == 0:
                    for first, end in COLUMN_GROUPS[1:]:
                        with pe.If(columns > first):
                            project(first, end)
                if n == TOTALS_AT:
                    end_totals()
                if n == FACTORS_AT:
                    pe.wait_ge(s_parts, 1)
                    row_values(0)
                    for first, end in COLUMN_GROUPS[1:]:
                        with pe.If(columns > first):
                            for c in range(first, end):
                                row_values(c)
                if n == FINISH_FROM - 1:
                    for first, end in COLUMN_GROUPS[1:]:
                        with pe.If(columns > first):
                            for c in range(first, end):
                                more_corrections(c)
                if n == FINISH_FROM:
                    pe.wait_ge(s_more, 1)
                    pe.wait_ge(s_y0, 1)
                for b in FINISH_AT[n]:
                    if b >= 4:
                        pe.wait_ge(s_res1, b - 3)
                    for j in range(2):
                        r = nc.tensor.matmul(ps[:, CORR_BANKS[b % 4], :], onehot[0][:, b], y_[0][:, j], start=j == 0, stop=j == 1)
                    r.then_inc(s_mmc, 1)

            EARLY = NB - 4

            def part(b, rhs, bank, k_first, k_end):
                for k in range(k_first, k_end):
                    for j in range(2):
                        r = nc.tensor.matmul(ps[:, bank, :], staged16[(b + 2) % 4][:, k], rhs[:, k, j],
                                             start=(k == 0 and j == 0), stop=(k == NB - 1 and j == 1))
                return r

            pe.wait_ge(s_acc, NB)
            pe.wait_ge(s_vlo, EARLY)
            for b in range(4):
                pe.wait_ge(s_st2, b + 1)
                part(b, vhl, SYM_BANKS[b], 0, EARLY)
            pe.wait_ge(s_vlo, NB)
            for b in range(4):
                part(b, vhl, SYM_BANKS[b], EARLY, NB).then_inc(s_mm2, 1)
            with pe.Fori(4, NB - 3, 4) as b0:
                for s in range(4):
                    pe.wait_ge(s_st2, b0 + s + 1)
                    pe.wait_ge(s_zlo, b0 + s - 3)
                    part(s, vhl, SYM_BANKS[s], 0, NB).then_inc(s_mm2, 1)
            pe.wait_ge(s_zlo, NB - 2)
            pe.wait_ge(s_st3, 1)
            part(0, xhl, ADJ_BANKS[0], 0, NB - 2)
            pe.wait_ge(s_zlo, NB)
            part(0, xhl, ADJ_BANKS[0], NB - 2, NB).then_inc(s_mm3, 1)
            for s in range(1, 4):
                pe.wait_ge(s_st3, s + 1)
                part(s, xhl, ADJ_BANKS[s], 0, NB).then_inc(s_mm3, 1)
            with pe.Fori(4, NB - 3, 4) as b0:
                for s in range(4):
                    pe.wait_ge(s_st3, b0 + s + 1)
                    pe.wait_ge(s_res3, b0 + s - 3)
                    part(s, xhl, ADJ_BANKS[s], 0, NB).then_inc(s_mm3, 1)

        @block.scalar
        def _(act):
            def drain_adj(b):
                for q in range(4):
                    act.wait_ge(s_fill, 4 * b + q + 1)
                    nc.scalar.activation(adjT8[:, 4 * q:4 * q + 4, b * P:(b + 1) * P],
                                         ps[:, q, :].rearrange("p (u i) -> p u i", u=4), ACT.Copy).then_inc(s_drain, 1)

            act.wait_ge(s_const, 1)
            for g in range(TRANSPOSES):
                act.wait_ge(s_tr, g + 1)
                nc.scalar.activation(wT[:, g // KB, g % KB, 0], ps[:, g % 8, :], ACT.Copy, scale=WS).then_inc(s_trhi, 1)
            for b in range(NB):
                if b % 4 == 0:
                    act.wait_ge(s_x[b // 4], 16)
                nc.scalar.activation(xhl[:, b, 0], xf[:, b], ACT.Copy, scale=XS).then_inc(s_xhi, 1)
                if b % 2:
                    drain_adj(b // 2)
            for b in range(NB // 2, NB):
                drain_adj(b)

            def copy_hotT(n, W):
                for g in range(W // 4):
                    act.wait_ge(s_group, G4 * n + g + 1)
                    nc.scalar.activation(hotT[:, 4 * g:4 * g + 4], ps_hotT[g % 2][:, 0:4, 0:EP], ACT.Copy).then_inc(s_hotT, 1)

            def sum_rows(first, end):
                for m in range(first, end):
                    nc.scalar.activation(sym8[:, m], sym8[:, m], ACT.Copy, accum_out=vscale[:, m:m + 1]).then_inc(s_symsum, 1)

            copy_hotT(0, EC)
            act.wait_ge(s_width, 1)
            columns = act.value_load(widthI[0:1, 0:1], min_val=1, max_val=EC)
            with act.If(columns > FEW):
                copy_hotT(1, EC)
            with act.Else():
                copy_hotT(1, FEW)
            act.wait_ge(s_perm, 2)
            nc.scalar.activation(staged16[0], adjT8[:, :, 0:P], ACT.Copy).then_inc(s_st0, 1)

            def split_edges(first, end):
                for c in range(first, end):
                    for w in range(2):
                        if c:
                            act.wait_ge(s_projected, 2 * c - 1 + w)
                        act.wait_ge(s_edgeT, 2 * c + 1 + w)
                        nc.scalar.activation(edge_xT[:, w, :, 0], ps[:, w, 0:KB * EP].rearrange("p (k e) -> p k e", k=KB),
                                             ACT.Copy, scale=XS).then_inc(s_edgehi, 1)
                    if c:
                        act.wait_ge(s_prod, c)
                    act.wait_ge(s_projected, 2 * c + 2)
                    nc.scalar.activation(query, ps[0:EP, 5, :], ACT.Copy).then_inc(s_query, 1)

            split_edges(*COLUMN_GROUPS[0])
            for first, end in COLUMN_GROUPS[1:]:
                with act.If(columns > first):
                    split_edges(first, end)

            def keep(b):
                act.wait_ge(s_mm1, b + 1)
                nc.scalar.activation(acc[:, b], ps[:, 2 + b % 2, :], ACT.Copy, scale=1.0 / XS).then_inc(s_acc, 1)

            def start_x1(first, end):
                for b in range(first, end):
                    act.wait_ge(s_xt[b % 4], 16 * (b // 4 + 1))
                    nc.scalar.activation(x1[:, b], xt[b % 4], ACT.Copy, scale=diag1[:, b:b + 1]).then_inc(s_x1init, 1)

            def stage(src, b, s, signal):
                nc.scalar.activation(staged16[(s + 2) % 4], src[:, :, bass.ds(b * P, P)], ACT.Copy).then_inc(signal, 1)

            def deviation(variance, root, b, s):
                act.wait_ge(variance, b + 1)
                nc.scalar.activation(stat[:, s, 1:2], stat[:, s, 0:1], ACT.Sqrt).then_inc(root, 1)

            def high_v(b):
                act.wait_ge(s_x1, b + 1)
                nc.scalar.activation(vhl[:, b, 0], x1[:, b], ACT.Copy, scale=vscale[:, b:b + 1]).then_inc(s_vhi, 1)

            for n in range(NB):
                keep(n)
                if n % 2 and n + 2 < NB:
                    nc.scalar.activation(staged16[1], adjT8[:, :, (n + 2) * P:(n + 3) * P], ACT.Copy).then_inc(s_st0, 1)
                if n in SUMS_AT:
                    act.wait_ge(s_symadd, 1)
                    sum_rows(*SUMS_AT[n])
                if n == EXP_AT:
                    act.wait_ge(s_args, 1)
                    with act.If(columns > FEW):
                        nc.scalar.activation(arg, arg, ACT.Exp).then_inc(s_exp, 1)
                    with act.Else():
                        few = arg.rearrange("p k h c -> p (k h c)")[:, 0:3 * HEADS * FEW]
                        nc.scalar.activation(few, few, ACT.Exp).then_inc(s_exp, 1)
                if n in X1_AT:
                    act.wait_ge(s_base, 1)
                    start_x1(*X1_AT[n])
                if n == FACTORS_AT:
                    act.wait_ge(s_deg, 1)
                    nc.scalar.activation(dinv, dinv, ACT.Sqrt).then_inc(s_degroot, 1)
                if n == FINISH_FROM:
                    act.wait_ge(s_vscale, 1)
                if n == NB - 2:
                    act.wait_ge(s_symdiag, NB)
                    act.wait_ge(s_more, 1)
                    stage(sym8, 0, 0, s_st2)
                    stage(sym8, 1, 1, s_st2)
                if n == NB - 1:
                    stage(sym8, 2, 2, s_st2)
                    stage(sym8, 3, 3, s_st2)
                for b in FINISH_AT[n]:
                    deviation(s_var1, s_root1, b, b % 2)
                    if b:
                        high_v(b - 1)
            high_v(NB - 1)

            def high_z(b, s):
                act.wait_ge(s_mm2, b + 1)
                nc.scalar.activation(xhl[:, b, 0], ps[:, SYM_BANKS[s], :], ACT.Copy,
                                     scale=zscale[:, bass.ds(b, 1)]).then_inc(s_zhi, 1)

            with act.Fori(0, NB - 7, 4) as b0:
                for s in range(4):
                    high_z(b0 + s, s)
                    stage(sym8, b0 + s + 4, s, s_st2)
            for s in range(4):
                high_z(NB - 4 + s, s)
                stage(adjT8, s, s, s_st3)
            with act.Fori(0, NB - 7, 4) as b0:
                for s in range(4):
                    act.wait_ge(s_mm3, b0 + s + 1)
                    stage(adjT8, b0 + s + 4, s, s_st3)
                    deviation(s_var3, s_root3, b0 + s, s % 2)
            for s in range(4):
                deviation(s_var3, s_root3, NB - 4 + s, s % 2)

        @block.vector
        def _(dve):
            V = nc.vector
            chain = [0]

            def link(ins):
                chain[0] += 1
                ins.then_inc(s_dve, 1)
                dve.wait_ge(s_dve, chain[0])

            def wide(v, mid):
                return v.unsqueeze(1).to_broadcast([v.shape[0], mid, v.shape[1]])

            def deep(v, last):
                return v.unsqueeze(2).to_broadcast([v.shape[0], v.shape[1], last])

            def over(v, W):
                return packed(v, *v.shape[1:-1], W)

            intA, intB = raw.rearrange("p c f -> p (c f)")[:, 0:EC], raw.rearrange("p c f -> p (c f)")[:, EC:2 * EC]

            def one_hots(W):
                a, b = intA[:, 0:W], intB[:, 0:W]
                link(V.tensor_copy(key16[:, 0:W], key[:, 0:W]))
                link(V.tensor_copy(a, key[:, 0:W]))
                link(V.tensor_single_scalar(b, a, LOG_LO, ALU.logical_shift_right))
                link(V.tensor_single_scalar(a, a, LO - 1, ALU.bitwise_and))
                link(V.tensor_tensor(hotlo[:, 0:W], wide(iota[0:EP, 0:LO], W), deep(a, LO), ALU.is_equal))
                high_hots(W, 0)

            def high_hots(W, chunk):
                _k, first, end = chunks(W)[chunk]
                V.tensor_tensor(hot[:, first:end], wide(iota[0:EP], end - first), deep(intB[:, first:end], HI),
                                ALU.is_equal).then_inc(s_hot, 1)

            dve.wait_ge(s_raw, 16)
            link(V.tensor_single_scalar(adj_idx, raw[:, :, 0], LOG_N, ALU.logical_shift_left))
            V.tensor_tensor(adj_idx, adj_idx, raw[:, :, 1], ALU.bitwise_or).then_inc(s_idx, 1)
            link(V.tensor_copy(payload[:, 0], raw[:, :, 0]))
            link(V.tensor_copy(payload[:, 1], raw[:, :, 1]))
            dve.wait_ge(s_const, 1)
            dve.wait_ge(s_b, 32)
            link(V.tensor_copy(bias_hi, bias_in))
            link(V.tensor_copy(bias16[0:1], bias_hi[0:1]))
            link(V.tensor_tensor(bias_in, bias_in, bias_hi, ALU.subtract))
            link(V.tensor_copy(bias_mid, bias_in))
            link(V.tensor_copy(bias16[32:33], bias_mid[32:33]))
            V.tensor_tensor(bias16[64:65], bias_in[64:65], bias_mid[64:65], ALU.subtract).then_inc(s_bias, 1)
            for g in range(TRANSPOSES):
                dve.wait_ge(s_trhi, g + 1)
                w = wT[:, g // KB, g % KB]
                V.scalar_tensor_tensor(w[:, 1], ps[:, g % 8, :], WS, w[:, 0], ALU.mult, ALU.subtract).then_inc(s_trlo, 1)
            for b in range(NB):
                dve.wait_ge(s_adj[b % 2], 16 * (b // 2 + 1))
                V.scalar_tensor_tensor(sym8[:, b], adj_in[:, b % 2], 1.0, adj_in[:, b % 2], ALU.mult, ALU.mult,
                                       accum_out=rowsum[:, b:b + 1]).then_inc(s_adjrow, 1)
                dve.wait_ge(s_xhi, b + 1)
                V.scalar_tensor_tensor(xhl[:, b, 1], xf[:, b], XS, xhl[:, b, 0], ALU.mult, ALU.subtract).then_inc(s_xlo, 1)
            dve.wait_ge(s_xlo, NB)

            def row_degrees():
                dve.wait_ge(s_adjrow, NB)
                dve.wait_ge(s_drain, QUARTERS)
                for b in range(NB):
                    link(V.scalar_tensor_tensor(junk, adjT8[:, b, b * P:(b + 1) * P], 1.0, ident32, ALU.mult, ALU.mult,
                                                accum_out=adjii[:, b:b + 1]))
                V.tensor_tensor(degm, rowsum, adjii, ALU.subtract).then_inc(s_degm, 1)

            def by_width(place, part, col, parts):
                w, per = width[0:parts], perwidth[0:parts]
                link(V.tensor_scalar(col, w.to_broadcast([parts, col.shape[1]]), -0.5, 0.5, ALU.mult, ALU.add))
                link(V.tensor_tensor(part, place, col, ALU.add))
                link(V.tensor_scalar(part, part, per, None, ALU.mult))
                link(V.tensor_scalar(part, part, MAGIC, None, ALU.add))
                link(V.tensor_scalar(part, part, MAGIC, None, ALU.subtract))
                link(V.tensor_scalar(col, part, w, None, ALU.mult))
                link(V.tensor_tensor(col, place, col, ALU.subtract))

            def whole(v):
                link(V.tensor_scalar(v, v, MAGIC, None, ALU.add))
                link(V.tensor_scalar(v, v, MAGIC, None, ALU.subtract))

            def sort(n, W):
                fields, last = FIELDS[n], W - 1
                counts, before_, again = packed(cnt, LO, W), packed(incl, LO, W), packed(restart, LO, W)
                table, ranks, at = tab[:, 0:W], rank[:, 0:W], posf[:, 0:W]
                col, part_ = tcol[:, 0:W], tpart[:, 0:W]
                link(V.memset(again, 1.0))
                link(V.memset(again[:, :, 0:1], 0.0))
                for g in range(W // 4):
                    chunk, within = divmod(4 * g, EC // CHUNKS)
                    if within == 0 and chunk + 1 < len(chunks(W)):
                        high_hots(W, chunk + 1)
                    dve.wait_ge(s_group, G4 * n + g + 1)
                    for u in range(4):
                        keys = ps[0:EP, KEY_BANKS[g % 3], u * P:u * P + EP]
                        r = V.scalar_tensor_tensor(keys, keys, key[:, 4 * g + u:4 * g + u + 1], lower[:, 0:EP],
                                                   ALU.is_equal, ALU.mult,
                                                   accum_out=rank[:, 4 * g + u:4 * g + u + 1])
                    r.then_inc(s_rank, 1)
                dve.wait_ge(s_rank, G4 * n + W // 4)
                link(V.tensor_copy(counts, ps_cnt[:, 0:W * LO].rearrange("p (c b) -> p b c", b=LO)))
                link(V.tensor_tensor_scan(before_.rearrange("p b c -> p (b c)"), again.rearrange("p b c -> p (b c)"),
                                          counts.rearrange("p b c -> p (b c)"), 0.0, ALU.mult, ALU.add))
                link(V.tensor_copy(tot, before_[:, :, last]))
                link(V.tensor_tensor_scan(off, tot, zeros[:, 0:LO], 0.0, ALU.add, ALU.add))
                V.tensor_copy(rowtot, off[:, LO - 1:LO]).then_inc(s_rowtot, 1)
                link(V.tensor_tensor(before_, before_, counts, ALU.subtract))
                dve.wait_ge(s_aoff, n + 1)
                link(V.tensor_copy(spread, ps[:, 3, 0:2]))
                link(V.scalar_tensor_tensor(off, off, aoff, tot, ALU.add, ALU.subtract))
                link(V.tensor_tensor(before_, before_, deep(off, W), ALU.add))
                high, low = (table[:, :, f].rearrange("p c b -> p b c") for f in (0, 1))
                link(V.tensor_scalar(counts, before_, 1.0 / P, MAGIC, ALU.mult, ALU.add))
                link(V.tensor_scalar(high, counts, MAGIC, None, ALU.subtract))
                if n == 1:
                    dve.wait_ge(s_degr, 16)
                    link(V.tensor_copy(table[:, :, 2], wide(degr, W)))
                V.scalar_tensor_tensor(low, high, -float(P), before_, ALU.mult, ALU.add).then_inc(s_tab, 1)
                if n == 0:
                    link(V.tensor_scalar(width, placed, (EP - 1) / 2.0, 1.0 / EP, ALU.add, ALU.mult))
                    whole(width)
                    link(V.tensor_scalar(width, width, 1.0, None, ALU.max))
                    link(V.tensor_copy(widthI, width))
                    V.reciprocal(perwidth, width).then_inc(s_width, 1)
                    dve.wait_ge(s_width, 1)
                for g in range(W // 8):
                    dve.wait_ge(s_pick, G8 * n + g + 1)
                    took = picked[:, g % 2, 0:8 * fields * LO].rearrange("p (c f b) -> p c f b", c=8, f=fields)
                    src = ps[0:EP, 3 + g % 2, 0:8 * fields * LO].rearrange("p (c f b) -> p c f b", c=8, f=fields)
                    low_hot = hotlo[:, 8 * g:8 * g + 8].unsqueeze(2).to_broadcast([EP, 8, fields, LO])
                    V.tensor_tensor(took, src, low_hot, ALU.mult).then_inc(s_pickmul, 1)
                    dve.wait_ge(s_pickmul, G8 * n + g + 1)
                    V.tensor_reduce(posf[:, 8 * g:8 * g + 8, 0:fields], took, AX.X, ALU.add).then_inc(s_picked, 1)
                dve.wait_ge(s_picked, G8 * n + W // 8)
                link(V.scalar_tensor_tensor(col, at[:, :, 0], float(P), at[:, :, 1], ALU.mult, ALU.add))
                link(V.tensor_tensor(ranks, ranks, col, ALU.add))
                if n == 0:
                    link(V.tensor_scalar(col, ranks, -(EP - 1) / 2.0, 1.0 / EP, ALU.add, ALU.mult))
                    whole(col)
                    link(V.scalar_tensor_tensor(part_, col, -float(EP), ranks, ALU.mult, ALU.add))
                else:
                    by_width(ranks, part_, col, EP)
                    link(V.tensor_copy(payload[:, 2, 0:W], at[:, :, 2]))
                link(V.tensor_scalar(valid[:, 0:W], payload[:, 0, 0:W], 0.0, None, ALU.is_gt))
                link(V.scalar_tensor_tensor(col, col, 1.0, valid[:, 0:W], ALU.add, ALU.mult))
                link(V.tensor_scalar(col, col, -1.0, None, ALU.add))
                hots, degree = packed(payhot, W, 2, W), packed(deghot, W, W)
                for k, a, z in chunks(W):
                    first, m = hots[:, a:z, 0], z - a
                    V.tensor_tensor(first, wide(iota[0:EP, 0:W], m), deep(col[:, a:z], W), ALU.is_equal).then_inc(s_columns, 1)
                    dve.wait_ge(s_columns, CHUNKS * n + k + 1)
                    V.tensor_tensor(tgt[:, a:z], wide(iota[0:EP, 0:EP], m), deep(part_[:, a:z], EP),
                                    ALU.is_equal).then_inc(s_tgt, 1)
                    if n == 1:
                        V.tensor_tensor(degree[:, a:z], first, deep(payload[:, 2, a:z], W), ALU.mult).then_inc(s_degreehot, 1)
                        dve.wait_ge(s_degreehot, k + 1)
                    dve.wait_ge(s_objhot, CHUNKS * n + k + 1)
                    V.tensor_tensor(first, first, deep(payload[:, 0, a:z], W), ALU.mult).then_inc(s_onehots, 1)
                dve.wait_ge(s_perm, n + 1)
                if n == 1:
                    link(V.tensor_copy(payload[:, 2, 0:W], ps[0:EP, 6, 0:W]))
                V.tensor_copy(payload[:, 0:2, 0:W],
                              ps[0:EP, 5, 0:2 * W].rearrange("p (f c) -> p f c", f=2)).then_inc(s_permcopied, 1)
                dve.wait_ge(s_permcopied, n + 1)

            row_degrees()
            dve.wait_ge(s_valid, 16 * EC)
            link(V.tensor_scalar(valid, valid, 1.0, None, ALU.is_equal))
            link(V.scalar_tensor_tensor(payload[:, 0], payload[:, 0], 1.0, valid, ALU.add, ALU.mult))
            link(V.scalar_tensor_tensor(key, payload[:, 1], 1.0, valid, ALU.add, ALU.mult))
            link(V.tensor_scalar(key, key, -1.0, None, ALU.add))
            one_hots(EC)
            sort(0, EC)
            columns = dve.value_load(widthI[0:1, 0:1], min_val=1, max_val=EC)

            def by_columns(steps):
                start = chain[0]
                with dve.If(columns > FEW):
                    steps(EC)
                end, chain[0] = chain[0], start
                with dve.Else():
                    steps(FEW)
                assert chain[0] == end

            def second(W):
                link(V.tensor_scalar(key[:, 0:W], payload[:, 0, 0:W], -1.0, None, ALU.add))
                one_hots(W)
                sort(1, W)

            by_columns(second)

            link(V.tensor_scalar(tmpE, payload[:, 0], -1.0, None, ALU.add))
            link(V.tensor_scalar(subI, tmpE, 0.0, None, ALU.max))
            V.tensor_copy(objI, payload[:, 1]).then_inc(s_eidx, 1)
            link(V.tensor_tensor_scan(sub, tmpE, tmpE, -1.0, ALU.max, ALU.max))
            link(V.tensor_copy(obj, payload[:, 1]))
            V.memset(att, 0.0).then_inc(s_attz, 1)
            link(V.memset(shift, 0.0))
            link(V.tensor_copy(shift[:, 1:EP], ident16[0:EP, 0:EP - 1]))

            def neighbours(W):
                last = W - 1
                flag, back = over(flagF, W), over(flagB, W)
                isF, isL, tmp, first, wgt = selF[:, 0:W], selL[:, 0:W], tmpE[:, 0:W], firstE[:, 0:W], weight[:, 0:W]
                link(V.tensor_scalar(before16[:, 0, 0:1], sub[:, last:W], 1.0, None, ALU.add))
                link(V.tensor_scalar(isF, payload[:, 0, 0:W], 0.0, None, ALU.is_gt))
                link(V.tensor_copy(isL[:, last:W], isF[:, last:W]))
                link(V.tensor_tensor(isL[:, 0:last], isF[:, 0:last], isF[:, 1:W], ALU.subtract))
                link(V.tensor_tensor(isL, isL, obj[:, 0:W], ALU.mult))
                link(V.tensor_reduce(before[:, 0:1], isL, AX.X, ALU.add))
                link(V.tensor_copy(before16[:, 1, 0:1], sub[:, 0:1]))
                link(V.tensor_copy(before16[:, 1, 1:2], sub[:, last:W]))
                V.tensor_copy(before16[:, 0, 1:2], before[:, 0:1]).then_inc(s_before16, 1)
                link(V.memset(flag, 0.0))
                link(V.memset(back, 0.0))
                link(V.tensor_tensor(flag[:, :, 1:W], wide(sub[:, 1:W], NV), wide(sub[:, 0:last], NV), ALU.is_equal))
                link(V.tensor_copy(back[:, :, 0:last], flag[:, :, 1:W]))
                link(V.tensor_scalar(isF, sub[:, 0:W], sub[:, 0:1], None, ALU.is_equal))
                link(V.tensor_scalar(isL, sub[:, 0:W], sub[:, last:W], None, ALU.is_equal))
                dve.wait_ge(s_before, 1)
                link(V.tensor_copy(before, ps[0:EP, 6, 0:2]))
                link(V.tensor_tensor(tmp[:, 1:W], obj[:, 1:W], obj[:, 0:last], ALU.is_equal))
                link(V.tensor_tensor(tmp[:, 1:W], tmp[:, 1:W], flag[:, 0, 1:W], ALU.mult))
                link(V.scalar_tensor_tensor(tmp[:, 0:1], sub[:, 0:1], 1.0, before[:, 0:1], ALU.add, ALU.is_equal))
                link(V.tensor_copy(first, flag[:, 0]))
                link(V.tensor_copy(first[:, 0:1], tmp[:, 0:1]))
                link(V.tensor_scalar(first, first, -1.0, 1.0, ALU.mult, ALU.add))
                link(V.scalar_tensor_tensor(first, payload[:, 0, 0:W], 0.0, first, ALU.is_gt, ALU.mult))
                dve.wait_ge(s_ends, 1)
                for end, edge in ((0, sub[:, 0:1]), (1, sub[:, last:W])):
                    link(V.tensor_scalar(same_row[:, end].rearrange("q k p -> q (k p)"), ps[0:EP, 7, 0:2 * EP], edge, None,
                                         ALU.is_equal))
                link(V.scalar_tensor_tensor(tmp[:, 0:1], obj[:, 0:1], before[:, 1:2], tmp[:, 0:1], ALU.is_equal, ALU.mult))
                link(V.tensor_scalar(tmp, tmp, -1.0, 1.0, ALU.mult, ALU.add))
                link(V.tensor_tensor(wgt, sub[:, 0:W], obj[:, 0:W], ALU.not_equal))
                link(V.tensor_tensor(wgt, wgt, tmp, ALU.mult))
                link(V.scalar_tensor_tensor(wgt, payload[:, 0, 0:W], 0.0, wgt, ALU.is_gt, ALU.mult))

            by_columns(neighbours)

            dve.wait_ge(s_attz, 1)

            def scores(first, end):
                for c in range(first, end):
                    for w in range(2):
                        if c:
                            dve.wait_ge(s_projected, 2 * c - 1 + w)
                        dve.wait_ge(s_edgehi, 2 * c + 1 + w)
                        V.scalar_tensor_tensor(edge_xT[:, w, :, 1], ps[:, w, 0:KB * EP].rearrange("p (k e) -> p k e", k=KB),
                                               XS, edge_xT[:, w, :, 0], ALU.mult, ALU.subtract).then_inc(s_edgelo, 1)
                    if c == 0:
                        pair_sym, pair_T = (m.rearrange("p b j -> p (b j)").bitcast(u16) for m in (sym8, adjT8))
                        V.tensor_tensor(pair_sym, pair_sym, pair_T, ALU.add).then_inc(s_symadd, 1)
                    dve.wait_ge(s_query, c + 1)
                    if c:
                        dve.wait_ge(s_att, c)
                    V.tensor_tensor(prod[:, 0], query, ps[0:EP, 4, :], ALU.mult).then_inc(s_prod, 1)
                    dve.wait_ge(s_prod, c + 1)
                    V.tensor_reduce(att[:, :, c], prod[:, 0].rearrange("p (h d) -> p h d", h=HEADS),
                                    AX.X, ALU.add).then_inc(s_att, 1)
                dve.wait_ge(s_att, end)

            scores(*COLUMN_GROUPS[0])
            for first, end in COLUMN_GROUPS[1:]:
                with dve.If(columns > first):
                    scores(first, end)

            def softmax(W):
                last = W - 1
                vals, fwd, bwd, flag, back, args = (over(v, W) for v in (val, scF, scB, flagF, flagB, arg))
                isF, isL, tmp, wgt, scores_ = selF[:, 0:W], selL[:, 0:W], tmpE[:, 0:W], weight[:, 0:W], att[:, :, 0:W]
                corr, sum_ = corrE[:, 0:W], sums[:, :, 0:W]

                def scan_both(heads, op):
                    v, f, b, ff, fb = (a[:, 0:heads].rearrange("p h c -> p (h c)") for a in (vals, fwd, bwd, flag, back))
                    link(V.tensor_tensor_scan(f, ff, v, 0.0, ALU.mult, op))
                    link(V.tensor_tensor_scan(b[:, ::-1], fb[:, ::-1], v[:, ::-1], 0.0, ALU.mult, op))
                    link(V.tensor_tensor(f, f, b, op))
                    if op is ALU.add:
                        link(V.tensor_tensor(f, f, v, ALU.subtract))
                    link(V.tensor_scalar(tmp[:, 0:1], sub[:, 0:1], sub[:, last:W], None, ALU.not_equal))

                def take_totals(heads):
                    T, other = fwd[:, 0:heads], bwd[:, 0:heads]
                    for k, sel in ((0, isF), (1, isL)):
                        link(V.tensor_tensor(other, deep(totals[:, k, 0:heads], W), T, ALU.subtract))
                        link(V.tensor_tensor(other, other, wide(sel, heads), ALU.mult))
                        link(V.tensor_tensor(T, T, other, ALU.add))

                def row_maxima():
                    scan_both(HEADS, ALU.max)
                    T = fwd[:, 0:HEADS]
                    link(V.memset(piece, 0.0))
                    link(V.tensor_copy(piece[:, 0, 0:1], sub[:, 0:1]))
                    link(V.tensor_copy(piece[:, 1, 0:1], sub[:, last:W]))
                    link(V.tensor_copy(piece[:, 0, 1:1 + HEADS], T[:, :, 0]))
                    V.tensor_scalar(piece[:, 1, 1:1 + HEADS], T[:, :, last], tmp[:, 0:1], None,
                                    ALU.mult).then_inc(s_piece, 1)
                    dve.wait_ge(s_rec, 16)
                    for k, edge in ((0, sub[:, 0:1]), (1, sub[:, last:W])):
                        link(V.tensor_scalar(eqs[:, k], rec[:, :, 0], edge, None, ALU.is_equal))
                    for k in range(2):
                        link(V.tensor_tensor(recprod[:, 0:HEADS], rec[:, :, 1:1 + HEADS].rearrange("p q h -> p h q"),
                                             wide(eqs[:, k], HEADS), ALU.mult))
                        link(V.tensor_reduce(totals[:, k, 0:HEADS], recprod[:, 0:HEADS], AX.X, ALU.max))
                    take_totals(HEADS)

                def row_sums():
                    scan_both(NV, ALU.add)
                    link(V.tensor_copy(ends[:, 0], fwd[:, :, 0]))
                    link(V.tensor_scalar(ends[:, 1], fwd[:, :, last], tmp[:, 0:1], None, ALU.mult))
                    link(V.tensor_scalar(sums16[:, 0], ends, SS, None, ALU.mult))
                    V.scalar_tensor_tensor(sums16[:, 1], ends, SS, sums16[:, 0], ALU.mult, ALU.subtract).then_inc(s_sumparts, 1)
                    dve.wait_ge(s_totals, 1)
                    link(V.tensor_scalar(totals.rearrange("p k v -> p (k v)"), ps[0:EP, 7, 0:2 * NV], 1.0 / SS, None, ALU.mult))
                    take_totals(NV)

                link(V.tensor_scalar(scores_, scores_, DK ** -0.5 / (XS * WS) ** 2, None, ALU.mult))
                link(V.scalar_tensor_tensor(vals[:, 0:HEADS], scores_, 0.0, wide(wgt, HEADS), ALU.max, ALU.mult))
                row_maxima()
                top = fwd[:, 0:HEADS]
                link(V.tensor_scalar(top, top, DIAG, None, ALU.max))
                link(V.tensor_tensor(args[:, 0], scores_, top, ALU.subtract))
                link(V.tensor_scalar(args[:, 0], args[:, 0], 0.0, None, ALU.min))
                link(V.tensor_scalar(args[:, 1], top, -1.0, None, ALU.mult))
                V.tensor_scalar(args[:, 2], top, -1.0, DIAG, ALU.mult, ALU.add).then_inc(s_args, 1)
                dve.wait_ge(s_exp, 1)
                link(V.tensor_tensor(vals[:, 0:HEADS], args[:, 0], wide(wgt, HEADS), ALU.mult))
                link(V.tensor_copy(vals[:, HEADS], wgt))
                row_sums()
                den = fwd[:, 0:HEADS]
                link(V.tensor_tensor(tmp, payload[:, 2, 0:W], fwd[:, HEADS], ALU.subtract))
                link(V.tensor_tensor(bwd[:, 0:HEADS], args[:, 1], wide(tmp, HEADS), ALU.mult))
                link(V.tensor_tensor(den, den, bwd[:, 0:HEADS], ALU.add))
                link(V.tensor_tensor(den, den, args[:, 2], ALU.add))
                link(V.reciprocal(den, den))
                for k in range(3):
                    link(V.tensor_tensor(args[:, k], args[:, k], den, ALU.mult))
                    link(V.tensor_reduce(sum_[:, k], args[:, k].rearrange("p h c -> p c h"), AX.X, ALU.add))
                link(V.tensor_tensor(corr, sum_[:, 0], sum_[:, 1], ALU.subtract))
                link(V.scalar_tensor_tensor(corr, corr, XS / HEADS, wgt, ALU.mult, ALU.mult))
                for k in range(2):
                    got = row_vals[:, k, 0:W]
                    link(V.scalar_tensor_tensor(got, sum_[:, 1 + k], AS / HEADS, firstE[:, 0:W], ALU.mult, ALU.mult))
                    link(V.tensor_copy(row_parts[:, 0:W, 2 * k], got))
                    link(V.tensor_tensor(row_parts[:, 0:W, 2 * k + 1], got, row_parts[:, 0:W, 2 * k], ALU.subtract))
                V.tensor_copy(row_parts[:, 0:W, 4], firstE[:, 0:W]).then_inc(s_parts, 1)

            by_columns(softmax)

            def row_one_hot(c, relative, built, n):
                V.tensor_scalar(sub_in_block, neg_blocks[0:EP], sub[:, c:c + 1], None, ALU.add).then_inc(relative, 1)
                dve.wait_ge(relative, n)
                V.tensor_tensor(onehot[c > 0], wide(iota[0:EP], NB), deep(sub_in_block, P), ALU.is_equal).then_inc(built, 1)
                dve.wait_ge(built, n)

            def corrected_rows(c, x_rows, high, built, n):
                y = y_[c > 0]
                V.tensor_scalar(y[:, 0], x_rows, corrE[:, c:c + 1], None, ALU.mult).then_inc(high, 1)
                dve.wait_ge(high, n)
                V.scalar_tensor_tensor(y[:, 1], x_rows, corrE[:, c:c + 1], y[:, 0], ALU.mult, ALU.subtract).then_inc(built, 1)
                dve.wait_ge(built, n)

            row_one_hot(0, s_rel, s_onehot, 1)
            dve.wait_ge(s_xfirst, 16)
            corrected_rows(0, x_first, s_y0hi, s_y0, 1)
            dve.wait_ge(s_rowmm, 1)
            V.tensor_copy(row_got.rearrange("p b v -> p (b v)"), ps[:, 4, 0:5 * NB]).then_inc(s_rowadd, 1)
            dve.wait_ge(s_rowadd, 1)
            for first, end in COLUMN_GROUPS[1:]:
                with dve.If(columns > first):
                    for c in range(first, end):
                        row_one_hot(c, s_rel, s_onehot, c + 1)
                        dve.wait_ge(s_rowmm, c + 1)
                        V.tensor_tensor(row_got.rearrange("p b v -> p (b v)"), row_got.rearrange("p b v -> p (b v)"),
                                        ps[:, 4 + c % 2, 0:5 * NB], ALU.add).then_inc(s_rowadd, 1)
                        dve.wait_ge(s_rowadd, c + 1)
            e0 = 1.0 - DIAG
            default, lacks = diag1, rowsum
            link(V.tensor_scalar(default, degm, e0, 1.0, ALU.mult, ALU.add))
            link(V.reciprocal(default, default))
            link(V.tensor_scalar(lacks, row_got[:, :, 4], -1.0, 1.0, ALU.mult, ALU.add))
            link(V.tensor_tensor(default, default, lacks, ALU.mult))
            for k in range(2):
                got = row_got[:, :, 2 * k]
                link(V.tensor_tensor(got, got, row_got[:, :, 2 * k + 1], ALU.add))
                link(V.tensor_scalar(got, got, 1.0 / AS, None, ALU.mult))
            link(V.scalar_tensor_tensor(base, default, e0, row_got[:, :, 0], ALU.mult, ALU.add))
            link(V.tensor_tensor(diag1, default, row_got[:, :, 2], ALU.add))
            link(V.tensor_tensor(rowsum, base, adjii, ALU.mult))
            V.scalar_tensor_tensor(diag1, diag1, 1.0, rowsum, ALU.add, ALU.subtract).then_inc(s_base, 1)
            dve.wait_ge(s_symsum, NB)
            V.tensor_scalar(dinv, vscale, 0.5, 1.0, ALU.mult, ALU.add).then_inc(s_deg, 1)
            for b in range(NB):
                blk = sym8[:, b, b * P:(b + 1) * P]
                V.scalar_tensor_tensor(blk, ident32, 2.0, blk, ALU.mult, ALU.add).then_inc(s_symdiag, 1)
            dve.wait_ge(s_degroot, 1)
            link(V.reciprocal(dinv, dinv))
            link(V.tensor_scalar(zscale, dinv, ZS / (2 * VS), None, ALU.mult))
            V.tensor_scalar(vscale, dinv, VS, None, ALU.mult).then_inc(s_vscale, 1)
            for first, end in COLUMN_GROUPS[1:]:
                with dve.If(columns > first):
                    dve.wait_ge(s_x1init, NB)
                    for c in range(first, end):
                        if c > 1:
                            dve.wait_ge(s_moremm, NB * (c - 1))
                        row_one_hot(c, s_morerel, s_moreoh, c)
                        dve.wait_ge(s_xmore, 16 * c)
                        corrected_rows(c, x_more, s_morehi, s_morey, c)
                        for b in range(NB):
                            n = NB * (c - 1) + b
                            dve.wait_ge(s_moremm, n + 1)
                            V.scalar_tensor_tensor(x1[:, b], ps[:, n % 2, :], 1.0 / XS, x1[:, b], ALU.mult,
                                                   ALU.add).then_inc(s_moreadd, 1)
                        dve.wait_ge(s_moreadd, NB * c)
            V.memset(sub_in_block, 0.0).then_inc(s_more, 1)

            def moments(signal, variance, b, s):
                V.bn_stats(stat[:, s, 2:8], res[:, s]).then_inc(signal, 1)
                dve.drain()
                V.bn_aggr(mean_var[:, s], stat[:, s, 2:8]).then_inc(signal, 1)
                dve.wait_ge(signal, 2 * b + 2)
                V.tensor_scalar(stat[:, s, 0:1], mean_var[:, s, 1:2], EPS, None, ALU.add).then_inc(variance, 1)

            def normalise(root, inverse, b, s, dst, done):
                dve.wait_ge(root, b + 1)
                V.reciprocal(stat[:, s, 0:1], stat[:, s, 1:2]).then_inc(inverse, 1)
                dve.wait_ge(inverse, b + 1)
                V.tensor_scalar(dst, res[:, s], mean_var[:, s, 0:1], stat[:, s, 0:1], ALU.subtract, ALU.mult).then_inc(done, 1)

            def sum1(b, s):
                dve.wait_ge(s_acc, b + 1)
                dve.wait_ge(s_x1init, b + 1)
                if b >= 2:
                    dve.wait_ge(s_x1, b - 1)
                V.scalar_tensor_tensor(res[:, s], acc[:, b], base[:, b:b + 1], x1[:, b], ALU.mult, ALU.add).then_inc(s_accx, 1)
                dve.wait_ge(s_accx, b + 1)
                dve.wait_ge(s_mmc, b + 1)
                V.scalar_tensor_tensor(res[:, s], ps[:, CORR_BANKS[b % 4], :], 1.0 / XS, res[:, s], ALU.mult, ALU.add).then_inc(s_res1, 1)
                dve.wait_ge(s_res1, b + 1)
                moments(s_ln1, s_var1, b, s)

            def low_v(b):
                dve.wait_ge(s_vhi, b + 1)
                V.scalar_tensor_tensor(vhl[:, b, 1], x1[:, b], vscale[:, b:b + 1], vhl[:, b, 0], ALU.mult,
                                       ALU.subtract).then_inc(s_vlo, 1)

            for b in range(NB):
                sum1(b, b % 2)
                if b:
                    normalise(s_root1, s_inv1, b - 1, (b - 1) % 2, x1[:, b - 1], s_x1)
                if b >= 2:
                    low_v(b - 2)
            normalise(s_root1, s_inv1, NB - 1, 1, x1[:, NB - 1], s_x1)
            low_v(NB - 2)
            low_v(NB - 1)

            with dve.Fori(0, NB - 3, 4) as b0:
                for s in range(4):
                    dve.wait_ge(s_zhi, b0 + s + 1)
                    V.scalar_tensor_tensor(xhl[:, b0 + s, 1], ps[:, SYM_BANKS[s], :], zscale[:, bass.ds(b0 + s, 1)],
                                           xhl[:, b0 + s, 0], ALU.mult, ALU.subtract).then_inc(s_zlo, 1)

            def post3(b, turn):
                s = turn % 2
                dve.wait_ge(s_mm3, b + 1)
                if not isinstance(b, int) or b >= 2:
                    dve.wait_ge(s_y, b - 1)
                V.scalar_tensor_tensor(res[:, s], ps[:, ADJ_BANKS[turn], :], 1.0 / ZS, x1[:, b], ALU.mult, ALU.add).then_inc(s_res3, 1)
                dve.wait_ge(s_res3, b + 1)
                moments(s_ln3, s_var3, b, s)
                if not isinstance(b, int) or b >= 2:
                    dve.wait_ge(s_out[s], (b - s) * 8)
                normalise(s_root3, s_inv3, b, s, xt[s], s_y)

            for b in range(4):
                post3(b, b)
            with dve.Fori(4, NB - 3, 4) as b0:
                for turn in range(4):
                    post3(b0 + turn, turn)


_INS = ['x', 'adj', 'L0_gnn_rel_pair_index', 'L0_gnn_Wq', 'L0_gnn_bq', 'L0_gnn_Wk', 'L0_gnn_bk']
_OUTS = [((2048, 512), 'float32')]


def kernel(**inputs):
    import numpy as _np
    import concourse.bacc as _bacc
    from concourse import mybir as _mybir
    from concourse.bass_utils import run_bass_kernel_spmd as _run

    nc = _bacc.Bacc("TRN2", target_bir_lowering=False, num_devices=1)
    arrays, args = {}, []
    for name in _INS:
        a = _np.ascontiguousarray(inputs[name])
        arrays[f"in_{name}_dram"] = a
        args.append(nc.dram_tensor(f"in_{name}_dram", a.shape, _mybir.dt.from_np(a.dtype), kind="ExternalInput").ap())
    for i, (shape, dtype) in enumerate(_OUTS):
        dt = _mybir.dt.from_np(_np.dtype(dtype))
        args.append(nc.dram_tensor(f"out_{i}_dram", shape, dt, kind="ExternalOutput").ap())
    gnn_resnorm_kernel(nc, *args)
    r = _run(nc, [arrays], core_ids=[0])
    return r.results[0]["out_0_dram"]
```
